# Optimizing a Trainium2 kernel written in Bass

```python
import numpy as np
import jax
import jax.numpy as jnp

def _softmax(x, axis=-1):
    return jax.nn.softmax(x, axis=axis)

def _gelu(x):
    return jax.nn.gelu(x, approximate=True)

def _silu(x):
    return jax.nn.silu(x)

def _sigmoid(x):
    return jax.nn.sigmoid(x)

def _layernorm(x, axis=-1, eps=1e-05):
    m = jnp.mean(x, axis=axis, keepdims=True)
    v = jnp.var(x, axis=axis, keepdims=True)
    return (x - m) / jnp.sqrt(v + eps)

def _scatter_add(tgt, idx, src, axis=0):
    return tgt.at[idx].add(src)

def _segment_sum(src, seg, n):
    return jax.ops.segment_sum(src, seg, n)
kernel_name = 'mk_decoder_postln_d1_seqx_r8_1a0ea6'

def setup_inputs(seed: int=0):
    np.random.seed(seed)
    _w = jnp.asarray

    def _rec_inputs():
        import jax
        import jax.numpy as jnp
        _rk = jax.random.key(seed)
        x = -0.0005207 + 1.001 * jax.random.normal(jax.random.fold_in(_rk, 1), (32, 128, 128), jnp.float32)
        _lenS = 128 - jax.random.randint(jax.random.fold_in(_rk, 7), (32,), 0, max(1, 128 // 4) + 1, jnp.int32)
        _lenS2 = 128 - jax.random.randint(jax.random.fold_in(_rk, 8), (32,), 0, max(1, 128 // 4) + 1, jnp.int32)
        _ctx_1024P = jax.random.normal(jax.random.fold_in(_rk, 11), (32, 16, 128), jnp.float32)
        _ctx_1024c = jax.random.dirichlet(jax.random.fold_in(_rk, 511), 0.3 * jnp.ones((16,), jnp.float32), (32, 128))
        _ctx_1024t = jnp.einsum('bsk,bkd->bsd', _ctx_1024c, _ctx_1024P)
        _ctx_1024t = _ctx_1024t * jax.lax.rsqrt(jnp.mean(jnp.square(_ctx_1024t)) + 1e-12) * 0.953939
        ctx_1024 = -0.000514642 + 1.00011 * (_ctx_1024t + 0.3 * jax.random.normal(jax.random.fold_in(_rk, 611), (32, 128, 128), jnp.float32))
        return (x, ctx_1024)
    x, ctx_1024 = _rec_inputs()

    def _L0_attn_setup():
        import jax, jax.numpy as jnp
        import numpy as np
        import math
        DIM_EMB = 128
        DIM_QK = 128
        DIM_V = 128
        NORM_FACT = 1.0 / math.sqrt(DIM_EMB)
        key = jax.random.key(seed)
        k0, k1, k2, k3 = jax.random.split(key, 4)
        x = jax.random.normal(k0, (4, 512, DIM_EMB), dtype=jnp.float32)
        s = 1.0 / math.sqrt(DIM_EMB)
        Wq = jax.random.uniform(k1, (DIM_QK, DIM_EMB), jnp.float32, -s, s)
        Wk = jax.random.uniform(k2, (DIM_QK, DIM_EMB), jnp.float32, -s, s)
        Wv = jax.random.uniform(k3, (DIM_V, DIM_EMB), jnp.float32, -s, s)
        return {'x': x, 'Wq': Wq, 'Wk': Wk, 'Wv': Wv}
    _L0_attn_all = _L0_attn_setup()
    _L0_attn_in = {k: v for k, v in _L0_attn_all.items() if k in ('Wq', 'Wk', 'Wv')}
    del _L0_attn_all

    def _L0_xattn_setup():
        import jax, jax.numpy as jnp
        import numpy as np
        B, S, E, NH = (1, 256, 128, 8)
        DH = E // NH
        EPS = 1e-06
        LN_EPS = 1e-05
        key = jax.random.key(seed)
        ks = jax.random.split(key, 8)
        q = jax.random.normal(ks[0], (B, S, E), dtype=jnp.float32)
        k = jax.random.normal(ks[1], (B, S, E), dtype=jnp.float32)
        v = jax.random.normal(ks[2], (B, S, E), dtype=jnp.float32)
        scale = 1.0 / np.sqrt(3 * E)
        igate_w = jax.random.normal(ks[3], (NH, 3 * E), dtype=jnp.float32) * scale
        igate_b = jax.random.normal(ks[4], (NH,), dtype=jnp.float32) * 0.1
        fgate_w = jax.random.normal(ks[5], (NH, 3 * E), dtype=jnp.float32) * scale
        fgate_b = jnp.linspace(3.0, 6.0, NH, dtype=jnp.float32)
        out_w = 1.0 + 0.1 * jax.random.normal(ks[6], (E,), dtype=jnp.float32)
        return {'q': q, 'k': k, 'v': v, 'igate_w': igate_w, 'igate_b': igate_b, 'fgate_w': fgate_w, 'fgate_b': fgate_b, 'out_w': out_w}
    _L0_xattn_all = _L0_xattn_setup()
    _L0_xattn_in = {k: v for k, v in _L0_xattn_all.items() if k in ('igate_w', 'igate_b', 'fgate_w', 'fgate_b', 'out_w')}
    del _L0_xattn_all

    def _L0_ffn_setup():
        import jax, jax.numpy as jnp
        import numpy as np
        E, K, H, F, R = (8, 2, 128, 256, 64)
        B, S = (2, 256)
        key = jax.random.key(seed)
        k0, k1, k2, k3, k4 = jax.random.split(key, 5)
        return {'hidden_states': jax.random.normal(k0, (B, S, H), dtype=jnp.float32), 'W_A': jax.random.normal(k1, (E, R, H), dtype=jnp.float32) * 0.02, 'W_B': jax.random.normal(k2, (E, F, R), dtype=jnp.float32) * 0.02, 'W_up': jax.random.normal(k3, (E, F, H), dtype=jnp.float32) * 0.02, 'W_down': jax.random.normal(k4, (E, H, F), dtype=jnp.float32) * 0.02}
    _L0_ffn_all = _L0_ffn_setup()
    _L0_ffn_in = {k: v for k, v in _L0_ffn_all.items() if k in ('W_A', 'W_B', 'W_up', 'W_down')}
    del _L0_ffn_all
    return {'x': x, 'ctx_1024': ctx_1024, 'L0_attn_Wq': _L0_attn_in['Wq'], 'L0_attn_Wk': _L0_attn_in['Wk'], 'L0_attn_Wv': _L0_attn_in['Wv'], 'L0_xattn_igate_w': _L0_xattn_in['igate_w'], 'L0_xattn_igate_b': _L0_xattn_in['igate_b'], 'L0_xattn_fgate_w': _L0_xattn_in['fgate_w'], 'L0_xattn_fgate_b': _L0_xattn_in['fgate_b'], 'L0_xattn_out_w': _L0_xattn_in['out_w'], 'L0_ffn_W_A': _L0_ffn_in['W_A'], 'L0_ffn_W_B': _L0_ffn_in['W_B'], 'L0_ffn_W_up': _L0_ffn_in['W_up'], 'L0_ffn_W_down': _L0_ffn_in['W_down']}

def reference(x, ctx_1024, L0_attn_Wq, L0_attn_Wk, L0_attn_Wv, L0_xattn_igate_w, L0_xattn_igate_b, L0_xattn_fgate_w, L0_xattn_fgate_b, L0_xattn_out_w, L0_ffn_W_A, L0_ffn_W_B, L0_ffn_W_up, L0_ffn_W_down):
    import jax
    import jax.numpy as jnp

    def _L0_attn_ref(x, Wq, Wk, Wv):
        import jax, jax.numpy as jnp
        import numpy as np
        import math
        DIM_EMB = 128
        DIM_QK = 128
        DIM_V = 128
        NORM_FACT = 1.0 / math.sqrt(DIM_EMB)
        q = jnp.einsum('bne,de->bnd', x, Wq)
        k = jnp.einsum('bne,de->bnd', x, Wk)
        v = jnp.einsum('bne,de->bnd', x, Wv)
        logits = jnp.einsum('bnd,bmd->bnm', q, k)
        score = jax.nn.softmax(logits, axis=-1) * NORM_FACT
        att = jnp.einsum('bnm,bmv->bnv', score, v)
        return att

    def _L0_xattn_ref(q, k, v, igate_w, igate_b, fgate_w, fgate_b, out_w):
        import jax, jax.numpy as jnp
        import numpy as np
        B, S, E, NH = (1, 256, 128, 8)
        DH = E // NH
        EPS = 1e-06
        LN_EPS = 1e-05
        Bq, Sq, Eq = q.shape
        nh = igate_b.shape[0]
        dh = Eq // nh
        gi = jnp.concatenate([q, k, v], axis=-1)
        ig = (gi @ igate_w.T + igate_b).transpose(0, 2, 1)
        fg = (gi @ fgate_w.T + fgate_b).transpose(0, 2, 1)
        qh = q.reshape(Bq, Sq, nh, dh).transpose(0, 2, 1, 3)
        kh = k.reshape(Bq, Sq, nh, dh).transpose(0, 2, 1, 3)
        vh = v.reshape(Bq, Sq, nh, dh).transpose(0, 2, 1, 3)
        log_f = jax.nn.log_sigmoid(fg)
        cs = jnp.cumsum(log_f, axis=-1)
        diff = cs[..., :, None] - cs[..., None, :]
        mask = jnp.tril(jnp.ones((Sq, Sq), dtype=bool))
        log_fg_mat = jnp.where(mask, diff, -jnp.inf)
        log_D = log_fg_mat + ig[..., None, :]
        max_log_D = jnp.max(log_D, axis=-1, keepdims=True)
        D = jnp.exp(log_D - max_log_D)
        qk = jnp.einsum('bhsd,bhtd->bhst', qh, kh) / jnp.sqrt(jnp.float32(dh))
        C = qk * D
        normalizer = jnp.maximum(jnp.abs(C.sum(-1, keepdims=True)), jnp.exp(-max_log_D))
        h = jnp.einsum('bhst,bhtd->bhsd', C / (normalizer + EPS), vh)
        mean = h.mean(-1, keepdims=True)
        var = ((h - mean) ** 2).mean(-1, keepdims=True)
        hn = (h - mean) / jnp.sqrt(var + LN_EPS)
        hn = hn * out_w.reshape(nh, dh)[None, :, None, :]
        return hn.transpose(0, 2, 1, 3).reshape(Bq, Sq, Eq)

    def _L0_ffn_ref(hidden_states, W_A, W_B, W_up, W_down):
        import jax, jax.numpy as jnp
        import numpy as np
        E, K, H, F, R = (8, 2, 128, 256, 64)
        B, S = (2, 256)
        orig_shape = hidden_states.shape
        x = hidden_states.reshape(-1, orig_shape[-1])
        num_experts = W_A.shape[0]
        gate_hidden = jnp.einsum('nh,erh->ner', x, W_A)
        scores = jnp.sqrt(jnp.sum(gate_hidden * gate_hidden, axis=-1))
        topk_scores, topk_idx = jax.lax.top_k(scores, K)
        topk_w = jax.nn.softmax(topk_scores, axis=-1)
        w_full = jnp.sum(jax.nn.one_hot(topk_idx, num_experts, dtype=topk_w.dtype) * topk_w[..., None], axis=1)
        g = jnp.einsum('ner,efr->nef', gate_hidden, W_B)
        up = jnp.einsum('nh,efh->nef', x, W_up)
        y = jnp.einsum('nef,ehf->neh', jax.nn.silu(g) * up, W_down)
        out = jnp.einsum('neh,ne->nh', y, w_full)
        return out.reshape(orig_shape)
    x = _layernorm(x + _L0_attn_ref(x, L0_attn_Wq, L0_attn_Wk, L0_attn_Wv), axis=-1)
    x = _layernorm(x + _L0_xattn_ref(x, ctx_1024, ctx_1024, L0_xattn_igate_w, L0_xattn_igate_b, L0_xattn_fgate_w, L0_xattn_fgate_b, L0_xattn_out_w), axis=-1)
    x = _layernorm(x + _L0_ffn_ref(x, L0_ffn_W_A, L0_ffn_W_B, L0_ffn_W_up, L0_ffn_W_down), axis=-1)
    return x

_drawn_inputs = setup_inputs


def setup_inputs(seed=0):
    import zlib

    import numpy as np

    out = dict(_drawn_inputs(seed))
    spreads = {}
    factors = {'L0_xattn_igate_b': 47.016,
     'L0_ffn_W_A': 8.0,
     'L0_ffn_W_B': 8.0,
     'L0_ffn_W_up': 8.0,
     'L0_ffn_W_down': 8.0}
    for name, (base, spread) in spreads.items():
        noise = np.random.default_rng([zlib.crc32(name.encode()), seed]).standard_normal(out[name].shape)
        drawn = base * np.exp(spread * noise) if base else spread * noise
        out[name] = jnp.asarray(drawn.astype(out[name].dtype))
    for name, factor in factors.items():
        out[name] = (out[name] * factor).astype(out[name].dtype)
    return out
```

```python
from contextlib import ExitStack

import concourse.bass as bass
from concourse import mybir

ALU = mybir.AluOpType
ACT = mybir.ActivationFunctionType
F32 = mybir.dt.float32
F32R = mybir.dt.float32r
BF16 = mybir.dt.bfloat16
AX_X = mybir.AxisListType.X

NORM_EPS = 1e-5
GATE_EPS = 1e-6
MASKED = 1e30


class Stage:

    def __init__(self, sem, per):
        self.sem, self.per = sem, per

    def at(self, g, k=None):
        k = self.per if k is None else k
        return g.j * (2 * self.per) + (g.off * self.per + k)

    def at_parity(self, g):
        return g.j * self.per + (g.off // 2 + 1) * self.per


class Group:

    def __init__(self, j, off):
        self.j, self.off = j, off

    def back(self, n):
        return Group(self.j, self.off - n)

    def number(self):
        return self.j * 2 + self.off

    def first(self, n):
        return isinstance(self.j, int) and self.number() < n


def decoder_kernel(nc, x, ctx_in, wq, wk, wv, igate_w, igate_b, fgate_w, fgate_b, out_w,
                   w_a, w_b, w_up, w_down, out):
    B, S, D = x.shape
    H = igate_b.shape[0]
    DH = D // H
    E, R, _ = w_a.shape
    F = w_up.shape[1]
    FB = F // 128
    G = 4
    N = G * S
    GROUPS = B // G
    HG = 4
    HALVES = G * H // HG
    AC = E * R // 128
    VW = 2 * DH + 1
    GH = G * H
    assert S == 128 and D == 128 and GROUPS % 2 == 0 and R == 64 and FB == 2

    x_g = x.rearrange("(g b) n e -> g n b e", b=G)
    c_g = ctx_in.rearrange("(g b) n e -> g n b e", b=G)
    o_g = out.rearrange("(g b) n e -> g n b e", b=G)

    with ExitStack() as ctx:
        def sb(name, shape, dt=F32):
            return ctx.enter_context(nc.sbuf_tensor(name, shape, dt))

        def psum(name, shape, dt=F32):
            return ctx.enter_context(nc.psum_tensor(name, shape, dt))

        def sem(name):
            return ctx.enter_context(nc.semaphore(name))

        def stage(name, per=1):
            return Stage(sem(name), per)

        psG = [psum(f"psG{i}", [128, N]) for i in range(2)]
        psU = [psum(f"psU{i}", [128, N]) for i in range(2)]
        psY = psum("psY", [128, G, D])
        psA = psum("psA", [128, 512])
        psB = psum("psB", [128, 512])
        psC = psum("psC", [128, 512])

        ident = sb("ident", [128, 128])
        identb = sb("identb", [128, 128], BF16)
        future = sb("future", [128, HG, 128], BF16)
        headmask = sb("headmask", [128, H])
        expertsum = sb("expertsum", [128, AC, E])
        restart = sb("restart", [128, G, E])
        epsilon = sb("epsilon", [128, G])
        minushalf = sb("minushalf", [128, GH])
        plushalf = sb("plushalf", [128, GH])
        ones = sb("ones", [GH, 128])

        wq_n = sb("wq_n", [D, D])
        wk_n = sb("wk_n", [D, D])
        wv_n = sb("wv_n", [D, D])
        gate_n = sb("gate_n", [2 * H, 3 * D])
        gbias = sb("gbias", [2 * GH, 1])
        outw = sb("outw", [128, D])
        wa_r = sb("wa_r", [R, E, D])
        wa_n = sb("wa_n", [128, AC, D])
        wb_n = sb("wb_n", [128, E, FB, R])
        wup_n = sb("wup_n", [128, E, FB, D])
        wdn_n = sb("wdn_n", [D, E, FB, 128])

        qk_w = sb("qk_w", [D, D])
        wvT = sb("wvT", [D, D])
        gate_xT = sb("gate_xT", [D, 2 * H])
        gate_cT = sb("gate_cT", [D, 2 * H])
        gate_t = sb("gate_t", [D, 2 * H])
        gate_p = sb("gate_p", [D, 2, G, 2 * GH])
        wbT = sb("wbT", [R, E, F])
        gw_hi = sb("gw_hi", [D, E, F], F32R)
        gw_lo = sb("gw_lo", [D, E, F], F32R)
        uw_hi = sb("uw_hi", [D, E, F], F32R)
        uw_lo = sb("uw_lo", [D, E, F], F32R)
        aw_hi = sb("aw_hi", [D, AC, 128], F32R)
        aw_lo = sb("aw_lo", [D, AC, 128], F32R)
        dwT = sb("dwT", [128, E, FB, D])

        xin = [sb(f"xin{i}", [128, G, D]) for i in range(2)]
        cin = [sb(f"cin{i}", [128, G, D]) for i in range(2)]
        xT = sb("xT", [D, G, S])
        zT = sb("zT", [D, G, S])
        v_sb = sb("v_sb", [S, G, D])
        rowmax = sb("rowmax", [S, G])
        negmax = sb("negmax", [S, G])
        probs = sb("probs", [S, G, S])
        rowsum = sb("rowsum", [S, G])
        rowsum_n = sb("rowsum_n", [S, G])
        rowinv = sb("rowinv", [S, G])
        probsT = sb("probsT", [S, G, S])
        res1 = sb("res1", [S, G, D])
        bn6 = sb("bn6", [S, G, 6])
        mv1 = sb("mv1", [S, G, 2])
        var1 = sb("var1", [S, G])
        rstd1 = sb("rstd1", [S, G])
        x1 = sb("x1", [S, G, D])
        x1T = sb("x1T", [D, G, S])
        cT = sb("cT", [D, G, S])
        kmask = sb("kmask", [D, G, H, S])
        vmean = sb("vmean", [S, GH])
        vsum = sb("vsum", [S, GH])
        vaug = sb("vaug", [S, GH, VW])
        f_in = sb("f_in", [GH, S])
        f_neg = sb("f_neg", [GH, S])
        f_exp = sb("f_exp", [GH, S])
        f_ln = sb("f_ln", [GH, S])
        logf = sb("logf", [GH, S])
        cumf = sb("cumf", [GH, S])
        arow = sb("arow", [GH, S])
        amax = sb("amax", [GH, S])
        mrow = sb("mrow", [GH, S])
        acol = sb("acol", [S, GH])
        expm = sb("expm", [S, GH])
        decay = [sb(f"decay{i}", [S, HG, S]) for i in range(2)]
        cmat = [sb(f"cmat{i}", [S, HG, S]) for i in range(2)]
        u_sb = sb("u_sb", [S, GH, VW])
        usq = sb("usq", [S, GH, DH])
        uss = sb("uss", [S, GH])
        sum_abs = sb("sum_abs", [S, GH])
        nrm = sb("nrm", [S, GH])
        nrm_e = sb("nrm_e", [S, GH])
        nrm_2 = sb("nrm_2", [S, GH])
        hvar = sb("hvar", [S, GH])
        hrstd = sb("hrstd", [S, GH])
        hn = sb("hn", [S, GH, DH])
        res2 = sb("res2", [S, G, D])
        bn6b = sb("bn6b", [S, G, 6])
        mv2 = sb("mv2", [S, G, 2])
        var2 = sb("var2", [S, G])
        rstd2 = sb("rstd2", [S, G])

        acc = [sb(f"acc{i}", [S, G, D]) for i in range(2)]
        x2hi = [sb(f"x2hi{i}", [D, G, S], F32R) for i in range(2)]
        x2lo = [sb(f"x2lo{i}", [D, G, S], F32R) for i in range(2)]
        hidsq = sb("hidsq", [128, AC, N])
        sc2 = sb("sc2", [S, G, E])
        score = sb("score", [S, G, E])
        top8 = sb("top8", [S, G, 8])
        is1 = sb("is1", [S, G])
        lim = sb("lim", [S, G])
        above = sb("above", [S, G, E])
        equal = sb("equal", [S, G, E])
        rank = sb("rank", [S, G, E])
        inlim = sb("inlim", [S, G, E])
        chosen2 = sb("chosen2", [S, G, E])
        chosen = sb("chosen", [S, G, E])
        sdiff = sb("sdiff", [S, G, E])
        sexp = sb("sexp", [S, G, E])
        wexp = sb("wexp", [S, G, E])
        wden = sb("wden", [S, G])
        winv = sb("winv", [S, G])
        wtok = [sb(f"wtok{i}", [S, G, E]) for i in range(2)]
        tanh = [sb(f"tanh{i}", [128, N]) for i in range(2)]
        silu2 = [sb(f"silu2{i}", [128, N]) for i in range(2)]
        hid = [[sb(f"hid{i}{f}", [128, N]) for f in range(FB)] for i in range(2)]
        bn6c = sb("bn6c", [S, G, 6])
        mv3 = sb("mv3", [S, G, 2])
        var3 = sb("var3", [S, G])
        rstd3 = sb("rstd3", [S, G])
        y_out = sb("y_out", [S, G, D])

        w_loaded = sem("w_loaded")
        e_loaded = sem("e_loaded")
        const_step = sem("const_step")
        const_ready = sem("const_ready")
        prep_ps = sem("prep_ps")
        prep_out = sem("prep_out")
        prep_hi = sem("prep_hi")
        gate_step = sem("gate_step")

        x_loaded = [stage(f"x_loaded{i}", 16) for i in range(2)]
        c_loaded = [stage(f"c_loaded{i}", 16) for i in range(2)]
        xT_ps, xT_sb = stage("xT_ps"), stage("xT_sb")
        z_ps, zT_sb = stage("z_ps"), stage("zT_sb")
        v_ps, v_out = stage("v_ps"), stage("v_out")
        logits_ps, max_out, negmax_out = stage("logits_ps"), stage("max_out"), stage("negmax_out")
        probs_out, rown_out, rowinv_out = stage("probs_out"), stage("rown_out"), stage("rowinv_out")
        pT_ps, pT_sb = stage("pT_ps"), stage("pT_sb")
        cT_ps, cT_sb = stage("cT_ps"), stage("cT_sb")
        kmask_out = stage("kmask_out", G)
        vsum_out, vmean_out, vc_out, vaug_out = stage("vsum_out"), stage("vmean_out"), stage("vc_out"), stage("vaug_out")
        att_ps, res1_out, bn1_out, mv1_out = stage("att_ps"), stage("res1_out"), stage("bn1_out"), stage("mv1_out")
        var1_out, rstd1_out, x1_out = stage("var1_out"), stage("rstd1_out"), stage("x1_out")
        x1T_ps, x1T_sb = stage("x1T_ps"), stage("x1T_sb")
        gates_ps = stage("gates_ps")
        f_out, fneg_out, fexp_out, fln_out = stage("f_out"), stage("fneg_out"), stage("fexp_out"), stage("fln_out")
        logf_out, cumf_out, arow_out = stage("logf_out"), stage("cumf_out"), stage("arow_out")
        amax_out, mrow_out = stage("amax_out"), stage("mrow_out")
        am_ps, acol_out, expm_out = stage("am_ps"), stage("acol_out"), stage("expm_out")
        mb_ps, qk_ps = stage("mb_ps", HALVES), stage("qk_ps", HALVES)
        decay_out, cmat_out = stage("decay_out", HALVES), stage("cmat_out", HALVES)
        u_ps, u_out = stage("u_ps", HALVES), stage("u_out", HALVES)
        usq_out, uss_out = stage("usq_out"), stage("uss_out")
        sumabs_out = stage("sumabs_out")
        nrm_out, nrme_out, nrm2_out = stage("nrm_out"), stage("nrme_out"), stage("nrm2_out")
        hvar_out, hrstd_out, hn_out = stage("hvar_out"), stage("hrstd_out"), stage("hn_out")
        res2_out, bn2_out, mv2_out = stage("res2_out"), stage("bn2_out"), stage("mv2_out")
        var2_out, rstd2_out, x2_out = stage("var2_out"), stage("rstd2_out"), stage("x2_out")
        x2T_ps, x2hi_out, x2lo_out = stage("x2T_ps"), stage("x2hi_out"), stage("x2lo_out")
        hid_ps, hidsq_out = stage("hid_ps", AC), stage("hidsq_out", AC)
        sc_ps, sc2_out, score_out = stage("sc_ps"), stage("sc2_out"), stage("score_out")
        top_out, is1_out, lim_out = stage("top_out"), stage("is1_out"), stage("lim_out")
        eq_out, rank_out, inlim_out = stage("eq_out"), stage("rank_out"), stage("inlim_out")
        ch2_out, sel_out, sdiff_out = stage("ch2_out"), stage("sel_out"), stage("sdiff_out")
        sexp_out, wexp_out, wden_out = stage("sexp_out"), stage("wexp_out"), stage("wden_out")
        winv_out, wtok_out = stage("winv_out"), stage("wtok_out")
        g_ps, u2_ps = stage("g_ps", E * FB), stage("u2_ps", E * FB)
        tanh_out, silu_out, hid_out = stage("tanh_out", E * FB), stage("silu_out", E * FB), stage("hid_out", E * FB)
        y_ps, acc_out = stage("y_ps", E), stage("acc_out", E)
        bn3_out, mv3_out, var3_out = stage("bn3_out"), stage("mv3_out"), stage("var3_out")
        rstd3_out, y_ready = stage("rstd3_out"), stage("y_ready")
        stored = stage("stored", 16)

        AB = ["xT", "zv", "logits", "pT", "att", "x1", "x1T", "gates", "scan", "am"]
        AB += [("half", k) for k in range(HALVES + 1)]
        AB += ["post", "x2", "x2T"] + [("hidden", c) for c in range(AC)] + ["scores", "router"]
        C = []
        for e in range(E):
            C += [("gu", e, 0), ("gu", e, 1)]
            if e:
                C += [("down", e - 1)]
        C += [("down", E - 1)]

        def merged():
            a = c = 0
            while a < len(AB) or c < len(C):
                if c < len(C) and c * len(AB) <= a * len(C):
                    yield "C", C[c]
                    c += 1
                else:
                    yield "AB", AB[a]
                    a += 1
            yield "C", "final"

        def whole_program(eng, ab, c):
            def both(g):
                for part, step in merged():
                    if part == "AB":
                        ab(Group(g.j, g.off + 1), step)
                    else:
                        c(g, step)
            for step in AB:
                ab(Group(0, 0), step)
            both(Group(0, 0))
            with eng.Fori(0, (GROUPS - 2) // 2) as j:
                both(Group(j, 1))
                both(Group(j, 2))
            for step in C + ["final"]:
                c(Group(0, GROUPS - 1), step)

        def plain_wait(eng):
            eng.wait_ge(const_ready, 1)

        block = ctx.enter_context(nc.Block())

        @block.sync
        def _(sp):
            def load(g):
                p = g.off % 2
                if not g.first(2):
                    sp.wait_ge(res1_out.sem, res1_out.at(g.back(2)))
                    sp.wait_ge(cT_ps.sem, cT_ps.at(g.back(2)))
                    sp.wait_ge(vc_out.sem, vc_out.at(g.back(2)))
                i = g.number()
                src_x = x_g[i] if isinstance(i, int) else x_g[bass.ds(i, 1)].rearrange("g n b e -> (g n) b e")
                src_c = c_g[i] if isinstance(i, int) else c_g[bass.ds(i, 1)].rearrange("g n b e -> (g n) b e")
                sp.dma_start(xin[p][:], src_x).then_inc(x_loaded[p].sem, 16)
                sp.dma_start(cin[p][:], src_c).then_inc(c_loaded[p].sem, 16)

            def store(g):
                p = g.off % 2
                i = g.number()
                dst = o_g[i] if isinstance(i, int) else o_g[bass.ds(i, 1)].rearrange("g n b e -> (g n) b e")
                sp.wait_ge(y_ready.sem, y_ready.at(g))
                sp.dma_start(dst, y_out[:]).then_inc(stored.sem, 16)

            load(Group(0, 0))
            for t, src in ((wq_n, wq), (wk_n, wk), (wv_n, wv)):
                sp.dma_start(t[:], src).then_inc(w_loaded, 16)
            sp.dma_start(gate_n[0:H, :], igate_w).then_inc(w_loaded, 16)
            sp.dma_start(gate_n[H:2 * H, :], fgate_w).then_inc(w_loaded, 16)
            for b in range(G):
                sp.dma_start(gbias[b * H:(b + 1) * H, :], igate_b.rearrange("(h a) -> h a", a=1)).then_inc(w_loaded, 16)
                sp.dma_start(gbias[GH + b * H:GH + (b + 1) * H, :],
                             fgate_b.rearrange("(h a) -> h a", a=1)).then_inc(w_loaded, 16)
            sp.dma_start(outw[:], out_w.rearrange("(a d) -> a d", a=1).to_broadcast([128, D])).then_inc(w_loaded, 16)
            sp.dma_start(wb_n[:], w_b.rearrange("e (k f) r -> f e k r", f=128)).then_inc(e_loaded, 16)
            sp.dma_start(wup_n[:], w_up.rearrange("e (k f) h -> f e k h", f=128)).then_inc(e_loaded, 16)
            sp.dma_start(wa_r[:], w_a.rearrange("e r h -> r e h")).then_inc(e_loaded, 16)
            sp.dma_start(wa_n[:], w_a.rearrange("(c a) r h -> (a r) c h", a=2)).then_inc(e_loaded, 16)
            sp.dma_start(wdn_n[:], w_down.rearrange("e h (k f) -> h e k f", f=128)).then_inc(e_loaded, 16)
            load(Group(0, 1))
            load(Group(0, 2))
            store(Group(0, 0))
            with sp.Fori(0, (GROUPS - 4) // 2) as j:
                load(Group(j, 3))
                store(Group(j, 1))
                load(Group(j, 4))
                store(Group(j, 2))
            load(Group(0, GROUPS - 1))
            for i in range(GROUPS - 3, GROUPS):
                store(Group(0, i))
            sp.wait_ge(stored.sem, stored.at(Group(0, GROUPS - 1)))

        W_DMAS = 3 + 2 + 2 * G + 1
        E_DMAS = 5

        UP_BANKS = E * FB // 4
        B_BANKS = E * FB // 4
        GW_BANKS = E // 2
        PREP = ["small"] + [("wbT", i) for i in range(B_BANKS)] + [("gw", i) for i in range(GW_BANKS)]
        PREP += [("up", i) for i in range(UP_BANKS)] + ["wa"] + [("down", i) for i in range(UP_BANKS)]
        prep_banks = [psG[0], psG[1], psU[0], psU[1]]

        def prep_bank(n):
            return prep_banks[n % 4]

        @block.gpsimd
        def _(pool):
            steps = [0]

            def done(ins):
                steps[0] += 1
                ins.then_inc(const_step, 1)
                pool.wait_ge(const_step, steps[0])

            done(pool.memset(ident[:], 0.0))
            done(pool.affine_select(out=ident[:], in_=ident[:], pattern=[[-1, 128]], base=0,
                                    channel_multiplier=1, compare_op=ALU.not_equal, fill=1.0))
            done(pool.tensor_copy(identb[:], ident[:]))
            done(pool.memset(ones[:], 1.0))
            done(pool.memset(epsilon[:], NORM_EPS))
            done(pool.memset(minushalf[:], -0.5))
            done(pool.memset(plushalf[:], 0.5))
            done(pool.memset(future[:], 0.0))
            done(pool.affine_select(out=future[:], in_=future[:], pattern=[[0, HG], [1, 128]], base=0,
                                    channel_multiplier=-1, compare_op=ALU.is_ge, fill=MASKED))
            done(pool.memset(headmask[:], 1.0))
            done(pool.affine_select(out=headmask[:], in_=headmask[:], pattern=[[-DH, H]], base=0,
                                    channel_multiplier=1, compare_op=ALU.is_ge, fill=0.0))
            done(pool.affine_select(out=headmask[:], in_=headmask[:], pattern=[[DH, H]], base=DH - 1,
                                    channel_multiplier=-1, compare_op=ALU.is_ge, fill=0.0))
            done(pool.memset(expertsum[:], 1.0))
            done(pool.affine_select(out=expertsum[:], in_=expertsum[:], pattern=[[128, AC], [-R, E]], base=0,
                                    channel_multiplier=1, compare_op=ALU.is_ge, fill=0.0))
            done(pool.affine_select(out=expertsum[:], in_=expertsum[:], pattern=[[-128, AC], [R, E]], base=R - 1,
                                    channel_multiplier=-1, compare_op=ALU.is_ge, fill=0.0))
            done(pool.memset(restart[:], 1.0))
            done(pool.affine_select(out=restart[:], in_=restart[:], pattern=[[0, G], [1, E]], base=0,
                                    channel_multiplier=0, compare_op=ALU.not_equal, fill=0.0))
            done(pool.memset(gate_p[:], 0.0))
            pool.memset(vaug[:], 1.0).then_inc(const_ready, 1)
            pool.wait_ge(const_ready, 1)
            pool.wait_ge(w_loaded, 16 * W_DMAS)

            def rstd(g, mv, var, out_, mv_stage, var_stage, out_stage, readers):
                pool.wait_ge(mv_stage.sem, mv_stage.at(g))
                if not g.first(1):
                    pool.wait_ge(readers.sem, readers.at(g.back(1)))
                pool.tensor_tensor(var[:], mv[:, :, 1], epsilon[:, 0:G], ALU.add).then_inc(var_stage.sem, 1)
                pool.wait_ge(var_stage.sem, var_stage.at(g))
                pool.tensor_tensor(out_[:], var[:], minushalf[:, 0:G], ALU.pow).then_inc(out_stage.sem, 1)

            def ab(g, step):
                p = g.off % 2
                if step == "pT":
                    pool.wait_ge(vmean_out.sem, vmean_out.at(g))
                    if not g.first(1):
                        pool.wait_ge(u_ps.sem, u_ps.at(g.back(1)))
                    pool.tensor_tensor(vaug[:, :, 0:DH], cin[p][:].rearrange("t b (h d) -> t (b h) d", d=DH),
                                       vmean[:].unsqueeze(2).to_broadcast([S, GH, DH]),
                                       ALU.subtract).then_inc(vc_out.sem, 1)
                    pool.wait_ge(vc_out.sem, vc_out.at(g))
                    for b in range(G):
                        ins = pool.tensor_tensor(vaug[:, b * H:(b + 1) * H, DH:2 * DH], vaug[:, b * H:(b + 1) * H, 0:DH],
                                                 outw[:].rearrange("p (h d) -> p h d", d=DH), ALU.mult)
                    ins.then_inc(vaug_out.sem, 1)
                elif step == "x1T":
                    pool.wait_ge(cT_sb.sem, cT_sb.at(g))
                    if not g.first(1):
                        pool.wait_ge(qk_ps.sem, qk_ps.at(g.back(1)))
                    for b in range(G):
                        pool.tensor_tensor(kmask[:, b, :, :], cT[:, b, :].unsqueeze(1).to_broadcast([D, H, S]),
                                           headmask[:].unsqueeze(2).to_broadcast([D, H, S]),
                                           ALU.mult).then_inc(kmask_out.sem, 1)
                elif step == "att":
                    rstd(g, mv1, var1, rstd1, mv1_out, var1_out, rstd1_out, x1_out)
                elif step == "post":
                    pool.wait_ge(u_out.sem, u_out.at(g))
                    if not g.first(1):
                        pool.wait_ge(uss_out.sem, uss_out.at(g.back(1)))
                    pool.tensor_tensor(usq[:], u_sb[:, :, 0:DH], u_sb[:, :, 0:DH], ALU.mult).then_inc(usq_out.sem, 1)
                    pool.wait_ge(hvar_out.sem, hvar_out.at(g))
                    if not g.first(1):
                        pool.wait_ge(hn_out.sem, hn_out.at(g.back(1)))
                    pool.tensor_tensor(hrstd[:], hvar[:], minushalf[:], ALU.pow).then_inc(hrstd_out.sem, 1)
                    rstd(g, mv2, var2, rstd2, mv2_out, var2_out, rstd2_out, x2_out)
                elif step == "scores":
                    pool.wait_ge(sc2_out.sem, sc2_out.at(g))
                    if not g.first(1):
                        pool.wait_ge(sdiff_out.sem, sdiff_out.at(g.back(1)))
                    pool.tensor_tensor(score[:].rearrange("p g e -> p (g e)"), sc2[:].rearrange("p g e -> p (g e)"),
                                       plushalf[:], ALU.pow).then_inc(score_out.sem, 1)

            def c(g, step):
                if step == "final":
                    rstd(g, mv3, var3, rstd3, mv3_out, var3_out, rstd3_out, y_ready)

            whole_program(pool, ab, c)

        @block.tensor
        def _(pe):
            pe.wait_ge(const_ready, 1)
            pe.wait_ge(w_loaded, 16 * W_DMAS)
            for n, item in enumerate(PREP):
                ps = prep_bank(n)
                if n == 1:
                    pe.wait_ge(e_loaded, 16 * E_DMAS)
                if n >= 4:
                    pe.wait_ge(prep_out, n - 3)
                if item == "small":
                    pe.matmul(ps[:, 0:128], wq_n[:], wk_n[:], start=True, stop=True)
                    pe.transpose(ps[:, 128:256], wv_n[:], ident[:])
                    for k in range(3):
                        ins = pe.transpose(ps[:, 256 + 2 * H * k:256 + 2 * H * (k + 1)],
                                           gate_n[:, k * D:(k + 1) * D], ident[0:2 * H, 0:2 * H])
                elif item == "wa":
                    for k in range(AC):
                        ins = pe.transpose(ps[:, k * 128:(k + 1) * 128], wa_n[:, k, :], ident[:])
                elif item[0] == "wbT":
                    for k in range(4):
                        q = item[1] * 4 + k
                        ins = pe.transpose(ps[0:R, k * 128:(k + 1) * 128], wb_n[:, q // FB, q % FB, :], ident[:])
                elif item[0] == "gw":
                    if item[1] == 0:
                        pe.wait_ge(prep_out, 1 + B_BANKS)
                    for k in range(2):
                        e = item[1] * 2 + k
                        ins = pe.matmul(ps[:, k * F:(k + 1) * F], wa_r[:, e, :], wbT[:, e, :], start=True, stop=True)
                else:
                    src = wup_n if item[0] == "up" else wdn_n
                    for k in range(4):
                        q = item[1] * 4 + k
                        ins = pe.transpose(ps[:, k * 128:(k + 1) * 128], src[:, q // FB, q % FB, :], ident[:])
                ins.then_inc(prep_ps, 1)
            pe.wait_ge(prep_out, len(PREP))

            def split_product(out_, w_hi, w_lo, x_hi, x_lo):
                pe.matmul(out_, w_lo, x_hi, start=True, stop=False)
                pe.matmul(out_, w_hi, x_lo, start=False, stop=False)
                return pe.matmul(out_, w_hi, x_hi, start=False, stop=True)

            def ab(g, step):
                p = g.off % 2
                if step == "xT":
                    pe.wait_ge(x_loaded[p].sem, x_loaded[p].at_parity(g))
                    if not g.first(1):
                        pe.wait_ge(sc2_out.sem, sc2_out.at(g.back(1)))
                    for b in range(G):
                        ins = pe.transpose(psA[:, b * S:(b + 1) * S], xin[p][:, b, :], ident[:])
                    ins.then_inc(xT_ps.sem, 1)
                elif step == "zv":
                    pe.wait_ge(xT_sb.sem, xT_sb.at(g))
                    if not g.first(1):
                        pe.wait_ge(hidsq_out.sem, hidsq_out.at(g.back(1)))
                    pe.matmul(psB[:], qk_w[:], xT[:].rearrange("e b s -> e (b s)"), start=True, stop=True)\
                        .then_inc(z_ps.sem, 1)
                    for b in range(G):
                        ins = pe.matmul(psC[:, b * D:(b + 1) * D], xT[:, b, :], wvT[:], start=True, stop=True)
                    ins.then_inc(v_ps.sem, 1)
                elif step == "logits":
                    pe.wait_ge(zT_sb.sem, zT_sb.at(g))
                    for b in range(G):
                        ins = pe.matmul(psA[:, b * S:(b + 1) * S], zT[:, b, :], xT[:, b, :], start=True, stop=True)
                    ins.then_inc(logits_ps.sem, 1)
                elif step == "pT":
                    pe.wait_ge(c_loaded[p].sem, c_loaded[p].at_parity(g))
                    pe.wait_ge(v_out.sem, v_out.at(g))
                    for b in range(G):
                        ins = pe.transpose(psC[:, b * S:(b + 1) * S], cin[p][:, b, :], ident[:])
                    ins.then_inc(cT_ps.sem, 1)
                    pe.wait_ge(probs_out.sem, probs_out.at(g))
                    for b in range(G):
                        ins = pe.transpose(psB[:, b * S:(b + 1) * S], probs[:, b, :], ident[:])
                    ins.then_inc(pT_ps.sem, 1)
                elif step == "att":
                    pe.wait_ge(pT_sb.sem, pT_sb.at(g))
                    for b in range(G):
                        ins = pe.matmul(psA[:, b * D:(b + 1) * D], probsT[:, b, :], v_sb[:, b, :], start=True, stop=True)
                    ins.then_inc(att_ps.sem, 1)
                elif step == "x1T":
                    pe.wait_ge(x1_out.sem, x1_out.at(g))
                    for b in range(G):
                        ins = pe.transpose(psB[:, b * S:(b + 1) * S], x1[:, b, :], ident[:])
                    ins.then_inc(x1T_ps.sem, 1)
                elif step == "gates":
                    pe.wait_ge(x1T_sb.sem, x1T_sb.at(g))
                    pe.wait_ge(cT_sb.sem, cT_sb.at(g))
                    for b in range(G):
                        pe.matmul(psC[0:2 * GH, 0:S], gate_p[:, 0, b, :], x1T[:, b, :], start=(b == 0), stop=False)
                        ins = pe.matmul(psC[0:2 * GH, 0:S], gate_p[:, 1, b, :], cT[:, b, :], start=False,
                                        stop=(b == G - 1))
                    ins.then_inc(gates_ps.sem, 1)
                elif step == "am":
                    pe.wait_ge(arow_out.sem, arow_out.at(g))
                    pe.wait_ge(mrow_out.sem, mrow_out.at(g))
                    pe.wait_ge(res1_out.sem, res1_out.at(g))
                    pe.matmul(psA[:, 0:GH], arow[:], ident[0:GH, 0:GH], start=True, stop=True)
                    pe.matmul(psA[:, GH:2 * GH], mrow[:], ident[0:GH, 0:GH], start=True, stop=True)\
                        .then_inc(am_ps.sem, 1)
                elif step[0] == "half":
                    k = step[1]
                    if k < HALVES:
                        b, h0 = k // 2, HG * (k % 2)
                        if k == 0:
                            pe.wait_ge(amax_out.sem, amax_out.at(g))
                            pe.wait_ge(x1T_sb.sem, x1T_sb.at(g))
                            pe.wait_ge(arow_out.sem, arow_out.at(g))
                        else:
                            pe.wait_ge(decay_out.sem, decay_out.at(g, k))
                        pe.matmul(psB[:], identb[:], future[:].rearrange("t h s -> t (h s)"), start=True, stop=False)
                        for i in range(HG):
                            r = b * H + h0 + i
                            ins = pe.matmul(psB[:, i * S:(i + 1) * S], ident[0:GH, r:r + 1].to_broadcast([GH, 128]),
                                            amax[:], start=False,
                                            stop=(i == HG - 1))
                        ins.then_inc(mb_ps.sem, 1)
                        if k % 2 == 0:
                            pe.wait_ge(kmask_out.sem, kmask_out.at(g, b + 1))
                        if k:
                            pe.wait_ge(cmat_out.sem, cmat_out.at(g, k))
                        for i in range(HG):
                            ins = pe.matmul(psC[:, i * S:(i + 1) * S], kmask[:, b, h0 + i, :], x1T[:, b, :],
                                            start=True, stop=True)
                        ins.then_inc(qk_ps.sem, 1)
                    if k:
                        q = k - 1
                        b, h0 = q // 2, HG * (q % 2)
                        pe.wait_ge(cmat_out.sem, cmat_out.at(g, q + 1))
                        if q == 0:
                            pe.wait_ge(acol_out.sem, acol_out.at(g))
                            pe.wait_ge(expm_out.sem, expm_out.at(g))
                            pe.wait_ge(vaug_out.sem, vaug_out.at(g))
                        else:
                            pe.wait_ge(u_out.sem, u_out.at(g, q))
                        for i in range(HG):
                            ins = pe.matmul(psA[:, i * VW:(i + 1) * VW], cmat[q % 2][:, i, :], vaug[:, b * H + h0 + i, :],
                                            start=True, stop=True)
                        ins.then_inc(u_ps.sem, 1)
                elif step == "x2T":
                    pe.wait_ge(x2_out.sem, x2_out.at(g))
                    pe.wait_ge(u_out.sem, u_out.at(g))
                    for b in range(G):
                        ins = pe.transpose(psA[:, b * S:(b + 1) * S], acc[p][:, b, :], ident[:])
                    ins.then_inc(x2T_ps.sem, 1)
                elif step[0] == "hidden":
                    k = step[1]
                    if k == 0:
                        pe.wait_ge(x2lo_out.sem, x2lo_out.at(g))
                        pe.wait_ge(decay_out.sem, decay_out.at(g))
                        pe.wait_ge(cmat_out.sem, cmat_out.at(g))
                    if k >= 2:
                        pe.wait_ge(hidsq_out.sem, hidsq_out.at(g, k - 1))
                    split_product([psB, psC][k % 2][:], aw_hi[:, k, :], aw_lo[:, k, :],
                                  x2hi[p][:].rearrange("e b s -> e (b s)"),
                                  x2lo[p][:].rearrange("e b s -> e (b s)")).then_inc(hid_ps.sem, 1)
                elif step == "scores":
                    pe.wait_ge(hidsq_out.sem, hidsq_out.at(g))
                    pe.wait_ge(x2lo_out.sem, x2lo_out.at(g))
                    for b in range(G):
                        for k in range(AC):
                            ins = pe.matmul(psA[:, b * E:(b + 1) * E], hidsq[:, k, b * S:(b + 1) * S],
                                            expertsum[:, k, :], start=(k == 0), stop=(k == AC - 1))
                    ins.then_inc(sc_ps.sem, 1)

            def c(g, step):
                p = g.off % 2
                xh, xl = (t[p][:].rearrange("e b s -> e (b s)") for t in (x2hi, x2lo))
                if step[0] == "gu":
                    e, f = step[1], step[2]
                    n = e * FB + f
                    if n == 0:
                        pe.wait_ge(x2lo_out.sem, x2lo_out.at(g))
                        pe.wait_ge(x2hi_out.sem, x2hi_out.at(g))
                    cols = slice(f * 128, (f + 1) * 128)
                    if e:
                        pe.wait_ge(silu_out.sem, silu_out.at(g, n - 1))
                    elif not g.first(1):
                        pe.wait_ge(silu_out.sem, silu_out.at(g.back(1)))
                    split_product(psG[f][:], gw_hi[:, e, cols], gw_lo[:, e, cols], xh, xl).then_inc(g_ps.sem, 1)
                    if e:
                        pe.wait_ge(hid_out.sem, hid_out.at(g, n - 1))
                    elif not g.first(1):
                        pe.wait_ge(hid_out.sem, hid_out.at(g.back(1)))
                    split_product(psU[f][:], uw_hi[:, e, cols], uw_lo[:, e, cols], xh, xl).then_inc(u2_ps.sem, 1)
                elif step[0] == "down":
                    e = step[1]
                    pe.wait_ge(hid_out.sem, hid_out.at(g, e * FB + FB))
                    if e:
                        pe.wait_ge(acc_out.sem, acc_out.at(g, e))
                    elif not g.first(1):
                        pe.wait_ge(acc_out.sem, acc_out.at(g.back(1)))
                    for b in range(G):
                        for f in range(FB):
                            ins = pe.matmul(psY[:, b, :], hid[e % 2][f][:, b * S:(b + 1) * S], dwT[:, e, f, :],
                                            start=(f == 0), stop=(f == FB - 1))
                    ins.then_inc(y_ps.sem, 1)

            whole_program(pe, ab, c)

        @block.scalar
        def _(act):
            def ab(g, step):
                p = g.off % 2
                if step == "xT":
                    act.wait_ge(xT_ps.sem, xT_ps.at(g))
                    if not g.first(1):
                        act.wait_ge(logits_ps.sem, logits_ps.at(g.back(1)))
                    act.copy(xT[:].rearrange("e b s -> e (b s)"), psA[:]).then_inc(xT_sb.sem, 1)
                elif step == "zv":
                    act.wait_ge(z_ps.sem, z_ps.at(g))
                    act.copy(zT[:].rearrange("e b s -> e (b s)"), psB[:]).then_inc(zT_sb.sem, 1)
                elif step == "logits":
                    act.wait_ge(negmax_out.sem, negmax_out.at(g))
                    if not g.first(1):
                        act.wait_ge(pT_ps.sem, pT_ps.at(g.back(1)))
                        act.wait_ge(rown_out.sem, rown_out.at(g.back(1)))
                    for b in range(G):
                        ins = act.activation(probs[:, b, :], psA[:, b * S:(b + 1) * S], ACT.Exp,
                                             bias=negmax[:, b:b + 1], scale=1.0, accum_out=rowsum[:, b:b + 1])
                    ins.then_inc(probs_out.sem, 1)
                elif step == "pT":
                    act.wait_ge(cT_ps.sem, cT_ps.at(g))
                    if not g.first(1):
                        act.wait_ge(gates_ps.sem, gates_ps.at(g.back(1)))
                        act.wait_ge(kmask_out.sem, kmask_out.at(g.back(1)))
                    act.copy(cT[:].rearrange("e b s -> e (b s)"), psC[:]).then_inc(cT_sb.sem, 1)
                    act.wait_ge(pT_ps.sem, pT_ps.at(g))
                    if not g.first(1):
                        act.wait_ge(att_ps.sem, att_ps.at(g.back(1)))
                    act.copy(probsT[:].rearrange("e b s -> e (b s)"), psB[:]).then_inc(pT_sb.sem, 1)
                elif step == "x1T":
                    act.wait_ge(x1T_ps.sem, x1T_ps.at(g))
                    if not g.first(1):
                        act.wait_ge(qk_ps.sem, qk_ps.at(g.back(1)))
                    act.copy(x1T[:].rearrange("e b s -> e (b s)"), psB[:]).then_inc(x1T_sb.sem, 1)
                elif step == "gates":
                    act.wait_ge(fneg_out.sem, fneg_out.at(g))
                    act.activation(f_exp[:], f_neg[:], ACT.Exp).then_inc(fexp_out.sem, 1)
                    act.wait_ge(fexp_out.sem, fexp_out.at(g))
                    if not g.first(1):
                        act.wait_ge(logf_out.sem, logf_out.at(g.back(1)))
                    act.activation(f_ln[:], f_exp[:], ACT.Ln, bias=1.0).then_inc(fln_out.sem, 1)
                elif step == "am":
                    act.wait_ge(am_ps.sem, am_ps.at(g))
                    if not g.first(1):
                        act.wait_ge(nrm_out.sem, nrm_out.at(g.back(1)))
                    act.activation(expm[:], psA[:, GH:2 * GH], ACT.Exp, scale=-1.0).then_inc(expm_out.sem, 1)
                elif step[0] == "half" and step[1] < HALVES:
                    k = step[1]
                    b, h0 = k // 2, HG * (k % 2)
                    act.wait_ge(mb_ps.sem, mb_ps.at(g, k + 1))
                    if k == 0:
                        act.wait_ge(acol_out.sem, acol_out.at(g))
                    if k >= 2:
                        act.wait_ge(cmat_out.sem, cmat_out.at(g, k - 1))
                    elif not g.first(1):
                        act.wait_ge(cmat_out.sem, cmat_out.at(g.back(1)))
                    for i in range(HG):
                        r = b * H + h0 + i
                        ins = act.activation(decay[k % 2][:, i, :], psB[:, i * S:(i + 1) * S], ACT.Exp,
                                             bias=acol[:, r:r + 1], scale=-1.0)
                    ins.then_inc(decay_out.sem, 1)
                elif step == "x2T":
                    act.wait_ge(x2T_ps.sem, x2T_ps.at(g))
                    if not g.first(2):
                        act.wait_ge(u2_ps.sem, u2_ps.at(g.back(2)))
                    act.copy(x2hi[p][:].rearrange("e b s -> e (b s)"), psA[:]).then_inc(x2hi_out.sem, 1)
                elif step[0] == "hidden":
                    k = step[1]
                    act.wait_ge(hid_ps.sem, hid_ps.at(g, k + 1))
                    if k == 0 and not g.first(1):
                        act.wait_ge(sc_ps.sem, sc_ps.at(g.back(1)))
                    act.activation(hidsq[:, k, :], [psB, psC][k % 2][:], ACT.Square).then_inc(hidsq_out.sem, 1)
                elif step == "router":
                    act.wait_ge(sdiff_out.sem, sdiff_out.at(g))
                    if not g.first(1):
                        act.wait_ge(wexp_out.sem, wexp_out.at(g.back(1)))
                    act.activation(sexp[:], sdiff[:], ACT.Exp).then_inc(sexp_out.sem, 1)

            def c(g, step):
                if step[0] == "gu":
                    e, f = step[1], step[2]
                    n = e * FB + f
                    act.wait_ge(g_ps.sem, g_ps.at(g, n + 1))
                    if e:
                        act.wait_ge(silu_out.sem, silu_out.at(g, n - 1))
                    elif not g.first(1):
                        act.wait_ge(silu_out.sem, silu_out.at(g.back(1)))
                    act.activation(tanh[f][:], psG[f][:], ACT.Tanh, scale=0.5).then_inc(tanh_out.sem, 1)

            whole_program(act, ab, c)

        @block.vector
        def _(dve):
            splits = 0
            for n, item in enumerate(PREP):
                ps = prep_bank(n)
                dve.wait_ge(prep_ps, n + 1)
                if item == "small":
                    dve.tensor_copy(qk_w[:], ps[:, 0:128])
                    dve.tensor_copy(wvT[:], ps[:, 128:256])
                    dve.tensor_copy(gate_xT[:], ps[:, 256:256 + 2 * H])
                    dve.tensor_copy(gate_t[:], ps[:, 256 + 2 * H:256 + 4 * H]).then_inc(gate_step, 1)
                    dve.wait_ge(gate_step, 1)
                    dve.tensor_tensor(gate_cT[:], ps[:, 256 + 4 * H:256 + 6 * H], gate_t[:], ALU.add)\
                        .then_inc(gate_step, 1)
                    dve.wait_ge(gate_step, 2)
                    dve.wait_ge(const_ready, 1)
                    for s, src in enumerate((gate_xT, gate_cT)):
                        for b in range(G):
                            for k in range(2):
                                ins = dve.tensor_copy(gate_p[:, s, b, k * GH + b * H:k * GH + (b + 1) * H],
                                                      src[:, k * H:(k + 1) * H])
                    ins.then_inc(prep_out, 1)
                    continue
                if item[0] == "wbT":
                    dve.tensor_copy(wbT[:, 2 * item[1]:2 * item[1] + 2, :].rearrange("r e f -> r (e f)"),
                                    ps[0:R, :]).then_inc(prep_out, 1)
                    continue
                if item[0] == "down":
                    dve.tensor_copy(dwT[:, 2 * item[1]:2 * item[1] + 2, :, :].rearrange("f e k h -> f (e k h)"),
                                    ps[:]).then_inc(prep_out, 1)
                    continue
                if item == "wa":
                    hi, lo = (t[:].rearrange("h c r -> h (c r)") for t in (aw_hi, aw_lo))
                else:
                    pair = (gw_hi, gw_lo) if item[0] == "gw" else (uw_hi, uw_lo)
                    hi, lo = (t[:, 2 * item[1]:2 * item[1] + 2, :].rearrange("h e f -> h (e f)") for t in pair)
                splits += 1
                dve.tensor_copy(hi, ps[:]).then_inc(prep_hi, 1)
                dve.wait_ge(prep_hi, splits)
                dve.tensor_tensor(lo, ps[:], hi.bitcast(F32), ALU.subtract).then_inc(prep_out, 1)

            def layer_stats(g, src, bn, mv, bn_stage, mv_stage):
                for b in range(G):
                    ins = dve.bn_stats(bn[:, b, :], src[:, b, :])
                ins.then_inc(bn_stage.sem, 1)
                plain_wait(dve)
                dve.wait_ge(bn_stage.sem, bn_stage.at(g))
                for b in range(G):
                    ins = dve.bn_aggr(mv[:, b, :], bn[:, b, :])
                ins.then_inc(mv_stage.sem, 1)

            def normalize(g, dst, src, mv, rstd, rstd_stage, out_stage):
                dve.wait_ge(rstd_stage.sem, rstd_stage.at(g))
                for b in range(G):
                    ins = dve.tensor_scalar(dst[:, b, :], src[:, b, :], mv[:, b, 0:1], rstd[:, b:b + 1],
                                            ALU.subtract, ALU.mult)
                ins.then_inc(out_stage.sem, 1)

            def ab(g, step):
                p = g.off % 2
                if step == "xT":
                    dve.wait_ge(c_loaded[p].sem, c_loaded[p].at_parity(g))
                    if not g.first(1):
                        dve.wait_ge(vmean_out.sem, vmean_out.at(g.back(1)))
                    dve.tensor_reduce(vsum[:], cin[p][:].rearrange("t b (h d) -> t (b h) d", d=DH), AX_X, ALU.add)\
                        .then_inc(vsum_out.sem, 1)
                    dve.wait_ge(vsum_out.sem, vsum_out.at(g))
                    if not g.first(1):
                        dve.wait_ge(vc_out.sem, vc_out.at(g.back(1)))
                    dve.tensor_scalar(vmean[:], vsum[:], 1.0 / DH, None, ALU.mult).then_inc(vmean_out.sem, 1)
                elif step == "zv":
                    dve.wait_ge(v_ps.sem, v_ps.at(g))
                    if not g.first(1):
                        dve.wait_ge(att_ps.sem, att_ps.at(g.back(1)))
                    dve.tensor_copy(v_sb[:].rearrange("e b s -> e (b s)"), psC[:]).then_inc(v_out.sem, 1)
                elif step == "logits":
                    dve.wait_ge(logits_ps.sem, logits_ps.at(g))
                    dve.tensor_reduce(rowmax[:], psA[:].rearrange("n (b m) -> n b m", b=G), AX_X, ALU.max)\
                        .then_inc(max_out.sem, 1)
                    dve.wait_ge(max_out.sem, max_out.at(g))
                    if not g.first(1):
                        dve.wait_ge(probs_out.sem, probs_out.at(g.back(1)))
                    dve.tensor_scalar(negmax[:], rowmax[:], -1.0, None, ALU.mult).then_inc(negmax_out.sem, 1)
                elif step == "pT":
                    dve.wait_ge(probs_out.sem, probs_out.at(g))
                    dve.tensor_scalar(rowsum_n[:], rowsum[:], float(D) ** 0.5, None, ALU.mult).then_inc(rown_out.sem, 1)
                    dve.wait_ge(rown_out.sem, rown_out.at(g))
                    dve.reciprocal(rowinv[:], rowsum_n[:]).then_inc(rowinv_out.sem, 1)
                elif step == "att":
                    dve.wait_ge(rowinv_out.sem, rowinv_out.at(g))
                    dve.wait_ge(att_ps.sem, att_ps.at(g))
                    for b in range(G):
                        ins = dve.scalar_tensor_tensor(out=res1[:, b, :], in0=psA[:, b * D:(b + 1) * D],
                                                       scalar=rowinv[:, b:b + 1], in1=xin[p][:, b, :],
                                                       op0=ALU.mult, op1=ALU.add)
                    ins.then_inc(res1_out.sem, 1)
                    dve.wait_ge(res1_out.sem, res1_out.at(g))
                    if not g.first(1):
                        dve.wait_ge(var1_out.sem, var1_out.at(g.back(1)))
                    layer_stats(g, res1, bn6, mv1, bn1_out, mv1_out)
                elif step == "x1":
                    if not g.first(1):
                        dve.wait_ge(x1T_ps.sem, x1T_ps.at(g.back(1)))
                        dve.wait_ge(res2_out.sem, res2_out.at(g.back(1)))
                    normalize(g, x1, res1, mv1, rstd1, rstd1_out, x1_out)
                elif step == "gates":
                    dve.wait_ge(gates_ps.sem, gates_ps.at(g))
                    dve.tensor_scalar(f_in[:], psC[GH:2 * GH, 0:S], gbias[GH:2 * GH, 0:1], None, ALU.add)\
                        .then_inc(f_out.sem, 1)
                    dve.wait_ge(f_out.sem, f_out.at(g))
                    if not g.first(1):
                        dve.wait_ge(fexp_out.sem, fexp_out.at(g.back(1)))
                    dve.scalar_tensor_tensor(out=f_neg[:], in0=f_in[:], scalar=-1.0, in1=f_in[:], op0=ALU.mult,
                                             op1=ALU.min).then_inc(fneg_out.sem, 1)
                elif step == "scan":
                    dve.wait_ge(fln_out.sem, fln_out.at(g))
                    dve.scalar_tensor_tensor(out=logf[:], in0=f_in[:], scalar=0.0, in1=f_ln[:], op0=ALU.min,
                                             op1=ALU.subtract).then_inc(logf_out.sem, 1)
                    dve.wait_ge(logf_out.sem, logf_out.at(g))
                    dve.tensor_tensor_scan(cumf[:], ones[:], logf[:], 0.0, ALU.mult, ALU.add)\
                        .then_inc(cumf_out.sem, 1)
                    dve.wait_ge(cumf_out.sem, cumf_out.at(g))
                    if not g.first(1):
                        dve.wait_ge(am_ps.sem, am_ps.at(g.back(1)))
                    dve.scalar_tensor_tensor(out=arow[:], in0=psC[0:GH, 0:S], scalar=gbias[0:GH, 0:1], in1=cumf[:],
                                             op0=ALU.add, op1=ALU.subtract).then_inc(arow_out.sem, 1)
                    dve.wait_ge(arow_out.sem, arow_out.at(g))
                    if not g.first(1):
                        dve.wait_ge(mb_ps.sem, mb_ps.at(g.back(1)))
                    dve.tensor_tensor_scan(amax[:], arow[:], arow[:], -3.0e38, ALU.max, ALU.max)\
                        .then_inc(amax_out.sem, 1)
                    dve.wait_ge(amax_out.sem, amax_out.at(g))
                    dve.tensor_tensor(mrow[:], cumf[:], amax[:], ALU.add).then_inc(mrow_out.sem, 1)
                elif step == "am":
                    dve.wait_ge(am_ps.sem, am_ps.at(g))
                    dve.wait_ge(expm_out.sem, expm_out.at(g))
                    if not g.first(1):
                        dve.wait_ge(decay_out.sem, decay_out.at(g.back(1)))
                    dve.tensor_copy(acol[:], psA[:, 0:GH]).then_inc(acol_out.sem, 1)
                elif step[0] == "half":
                    k = step[1]
                    if k < HALVES:
                        dve.wait_ge(qk_ps.sem, qk_ps.at(g, k + 1))
                        dve.wait_ge(decay_out.sem, decay_out.at(g, k + 1))
                        if k >= 2:
                            dve.wait_ge(u_ps.sem, u_ps.at(g, k - 1))
                        elif not g.first(1):
                            dve.wait_ge(u_ps.sem, u_ps.at(g.back(1)))
                        dve.scalar_tensor_tensor(out=cmat[k % 2][:].rearrange("t h s -> t (h s)"), in0=psC[:],
                                                 scalar=float(DH) ** -0.5,
                                                 in1=decay[k % 2][:].rearrange("t h s -> t (h s)"),
                                                 op0=ALU.mult, op1=ALU.mult).then_inc(cmat_out.sem, 1)
                    if k:
                        q = k - 1
                        dve.wait_ge(u_ps.sem, u_ps.at(g, q + 1))
                        if q == 0 and not g.first(1):
                            dve.wait_ge(usq_out.sem, usq_out.at(g.back(1)))
                            dve.wait_ge(hn_out.sem, hn_out.at(g.back(1)))
                        dve.tensor_copy(u_sb[:, q * HG:(q + 1) * HG, :].rearrange("s h d -> s (h d)"),
                                        psA[:, 0:HG * VW]).then_inc(u_out.sem, 1)
                elif step == "post":
                    dve.wait_ge(u_out.sem, u_out.at(g))
                    dve.wait_ge(expm_out.sem, expm_out.at(g))
                    dve.scalar_tensor_tensor(out=sum_abs[:], in0=u_sb[:, :, 2 * DH], scalar=-1.0,
                                             in1=u_sb[:, :, 2 * DH], op0=ALU.mult, op1=ALU.max)\
                        .then_inc(sumabs_out.sem, 1)
                    dve.wait_ge(sumabs_out.sem, sumabs_out.at(g))
                    dve.tensor_tensor(nrm[:], sum_abs[:], expm[:], ALU.max).then_inc(nrm_out.sem, 1)
                    dve.wait_ge(nrm_out.sem, nrm_out.at(g))
                    dve.tensor_scalar(nrm_e[:], nrm[:], GATE_EPS, NORM_EPS ** 0.5, ALU.add, ALU.mult)\
                        .then_inc(nrme_out.sem, 1)
                    dve.wait_ge(nrme_out.sem, nrme_out.at(g))
                    dve.tensor_tensor(nrm_2[:], nrm_e[:], nrm_e[:], ALU.mult).then_inc(nrm2_out.sem, 1)
                    dve.wait_ge(usq_out.sem, usq_out.at(g))
                    dve.tensor_reduce(uss[:], usq[:], AX_X, ALU.add).then_inc(uss_out.sem, 1)
                    dve.wait_ge(uss_out.sem, uss_out.at(g))
                    dve.wait_ge(nrm2_out.sem, nrm2_out.at(g))
                    if not g.first(1):
                        dve.wait_ge(hrstd_out.sem, hrstd_out.at(g.back(1)))
                    dve.scalar_tensor_tensor(out=hvar[:], in0=uss[:], scalar=1.0 / DH, in1=nrm_2[:],
                                             op0=ALU.mult, op1=ALU.add).then_inc(hvar_out.sem, 1)
                    dve.wait_ge(hrstd_out.sem, hrstd_out.at(g))
                    dve.tensor_tensor(hn[:], u_sb[:, :, DH:2 * DH], hrstd[:].unsqueeze(2).to_broadcast([S, GH, DH]),
                                      ALU.mult).then_inc(hn_out.sem, 1)
                    dve.wait_ge(hn_out.sem, hn_out.at(g))
                    dve.tensor_tensor(res2[:].rearrange("s b e -> s (b e)"), hn[:].rearrange("s h d -> s (h d)"),
                                      x1[:].rearrange("s b e -> s (b e)"), ALU.add).then_inc(res2_out.sem, 1)
                    dve.wait_ge(res2_out.sem, res2_out.at(g))
                    if not g.first(1):
                        dve.wait_ge(var2_out.sem, var2_out.at(g.back(1)))
                    layer_stats(g, res2, bn6b, mv2, bn2_out, mv2_out)
                elif step == "x2":
                    if not g.first(2):
                        dve.wait_ge(y_ready.sem, y_ready.at(g.back(2)))
                    normalize(g, acc[p], res2, mv2, rstd2, rstd2_out, x2_out)
                elif step == "x2T":
                    dve.wait_ge(x2hi_out.sem, x2hi_out.at(g))
                    if not g.first(2):
                        dve.wait_ge(u2_ps.sem, u2_ps.at(g.back(2)))
                    dve.tensor_tensor(x2lo[p][:].rearrange("e b s -> e (b s)"), psA[:],
                                      x2hi[p][:].rearrange("e b s -> e (b s)").bitcast(F32),
                                      ALU.subtract).then_inc(x2lo_out.sem, 1)
                elif step == "scores":
                    dve.wait_ge(sc_ps.sem, sc_ps.at(g))
                    if not g.first(1):
                        dve.wait_ge(score_out.sem, score_out.at(g.back(1)))
                    dve.tensor_copy(sc2[:].rearrange("p g e -> p (g e)"), psA[:, 0:G * E]).then_inc(sc2_out.sem, 1)
                elif step == "router":
                    def token(t):
                        return t.unsqueeze(2).to_broadcast([S, G, E])
                    plain_wait(dve)
                    dve.wait_ge(score_out.sem, score_out.at(g))
                    for b in range(G):
                        ins = dve.max(top8[:, b, :], score[:, b, :])
                    ins.then_inc(top_out.sem, 1)
                    dve.wait_ge(top_out.sem, top_out.at(g))
                    dve.tensor_tensor(is1[:], top8[:, :, 0], top8[:, :, 1], ALU.is_gt).then_inc(is1_out.sem, 1)
                    dve.tensor_tensor(above[:], score[:], token(top8[:, :, 1]), ALU.is_gt)
                    dve.tensor_tensor(equal[:], score[:], token(top8[:, :, 1]), ALU.is_equal).then_inc(eq_out.sem, 1)
                    if not g.first(1):
                        dve.wait_ge(sexp_out.sem, sexp_out.at(g.back(1)))
                    dve.tensor_tensor(sdiff[:], score[:], token(top8[:, :, 0]), ALU.subtract).then_inc(sdiff_out.sem, 1)
                    dve.wait_ge(is1_out.sem, is1_out.at(g))
                    dve.tensor_scalar(lim[:], is1[:], -1.0, 2.0, ALU.mult, ALU.add).then_inc(lim_out.sem, 1)
                    dve.wait_ge(eq_out.sem, eq_out.at(g))
                    dve.tensor_tensor_scan(rank[:].rearrange("p g e -> p (g e)"), restart[:].rearrange("p g e -> p (g e)"),
                                           equal[:].rearrange("p g e -> p (g e)"), 0.0, ALU.mult, ALU.add)\
                        .then_inc(rank_out.sem, 1)
                    dve.wait_ge(rank_out.sem, rank_out.at(g))
                    dve.wait_ge(lim_out.sem, lim_out.at(g))
                    dve.tensor_tensor(inlim[:], rank[:], token(lim[:]), ALU.is_le).then_inc(inlim_out.sem, 1)
                    dve.wait_ge(inlim_out.sem, inlim_out.at(g))
                    dve.tensor_tensor(chosen2[:], inlim[:], equal[:], ALU.mult).then_inc(ch2_out.sem, 1)
                    dve.wait_ge(ch2_out.sem, ch2_out.at(g))
                    dve.tensor_tensor(chosen[:], chosen2[:], above[:], ALU.add).then_inc(sel_out.sem, 1)
                    dve.wait_ge(sel_out.sem, sel_out.at(g))
                    dve.wait_ge(sexp_out.sem, sexp_out.at(g))
                    dve.tensor_tensor(wexp[:], chosen[:], sexp[:], ALU.mult).then_inc(wexp_out.sem, 1)
                    dve.wait_ge(wexp_out.sem, wexp_out.at(g))
                    dve.tensor_reduce(wden[:], wexp[:], AX_X, ALU.add).then_inc(wden_out.sem, 1)
                    dve.wait_ge(wden_out.sem, wden_out.at(g))
                    dve.reciprocal(winv[:], wden[:]).then_inc(winv_out.sem, 1)
                    dve.wait_ge(winv_out.sem, winv_out.at(g))
                    dve.tensor_tensor(wtok[p][:], wexp[:], token(winv[:]), ALU.mult).then_inc(wtok_out.sem, 1)

            def c(g, step):
                p = g.off % 2
                if step[0] == "gu":
                    e, f = step[1], step[2]
                    n = e * FB + f
                    dve.wait_ge(tanh_out.sem, tanh_out.at(g, n + 1))
                    dve.scalar_tensor_tensor(out=silu2[f][:], in0=tanh[f][:], scalar=1.0, in1=psG[f][:],
                                             op0=ALU.add, op1=ALU.mult).then_inc(silu_out.sem, 1)
                    dve.wait_ge(silu_out.sem, silu_out.at(g, n + 1))
                    dve.wait_ge(u2_ps.sem, u2_ps.at(g, n + 1))
                    if e >= 2:
                        dve.wait_ge(y_ps.sem, y_ps.at(g, e - 1))
                    elif not g.first(1):
                        dve.wait_ge(y_ps.sem, y_ps.at(g.back(1)))
                    dve.scalar_tensor_tensor(out=hid[e % 2][f][:], in0=silu2[f][:], scalar=0.5, in1=psU[f][:],
                                             op0=ALU.mult, op1=ALU.mult).then_inc(hid_out.sem, 1)
                elif step[0] == "down":
                    e = step[1]
                    dve.wait_ge(y_ps.sem, y_ps.at(g, e + 1))
                    if e == 0:
                        dve.wait_ge(wtok_out.sem, wtok_out.at(g))
                        dve.wait_ge(x2_out.sem, x2_out.at(g))
                        dve.wait_ge(x2T_ps.sem, x2T_ps.at(g))
                    else:
                        dve.wait_ge(acc_out.sem, acc_out.at(g, e))
                    for b in range(G):
                        ins = dve.scalar_tensor_tensor(out=acc[p][:, b, :], in0=psY[:, b, :],
                                                       scalar=wtok[p][:, b, e:e + 1], in1=acc[p][:, b, :],
                                                       op0=ALU.mult, op1=ALU.add)
                    ins.then_inc(acc_out.sem, 1)
                elif step == "final":
                    dve.wait_ge(acc_out.sem, acc_out.at(g))
                    if not g.first(1):
                        dve.wait_ge(var3_out.sem, var3_out.at(g.back(1)))
                    layer_stats(g, acc[p], bn6c, mv3, bn3_out, mv3_out)
                    if not g.first(1):
                        dve.wait_ge(stored.sem, stored.at(g.back(1)))
                    normalize(g, y_out, acc[p], mv3, rstd3, rstd3_out, y_ready)

            whole_program(dve, ab, c)


_INS = ["x", "ctx_1024", "L0_attn_Wq", "L0_attn_Wk", "L0_attn_Wv", "L0_xattn_igate_w", "L0_xattn_igate_b",
        "L0_xattn_fgate_w", "L0_xattn_fgate_b", "L0_xattn_out_w", "L0_ffn_W_A", "L0_ffn_W_B", "L0_ffn_W_up",
        "L0_ffn_W_down"]


def kernel(**inputs):
    import numpy as np
    import concourse.bacc as bacc
    from concourse.bass_utils import run_bass_kernel_spmd

    nc = bacc.Bacc("TRN2", target_bir_lowering=False, num_devices=1)
    arrays, args = {}, []
    for name in _INS:
        a = np.ascontiguousarray(inputs[name])
        arrays[f"in_{name}"] = a
        args.append(nc.dram_tensor(f"in_{name}", a.shape, mybir.dt.from_np(a.dtype), kind="ExternalInput").ap())
    args.append(nc.dram_tensor("out_0", inputs["x"].shape, F32, kind="ExternalOutput").ap())
    decoder_kernel(nc, *args)
    r = run_bass_kernel_spmd(nc, [arrays], core_ids=[0])
    return r.results[0]["out_0"]
```

```python
from contextlib import ExitStack

import concourse.bass as bass
from concourse import mybir

ALU = mybir.AluOpType
ACT = mybir.ActivationFunctionType
F32 = mybir.dt.float32
F32R = mybir.dt.float32r
BF16 = mybir.dt.bfloat16
AX_X = mybir.AxisListType.X

NORM_EPS = 1e-5
GATE_EPS = 1e-6
MASKED = 1e30


class Stage:

    def __init__(self, sem, per):
        self.sem, self.per = sem, per

    def at(self, g, k=None):
        k = self.per if k is None else k
        return g.j * (2 * self.per) + (g.off * self.per + k)

    def at_parity(self, g):
        return g.j * self.per + (g.off // 2 + 1) * self.per


class Group:

    def __init__(self, j, off):
        self.j, self.off = j, off

    def back(self, n):
        return Group(self.j, self.off - n)

    def number(self):
        return self.j * 2 + self.off

    def first(self, n):
        return isinstance(self.j, int) and self.number() < n


def decoder_kernel(nc, x, ctx_in, wq, wk, wv, igate_w, igate_b, fgate_w, fgate_b, out_w,
                   w_a, w_b, w_up, w_down, out):
    B, S, D = x.shape
    H = igate_b.shape[0]
    DH = D // H
    E, R, _ = w_a.shape
    F = w_up.shape[1]
    FB = F // 128
    G = 4
    N = G * S
    GROUPS = B // G
    HG = 4
    HALVES = G * H // HG
    AC = E * R // 128
    VW = 2 * DH + 1
    GH = G * H
    assert S == 128 and D == 128 and GROUPS % 2 == 0 and R == 64 and FB == 2

    x_g = x.rearrange("(g b) n e -> g n b e", b=G)
    c_g = ctx_in.rearrange("(g b) n e -> g n b e", b=G)
    o_g = out.rearrange("(g b) n e -> g n b e", b=G)

    with ExitStack() as ctx:
        def sb(name, shape, dt=F32):
            return ctx.enter_context(nc.sbuf_tensor(name, shape, dt))

        def psum(name, shape, dt=F32):
            return ctx.enter_context(nc.psum_tensor(name, shape, dt))

        def sem(name):
            return ctx.enter_context(nc.semaphore(name))

        def stage(name, per=1):
            return Stage(sem(name), per)

        psG = [psum(f"psG{i}", [128, N]) for i in range(2)]
        psU = [psum(f"psU{i}", [128, N]) for i in range(2)]
        psY = psum("psY", [128, G, D])
        psA = psum("psA", [128, 512])
        psB = psum("psB", [128, 512])
        psC = psum("psC", [128, 512])

        ident = sb("ident", [128, 128])
        identb = sb("identb", [128, 128], BF16)
        future = sb("future", [128, HG, 128], BF16)
        headmask = sb("headmask", [128, H])
        restart = sb("restart", [128, G, E])
        minusone = sb("minusone", [128, G])
        epsilon = sb("epsilon", [128, G])
        minushalf = sb("minushalf", [128, GH])
        plushalf = sb("plushalf", [128, GH])
        ones = sb("ones", [GH, 128])

        y_out = sb("y_out", [S, G, D])
        wq_n, wk_n, wv_n = (y_out[:, i, :] for i in range(3))
        gate_n = sb("gate_n", [2 * H, 3 * D])
        gbias = sb("gbias", [2 * GH, 1])
        outw = sb("outw", [128, D])
        wa_r = sb("wa_r", [R, E, D])
        wa_n = sb("wa_n", [128, AC, D])
        wb_n = sb("wb_n", [128, E, FB, R])
        wup_n = sb("wup_n", [128, E, FB, D])
        wdn_n = sb("wdn_n", [D, E, FB, 128])

        qk_w = sb("qk_w", [D, D])
        wvT = sb("wvT", [D, D])
        gate_xT = sb("gate_xT", [D, 2 * H])
        gate_cT = sb("gate_cT", [D, 2 * H])
        gate_t = sb("gate_t", [D, 2 * H])
        gate_p = sb("gate_p", [D, 2, G, 2 * GH])
        wbT = sb("wbT", [R, E, F])
        gw_hi = sb("gw_hi", [D, E, F], F32R)
        gw_lo = sb("gw_lo", [D, E, F], F32R)
        uw_hi = sb("uw_hi", [D, E, F], F32R)
        uw_lo = sb("uw_lo", [D, E, F], F32R)
        aw_hi = sb("aw_hi", [D, E * R], F32R)
        aw_lo = sb("aw_lo", [D, E * R], F32R)
        dwT = sb("dwT", [128, E, FB, D])

        xin = [sb(f"xin{i}", [128, G, D]) for i in range(2)]
        cin = [sb(f"cin{i}", [128, G, D]) for i in range(2)]
        xT = sb("xT", [D, G, S])
        zT = sb("zT", [D, G, S])
        v_sb = sb("v_sb", [S, G, D])
        rowmax = sb("rowmax", [S, G])
        negmax = sb("negmax", [S, G])
        probs = sb("probs", [S, G, S])
        rowsum = sb("rowsum", [S, G])
        rowsum_n = sb("rowsum_n", [S, G])
        rowinv = sb("rowinv", [S, G])
        probsT = sb("probsT", [S, G, S])
        res1 = sb("res1", [S, G, D])
        bn6 = sb("bn6", [S, G, 6])
        mv1 = sb("mv1", [S, G, 2])
        var1 = sb("var1", [S, G])
        rstd1 = sb("rstd1", [S, G])
        x1 = sb("x1", [S, G, D])
        x1T = sb("x1T", [D, G, S])
        cT = sb("cT", [D, G, S])
        kmask = sb("kmask", [D, 2, H, S])
        vmean = sb("vmean", [S, GH])
        vsum = sb("vsum", [S, GH])
        vaug = sb("vaug", [S, GH, VW])
        f_in = sb("f_in", [GH, S])
        f_neg = sb("f_neg", [GH, S])
        f_exp = sb("f_exp", [GH, S])
        f_ln = sb("f_ln", [GH, S])
        logf = sb("logf", [GH, S])
        cumf = sb("cumf", [GH, S])
        arow = sb("arow", [GH, S])
        amax = sb("amax", [GH, S])
        amax2 = sb("amax2", [2 * GH, S], F32R)
        amaxd = sb("amaxd", [2 * GH, H, S], F32R)
        batch_rows = sb("batch_rows", [2 * GH, G], F32R)
        batch_2 = sb("batch_2", [2 * GH, 2, G])
        head_rows = sb("head_rows", [2 * GH, H])
        head_8 = sb("head_8", [2 * GH, 2 * G, H])
        mrow = sb("mrow", [GH, S])
        acol = sb("acol", [S, GH])
        expm = sb("expm", [S, GH])
        decay = [sb(f"decay{i}", [S, HG, S]) for i in range(2)]
        cmat = [sb(f"cmat{i}", [S, HG, S]) for i in range(2)]
        u_sb = sb("u_sb", [S, GH, VW])
        usq = sb("usq", [S, H, DH])
        uss = sb("uss", [S, GH])
        sum_abs = sb("sum_abs", [S, GH])
        nrm = sb("nrm", [S, GH])
        nrm_e = sb("nrm_e", [S, GH])
        nrm_2 = sb("nrm_2", [S, GH])
        hvar = sb("hvar", [S, GH])
        hrstd = sb("hrstd", [S, GH])
        hn = sb("hn", [S, H, DH])
        res2 = sb("res2", [S, G, D])
        bn6b = sb("bn6b", [S, G, 6])
        mv2 = sb("mv2", [S, G, 2])
        var2 = sb("var2", [S, G])
        rstd2 = sb("rstd2", [S, G])

        acc = [sb(f"acc{i}", [S, G, D]) for i in range(2)]
        x2hi = [sb(f"x2hi{i}", [D, G, S], F32R) for i in range(2)]
        x2lo = [sb(f"x2lo{i}", [D, G, S], F32R) for i in range(2)]
        hidsq = [sb(f"hidsq{i}", [S, E * R]) for i in range(2)]
        sc2 = sb("sc2", [S, G, E])
        score = sb("score", [S, G, E])
        top8 = sb("top8", [S, G, 8])
        is1 = sb("is1", [S, G])
        smax = sb("smax", [S, G])
        lim = sb("lim", [S, G])
        above = sb("above", [S, G, E])
        equal = sb("equal", [S, G, E])
        rank = sb("rank", [S, G, E])
        inlim = sb("inlim", [S, G, E])
        chosen2 = sb("chosen2", [S, G, E])
        chosen = sb("chosen", [S, G, E])
        sdiff = sb("sdiff", [S, G, E])
        sexp = sb("sexp", [S, G, E])
        wexp = sb("wexp", [S, G, E])
        wden = sb("wden", [S, G])
        winv = sb("winv", [S, G])
        wtok = [sb(f"wtok{i}", [S, G, E]) for i in range(2)]
        tanh = [sb(f"tanh{i}", [128, N]) for i in range(2)]
        silu2 = [sb(f"silu2{i}", [128, N]) for i in range(2)]
        hid = [[sb(f"hid{i}{f}", [128, N]) for f in range(FB)] for i in range(2)]
        up = sb("up", [128, N])
        POOL_BLOCKS = (1,)
        bn6c = sb("bn6c", [S, G, 6])
        mv3 = sb("mv3", [S, G, 2])
        var3 = sb("var3", [S, G])
        rstd3 = sb("rstd3", [S, G])
        negmean3 = sb("negmean3", [S, G])
        nmr3 = sb("nmr3", [S, G])

        w_loaded = sem("w_loaded")
        e_loaded = sem("e_loaded")
        const_step = sem("const_step")
        const_ready = sem("const_ready")
        prep_ps = sem("prep_ps")
        prep_out = sem("prep_out")
        prep_hi = sem("prep_hi")
        gate_step = sem("gate_step")
        rows_ready = sem("rows_ready")

        x_loaded = [stage(f"x_loaded{i}", 16) for i in range(2)]
        c_loaded = [stage(f"c_loaded{i}", 16) for i in range(2)]
        xT_ps, xT_sb = stage("xT_ps"), stage("xT_sb")
        z_ps, zT_sb = stage("z_ps"), stage("zT_sb")
        v_ps, v_out = stage("v_ps"), stage("v_out")
        logits_ps, max_out, negmax_out = stage("logits_ps"), stage("max_out"), stage("negmax_out")
        probs_out, rown_out, rowinv_out = stage("probs_out"), stage("rown_out"), stage("rowinv_out")
        pT_ps, pT_sb = stage("pT_ps"), stage("pT_sb")
        cT_ps, cT_sb = stage("cT_ps"), stage("cT_sb")
        kmask_out = stage("kmask_out", G)
        vsum_out, vmean_out, vc_out, vaug_out = stage("vsum_out"), stage("vmean_out"), stage("vc_out"), stage("vaug_out")
        att_ps, res1_out, bn1_out, mv1_out = stage("att_ps"), stage("res1_out"), stage("bn1_out"), stage("mv1_out")
        var1_out, rstd1_out, x1_out = stage("var1_out"), stage("rstd1_out"), stage("x1_out")
        x1T_ps, x1T_sb = stage("x1T_ps"), stage("x1T_sb")
        gates_ps = stage("gates_ps")
        f_out, fneg_out, fexp_out, fln_out = stage("f_out"), stage("fneg_out"), stage("fexp_out"), stage("fln_out")
        logf_out, cumf_out, arow_out = stage("logf_out"), stage("cumf_out"), stage("arow_out")
        amaxd0_out, amaxd1_out = stage("amaxd0_out"), stage("amaxd1_out")
        amaxhi_out, amax2_out = stage("amaxhi_out"), stage("amax2_out")
        amax_out, mrow_out = stage("amax_out"), stage("mrow_out")
        am_ps, acol_out, expm_out = stage("am_ps"), stage("acol_out"), stage("expm_out")
        mb_ps, qk_ps = stage("mb_ps", HALVES), stage("qk_ps", HALVES)
        decay_out, cmat_out = stage("decay_out", HALVES), stage("cmat_out", HALVES)
        u_ps, u_out = stage("u_ps", HALVES), stage("u_out", HALVES)
        usq_out, uss_out = stage("usq_out", G), stage("uss_out", G)
        sumabs_out = stage("sumabs_out", G)
        nrm_out, nrme_out, nrm2_out = stage("nrm_out", G), stage("nrme_out", G), stage("nrm2_out", G)
        hvar_out, hrstd_out, hn_out = stage("hvar_out", G), stage("hrstd_out", G), stage("hn_out", G)
        res2_out, bn2_out, mv2_out = stage("res2_out", G), stage("bn2_out", G), stage("mv2_out", G)
        var2_out, rstd2_out, x2_out = stage("var2_out"), stage("rstd2_out"), stage("x2_out")
        x2T_ps, x2hi_out, x2lo_out = stage("x2T_ps"), stage("x2hi_out"), stage("x2lo_out")
        hid_ps, hidsq_out = stage("hid_ps", G), stage("hidsq_out", G)
        sc2_out, score_out = stage("sc2_out", G), stage("score_out")
        top_out, is1_out, lim_out = stage("top_out"), stage("is1_out"), stage("lim_out")
        above_out, smax_out, nmr3_out = stage("above_out"), stage("smax_out"), stage("nmr3_out")
        negmean3_out = stage("negmean3_out")
        up_out = stage("up_out", E)
        hid_pool_out = stage("hid_pool_out", E)
        eq_out, rank_out, inlim_out = stage("eq_out"), stage("rank_out"), stage("inlim_out")
        ch2_out, sel_out, sdiff_out = stage("ch2_out"), stage("sel_out"), stage("sdiff_out")
        sexp_out, wexp_out, wden_out = stage("sexp_out"), stage("wexp_out"), stage("wden_out")
        winv_out, wtok_out = stage("winv_out"), stage("wtok_out")
        g_ps, u2_ps = stage("g_ps", E * FB), stage("u2_ps", E * FB)
        tanh_out, silu_out, hid_out = stage("tanh_out", E * FB), stage("silu_out", E * FB), stage("hid_out", E)
        y_ps, acc_out = stage("y_ps", E), stage("acc_out", E)
        bn3_out, mv3_out, var3_out = stage("bn3_out"), stage("mv3_out"), stage("var3_out")
        rstd3_out, y_ready = stage("rstd3_out"), stage("y_ready")
        stored = stage("stored", 16)

        UP_BANKS = B_BANKS = E * FB // 4
        GW_BANKS = E // 2
        NAMES = ["small"] + [("wbT", i) for i in range(B_BANKS)] + [("gw", i) for i in range(GW_BANKS)]
        NAMES += [("up", i) for i in range(UP_BANKS)] + ["wa"] + [("down", i) for i in range(UP_BANKS)]
        PREP = list(enumerate(NAMES))
        SPLITS = [i for i in NAMES if i == "wa" or i[0] in ("gw", "up")]
        prep_banks = [psG[0], psG[1], psU[0], psU[1]]

        def prep_bank(n):
            return prep_banks[n % 4]

        def expert_steps():
            for e in range(E):
                for f in range(FB):
                    yield "gu", e, f
                if e:
                    yield "down", e - 1
                else:
                    yield "weights",
            yield "down", E - 1
            yield "stats",

        AB = [("xT", 1), ("zv", 1), ("logits", 2), ("pT", 2), ("att", 1), ("x1", 2), ("x1T", 1),
              ("gates", 1), ("scan", 2), ("am", 1)]
        for k in range(HALVES + 1):
            AB += [(("half", k), 0)]
            if k and k % 2 == 0:
                AB += [(("norm", k // 2 - 1), 0 if k < HALVES else 2)]
            if k >= 3 and k % 2 == 1:
                AB += [(("head", k // 2 - 1), 0)]
        AB += [(("head", G - 1), 1), ("x2", 2), ("x2T", 1)]
        AB += [(("hidden", b), b % 2) for b in range(G)]
        AB += [("scores", 0), ("choose", 2)]

        def both_stages():
            experts = list(expert_steps())

            def take(n):
                while experts and (n > 0 or experts[0][0] == "weights"):
                    n -= experts[0][0] in ("gu", "down")
                    yield "C", experts.pop(0)
            yield "C", ("finish",)
            for step, n in AB:
                yield "AB", step
                yield from take(n)
            while experts:
                yield "C", experts.pop(0)

        def whole_program(eng, prep, ab, c):
            def both(g):
                for part, step in both_stages():
                    if part == "AB":
                        ab(Group(g.j, g.off + 1), step)
                    elif step[0] != "finish":
                        c(g, step)
                    elif not g.first(1):
                        c(g.back(1), step)
            todo = list(PREP)
            for n, (step, _) in enumerate(AB):
                for item in todo[:2]:
                    prep(item)
                del todo[:2]
                ab(Group(0, 0), step)
            for item in todo:
                prep(item)
            both(Group(0, 0))
            with eng.Fori(0, (GROUPS - 2) // 2) as j:
                both(Group(j, 1))
                both(Group(j, 2))
            c(Group(0, GROUPS - 2), ("finish",))
            for step in expert_steps():
                c(Group(0, GROUPS - 1), step)
            c(Group(0, GROUPS - 1), ("finish",))

        def plain_wait(eng):
            eng.wait_ge(const_ready, 1)

        def spread_heads(eng, half):
            heads = slice(half * HG, (half + 1) * HG)
            return eng.tensor_tensor(amaxd[:, heads, :],
                                     amax2[:].bitcast(F32).unsqueeze(1).to_broadcast([2 * GH, HG, S]),
                                     head_rows[:, heads].unsqueeze(2).to_broadcast([2 * GH, HG, S]), ALU.mult)

        block = ctx.enter_context(nc.Block())

        @block.sync
        def _(sp):
            def load(g):
                p = g.off % 2
                if not g.first(2):
                    sp.wait_ge(res1_out.sem, res1_out.at(g.back(2)))
                    sp.wait_ge(cT_ps.sem, cT_ps.at(g.back(2)))
                    sp.wait_ge(vc_out.sem, vc_out.at(g.back(2)))
                i = g.number()
                src_x = x_g[i] if isinstance(i, int) else x_g[bass.ds(i, 1)].rearrange("g n b e -> (g n) b e")
                src_c = c_g[i] if isinstance(i, int) else c_g[bass.ds(i, 1)].rearrange("g n b e -> (g n) b e")
                sp.dma_start(xin[p][:], src_x).then_inc(x_loaded[p].sem, 16)
                sp.dma_start(cin[p][:], src_c).then_inc(c_loaded[p].sem, 16)

            def store(g):
                p = g.off % 2
                i = g.number()
                dst = o_g[i] if isinstance(i, int) else o_g[bass.ds(i, 1)].rearrange("g n b e -> (g n) b e")
                sp.wait_ge(y_ready.sem, y_ready.at(g))
                sp.dma_start(dst, y_out[:]).then_inc(stored.sem, 16)

            load(Group(0, 0))
            for t, src in ((wq_n, wq), (wk_n, wk), (wv_n, wv)):
                sp.dma_start(t, src).then_inc(w_loaded, 16)
            sp.dma_start(gate_n[0:H, :], igate_w).then_inc(w_loaded, 16)
            sp.dma_start(gate_n[H:2 * H, :], fgate_w).then_inc(w_loaded, 16)
            for b in range(G):
                sp.dma_start(gbias[b * H:(b + 1) * H, :], igate_b.rearrange("(h a) -> h a", a=1)).then_inc(w_loaded, 16)
                sp.dma_start(gbias[GH + b * H:GH + (b + 1) * H, :],
                             fgate_b.rearrange("(h a) -> h a", a=1)).then_inc(w_loaded, 16)
            sp.dma_start(outw[:], out_w.rearrange("(a d) -> a d", a=1).to_broadcast([128, D])).then_inc(w_loaded, 16)
            sp.dma_start(wb_n[:], w_b.rearrange("e (k f) r -> f e k r", f=128)).then_inc(e_loaded, 16)
            sp.dma_start(wup_n[:], w_up.rearrange("e (k f) h -> f e k h", f=128)).then_inc(e_loaded, 16)
            sp.dma_start(wa_r[:], w_a.rearrange("e r h -> r e h")).then_inc(e_loaded, 16)
            sp.dma_start(wa_n[:], w_a.rearrange("(c a) r h -> (a r) c h", a=2)).then_inc(e_loaded, 16)
            sp.dma_start(wdn_n[:], w_down.rearrange("e h (k f) -> h e k f", f=128)).then_inc(e_loaded, 16)
            load(Group(0, 1))
            load(Group(0, 2))
            store(Group(0, 0))
            with sp.Fori(0, (GROUPS - 4) // 2) as j:
                load(Group(j, 3))
                store(Group(j, 1))
                load(Group(j, 4))
                store(Group(j, 2))
            load(Group(0, GROUPS - 1))
            for i in range(GROUPS - 3, GROUPS):
                store(Group(0, i))
            sp.wait_ge(stored.sem, stored.at(Group(0, GROUPS - 1)))

        W_DMAS = 3 + 2 + 2 * G + 1
        E_DMAS = 5

        @block.gpsimd
        def _(pool):
            steps = [0]

            def done(ins):
                steps[0] += 1
                ins.then_inc(const_step, 1)
                pool.wait_ge(const_step, steps[0])

            done(pool.memset(ident[:], 0.0))
            done(pool.affine_select(out=ident[:], in_=ident[:], pattern=[[-1, 128]], base=0,
                                    channel_multiplier=1, compare_op=ALU.not_equal, fill=1.0))
            done(pool.tensor_copy(identb[:], ident[:]))
            done(pool.memset(ones[:], 1.0))
            done(pool.memset(minusone[:], -1.0))
            done(pool.memset(epsilon[:], NORM_EPS))
            done(pool.memset(minushalf[:], -0.5))
            done(pool.memset(plushalf[:], 0.5))
            done(pool.memset(future[:], 0.0))
            done(pool.affine_select(out=future[:], in_=future[:], pattern=[[0, HG], [1, 128]], base=0,
                                    channel_multiplier=-1, compare_op=ALU.is_ge, fill=MASKED))
            done(pool.memset(headmask[:], 1.0))
            done(pool.affine_select(out=headmask[:], in_=headmask[:], pattern=[[-DH, H]], base=0,
                                    channel_multiplier=1, compare_op=ALU.is_ge, fill=0.0))
            done(pool.affine_select(out=headmask[:], in_=headmask[:], pattern=[[DH, H]], base=DH - 1,
                                    channel_multiplier=-1, compare_op=ALU.is_ge, fill=0.0))
            done(pool.memset(batch_2[:], 1.0))
            done(pool.affine_select(out=batch_2[:], in_=batch_2[:], pattern=[[-GH, 2], [-H, G]], base=0,
                                    channel_multiplier=1, compare_op=ALU.is_ge, fill=0.0))
            done(pool.affine_select(out=batch_2[:], in_=batch_2[:], pattern=[[GH, 2], [H, G]], base=H - 1,
                                    channel_multiplier=-1, compare_op=ALU.is_ge, fill=0.0))
            done(pool.memset(head_8[:], 0.0))
            done(pool.affine_select(out=head_8[:], in_=head_8[:], pattern=[[-H, 2 * G], [-1, H]], base=0,
                                    channel_multiplier=1, compare_op=ALU.not_equal, fill=1.0))
            done(pool.memset(restart[:], 1.0))
            done(pool.affine_select(out=restart[:], in_=restart[:], pattern=[[0, G], [1, E]], base=0,
                                    channel_multiplier=0, compare_op=ALU.not_equal, fill=0.0))
            done(pool.memset(gate_p[:], 0.0))
            pool.memset(vaug[:], 1.0).then_inc(const_ready, 1)
            pool.wait_ge(const_ready, 1)
            pool.wait_ge(w_loaded, 16 * W_DMAS)

            def rstd(g, mv, var, out_, mv_stage, var_stage, out_stage, readers):
                pool.wait_ge(mv_stage.sem, mv_stage.at(g))
                if not g.first(1):
                    pool.wait_ge(readers.sem, readers.at(g.back(1)))
                pool.tensor_tensor(var[:], mv[:, :, 1], epsilon[:, 0:G], ALU.add).then_inc(var_stage.sem, 1)
                pool.wait_ge(var_stage.sem, var_stage.at(g))
                pool.tensor_tensor(out_[:], var[:], minushalf[:, 0:G], ALU.pow).then_inc(out_stage.sem, 1)

            def mask_heads(b):
                pool.tensor_tensor(kmask[:, b % 2, :, :], cT[:, b, :].unsqueeze(1).to_broadcast([D, H, S]),
                                   headmask[:].unsqueeze(2).to_broadcast([D, H, S]),
                                   ALU.mult).then_inc(kmask_out.sem, 1)

            def ab(g, step):
                p = g.off % 2
                if step == "pT":
                    pool.wait_ge(vmean_out.sem, vmean_out.at(g))
                    if not g.first(1):
                        pool.wait_ge(u_ps.sem, u_ps.at(g.back(1)))
                    pool.tensor_tensor(vaug[:, :, 0:DH], cin[p][:].rearrange("t b (h d) -> t (b h) d", d=DH),
                                       vmean[:].unsqueeze(2).to_broadcast([S, GH, DH]),
                                       ALU.subtract).then_inc(vc_out.sem, 1)
                    pool.wait_ge(vc_out.sem, vc_out.at(g))
                    for b in range(G):
                        ins = pool.tensor_tensor(vaug[:, b * H:(b + 1) * H, DH:2 * DH], vaug[:, b * H:(b + 1) * H, 0:DH],
                                                 outw[:].rearrange("p (h d) -> p h d", d=DH), ALU.mult)
                    ins.then_inc(vaug_out.sem, 1)
                elif step == "x1T":
                    pool.wait_ge(cT_sb.sem, cT_sb.at(g))
                    if not g.first(1):
                        pool.wait_ge(qk_ps.sem, qk_ps.at(g.back(1)))
                    mask_heads(0)
                    mask_heads(1)
                elif step[0] == "half" and step[1] in (2, 4):
                    pool.wait_ge(qk_ps.sem, qk_ps.at(g, step[1]))
                    mask_heads(step[1] // 2 + 1)
                elif step == "scan":
                    pool.wait_ge(amax2_out.sem, amax2_out.at(g))
                    if g.first(1):
                        pool.wait_ge(rows_ready, 1)
                    spread_heads(pool, 1).then_inc(amaxd1_out.sem, 1)
                elif step == "att":
                    rstd(g, mv1, var1, rstd1, mv1_out, var1_out, rstd1_out, x1_out)
                elif step[0] == "norm":
                    b = step[1]
                    heads = slice(b * H, (b + 1) * H)
                    pool.wait_ge(hvar_out.sem, hvar_out.at(g, b + 1))
                    if b == 0 and not g.first(1):
                        pool.wait_ge(hn_out.sem, hn_out.at(g.back(1)))
                    pool.tensor_tensor(hrstd[:, heads], hvar[:, heads], minushalf[:, 0:H], ALU.pow)\
                        .then_inc(hrstd_out.sem, 1)
                elif step == ("head", G - 1):
                    rstd(g, mv2, var2, rstd2, mv2_out, var2_out, rstd2_out, x2_out)
                elif step == "scores":
                    pool.wait_ge(sc2_out.sem, sc2_out.at(g))
                    if not g.first(1):
                        pool.wait_ge(sdiff_out.sem, sdiff_out.at(g.back(1)))
                    pool.tensor_tensor(score[:].rearrange("p g e -> p (g e)"), sc2[:].rearrange("p g e -> p (g e)"),
                                       plushalf[:], ALU.pow).then_inc(score_out.sem, 1)

            def c(g, step):
                if step[0] == "stats":
                    pool.wait_ge(mv3_out.sem, mv3_out.at(g))
                    pool.tensor_tensor(negmean3[:], mv3[:, :, 0], minusone[:, 0:G], ALU.mult).then_inc(negmean3_out.sem, 1)
                    rstd(g, mv3, var3, rstd3, mv3_out, var3_out, rstd3_out, y_ready)
                    pool.wait_ge(rstd3_out.sem, rstd3_out.at(g))
                    pool.wait_ge(negmean3_out.sem, negmean3_out.at(g))
                    pool.tensor_tensor(nmr3[:], negmean3[:], rstd3[:], ALU.mult).then_inc(nmr3_out.sem, 1)
                elif step[0] == "gu" and step[2] in POOL_BLOCKS:
                    e, f = step[1], step[2]
                    n = e * FB + f
                    pool.wait_ge(silu_out.sem, silu_out.at(g, n + 1))
                    pool.wait_ge(up_out.sem, up_out.at(g, e + 1))
                    if e >= 2:
                        pool.wait_ge(y_ps.sem, y_ps.at(g, e - 1))
                    elif not g.first(1):
                        pool.wait_ge(y_ps.sem, y_ps.at(g.back(1)))
                    pool.tensor_tensor(hid[e % 2][f][:], silu2[f][:], up[:], ALU.mult).then_inc(hid_pool_out.sem, 1)

            whole_program(pool, lambda item: None, ab, c)

        @block.tensor
        def _(pe):
            pe.wait_ge(const_ready, 1)
            pe.wait_ge(w_loaded, 16 * W_DMAS)
            def prep(numbered):
                n, item = numbered
                ps = prep_bank(n)
                if n == 1:
                    pe.wait_ge(e_loaded, 16 * E_DMAS)
                if n >= 4:
                    pe.wait_ge(prep_out, n - 3)
                if item == "small":
                    pe.matmul(ps[:, 0:128], wq_n, wk_n, start=True, stop=True)
                    pe.transpose(ps[:, 128:256], wv_n, ident[:])
                    for k in range(3):
                        ins = pe.transpose(ps[:, 256 + 2 * H * k:256 + 2 * H * (k + 1)],
                                           gate_n[:, k * D:(k + 1) * D], ident[0:2 * H, 0:2 * H])
                elif item == "wa":
                    for k in range(AC):
                        ins = pe.transpose(ps[:, k * 128:(k + 1) * 128], wa_n[:, k, :], ident[:])
                elif item[0] == "wbT":
                    for k in range(4):
                        q = item[1] * 4 + k
                        ins = pe.transpose(ps[0:R, k * 128:(k + 1) * 128], wb_n[:, q // FB, q % FB, :], ident[:])
                elif item[0] == "gw":
                    if item[1] == 0:
                        pe.wait_ge(prep_out, 1 + B_BANKS)
                    for k in range(2):
                        e = item[1] * 2 + k
                        ins = pe.matmul(ps[:, k * F:(k + 1) * F], wa_r[:, e, :], wbT[:, e, :], start=True, stop=True)
                else:
                    src = wup_n if item[0] == "up" else wdn_n
                    for k in range(4):
                        q = item[1] * 4 + k
                        ins = pe.transpose(ps[:, k * 128:(k + 1) * 128], src[:, q // FB, q % FB, :], ident[:])
                ins.then_inc(prep_ps, 1)

            def split_product(out_, w_hi, w_lo, x_hi, x_lo):
                pe.matmul(out_, w_lo, x_hi, start=True, stop=False)
                pe.matmul(out_, w_hi, x_lo, start=False, stop=False)
                return pe.matmul(out_, w_hi, x_hi, start=False, stop=True)

            def ab(g, step):
                p = g.off % 2
                if step == "xT":
                    if g.first(1):
                        pe.wait_ge(prep_out, 1)
                    pe.wait_ge(x_loaded[p].sem, x_loaded[p].at_parity(g))
                    if not g.first(1):
                        pe.wait_ge(x2lo_out.sem, x2lo_out.at(g.back(1)))
                    for b in range(G):
                        ins = pe.transpose(psA[:, b * S:(b + 1) * S], xin[p][:, b, :], ident[:])
                    ins.then_inc(xT_ps.sem, 1)
                elif step == "zv":
                    pe.wait_ge(xT_sb.sem, xT_sb.at(g))
                    if not g.first(1):
                        pe.wait_ge(hidsq_out.sem, hidsq_out.at(g.back(1)))
                    pe.matmul(psB[:], qk_w[:], xT[:].rearrange("e b s -> e (b s)"), start=True, stop=True)\
                        .then_inc(z_ps.sem, 1)
                    for b in range(G):
                        ins = pe.matmul(psC[:, b * D:(b + 1) * D], xT[:, b, :], wvT[:], start=True, stop=True)
                    ins.then_inc(v_ps.sem, 1)
                elif step == "logits":
                    pe.wait_ge(zT_sb.sem, zT_sb.at(g))
                    for b in range(G):
                        ins = pe.matmul(psA[:, b * S:(b + 1) * S], zT[:, b, :], xT[:, b, :], start=True, stop=True)
                    ins.then_inc(logits_ps.sem, 1)
                elif step == "pT":
                    pe.wait_ge(c_loaded[p].sem, c_loaded[p].at_parity(g))
                    pe.wait_ge(v_out.sem, v_out.at(g))
                    for b in range(G):
                        ins = pe.transpose(psC[:, b * S:(b + 1) * S], cin[p][:, b, :], ident[:])
                    ins.then_inc(cT_ps.sem, 1)
                    pe.wait_ge(probs_out.sem, probs_out.at(g))
                    for b in range(G):
                        ins = pe.transpose(psB[:, b * S:(b + 1) * S], probs[:, b, :], ident[:])
                    ins.then_inc(pT_ps.sem, 1)
                elif step == "att":
                    pe.wait_ge(pT_sb.sem, pT_sb.at(g))
                    for b in range(G):
                        ins = pe.matmul(psA[:, b * D:(b + 1) * D], probsT[:, b, :], v_sb[:, b, :], start=True, stop=True)
                    ins.then_inc(att_ps.sem, 1)
                elif step == "x1T":
                    pe.wait_ge(x1_out.sem, x1_out.at(g))
                    for b in range(G):
                        ins = pe.transpose(psB[:, b * S:(b + 1) * S], x1[:, b, :], ident[:])
                    ins.then_inc(x1T_ps.sem, 1)
                elif step == "gates":
                    pe.wait_ge(x1T_sb.sem, x1T_sb.at(g))
                    pe.wait_ge(cT_sb.sem, cT_sb.at(g))
                    for b in range(G):
                        pe.matmul(psC[0:2 * GH, 0:S], gate_p[:, 0, b, :], x1T[:, b, :], start=(b == 0), stop=False)
                        ins = pe.matmul(psC[0:2 * GH, 0:S], gate_p[:, 1, b, :], cT[:, b, :], start=False,
                                        stop=(b == G - 1))
                    ins.then_inc(gates_ps.sem, 1)
                elif step == "am":
                    pe.wait_ge(arow_out.sem, arow_out.at(g))
                    pe.wait_ge(mrow_out.sem, mrow_out.at(g))
                    pe.wait_ge(res1_out.sem, res1_out.at(g))
                    pe.matmul(psA[:, 0:GH], arow[:], ident[0:GH, 0:GH], start=True, stop=True)
                    pe.matmul(psA[:, GH:2 * GH], mrow[:], ident[0:GH, 0:GH], start=True, stop=True)\
                        .then_inc(am_ps.sem, 1)
                elif step[0] == "half":
                    k = step[1]
                    if k < HALVES:
                        b, h0 = k // 2, HG * (k % 2)
                        if k == 0:
                            if g.first(1):
                                pe.wait_ge(rows_ready, 1)
                            pe.wait_ge(amaxd0_out.sem, amaxd0_out.at(g))
                            pe.wait_ge(x1T_sb.sem, x1T_sb.at(g))
                            pe.wait_ge(arow_out.sem, arow_out.at(g))
                        else:
                            pe.wait_ge(decay_out.sem, decay_out.at(g, k))
                        if k == 1:
                            pe.wait_ge(amaxd1_out.sem, amaxd1_out.at(g))
                        pe.matmul(psB[:], identb[:], future[:].rearrange("t h s -> t (h s)"), start=True, stop=False)
                        pe.matmul(psB[:], batch_rows[:, b:b + 1].to_broadcast([2 * GH, 128]),
                                  amaxd[:, h0:h0 + HG, :].rearrange("r h s -> r (h s)"), start=False, stop=True)\
                            .then_inc(mb_ps.sem, 1)
                        if k % 2 == 0:
                            pe.wait_ge(kmask_out.sem, kmask_out.at(g, b + 1))
                        if k:
                            pe.wait_ge(cmat_out.sem, cmat_out.at(g, k))
                        for i in range(HG):
                            ins = pe.matmul(psC[:, i * S:(i + 1) * S], kmask[:, b % 2, h0 + i, :], x1T[:, b, :],
                                            start=True, stop=True)
                        ins.then_inc(qk_ps.sem, 1)
                    if k:
                        q = k - 1
                        b, h0 = q // 2, HG * (q % 2)
                        pe.wait_ge(cmat_out.sem, cmat_out.at(g, q + 1))
                        if q == 0:
                            pe.wait_ge(acol_out.sem, acol_out.at(g))
                            pe.wait_ge(expm_out.sem, expm_out.at(g))
                            pe.wait_ge(vaug_out.sem, vaug_out.at(g))
                        else:
                            pe.wait_ge(u_out.sem, u_out.at(g, q))
                        for i in range(HG):
                            ins = pe.matmul(psA[:, i * VW:(i + 1) * VW], cmat[q % 2][:, i, :], vaug[:, b * H + h0 + i, :],
                                            start=True, stop=True)
                        ins.then_inc(u_ps.sem, 1)
                elif step == "x2T":
                    pe.wait_ge(x2_out.sem, x2_out.at(g))
                    pe.wait_ge(u_out.sem, u_out.at(g))
                    for b in range(G):
                        ins = pe.transpose(psA[:, b * S:(b + 1) * S], acc[p][:, b, :], ident[:])
                    ins.then_inc(x2T_ps.sem, 1)
                elif step[0] == "hidden":
                    b = step[1]
                    if b == 0:
                        if g.first(1):
                            pe.wait_ge(prep_out, len(PREP))
                        pe.wait_ge(x2lo_out.sem, x2lo_out.at(g))
                        pe.wait_ge(decay_out.sem, decay_out.at(g))
                        pe.wait_ge(cmat_out.sem, cmat_out.at(g))
                    if b >= 2:
                        pe.wait_ge(hidsq_out.sem, hidsq_out.at(g, b - 1))
                    split_product([psB, psC][b % 2][:], x2hi[p][:, b, :], x2lo[p][:, b, :], aw_hi[:], aw_lo[:])\
                        .then_inc(hid_ps.sem, 1)

            def c(g, step):
                p = g.off % 2
                xh, xl = (t[p][:].rearrange("e b s -> e (b s)") for t in (x2hi, x2lo))
                if step[0] == "gu":
                    e, f = step[1], step[2]
                    n = e * FB + f
                    if n == 0:
                        pe.wait_ge(x2lo_out.sem, x2lo_out.at(g))
                        pe.wait_ge(x2hi_out.sem, x2hi_out.at(g))
                    cols = slice(f * 128, (f + 1) * 128)
                    if e:
                        pe.wait_ge(silu_out.sem, silu_out.at(g, n - 1))
                    elif not g.first(1):
                        pe.wait_ge(silu_out.sem, silu_out.at(g.back(1)))
                    split_product(psG[f][:], gw_hi[:, e, cols], gw_lo[:, e, cols], xh, xl).then_inc(g_ps.sem, 1)
                    psU_out = up_out if f in POOL_BLOCKS else hid_out
                    if e:
                        pe.wait_ge(psU_out.sem, psU_out.at(g, e))
                    elif not g.first(1):
                        pe.wait_ge(psU_out.sem, psU_out.at(g.back(1)))
                    split_product(psU[f][:], uw_hi[:, e, cols], uw_lo[:, e, cols], xh, xl).then_inc(u2_ps.sem, 1)
                elif step[0] == "down":
                    e = step[1]
                    pe.wait_ge(hid_out.sem, hid_out.at(g, e + 1))
                    pe.wait_ge(hid_pool_out.sem, hid_pool_out.at(g, e + 1))
                    if e:
                        pe.wait_ge(acc_out.sem, acc_out.at(g, e))
                    elif not g.first(1):
                        pe.wait_ge(acc_out.sem, acc_out.at(g.back(1)))
                    for b in range(G):
                        for f in range(FB):
                            ins = pe.matmul(psY[:, b, :], hid[e % 2][f][:, b * S:(b + 1) * S], dwT[:, e, f, :],
                                            start=(f == 0), stop=(f == FB - 1))
                    ins.then_inc(y_ps.sem, 1)

            whole_program(pe, prep, ab, c)

        @block.scalar
        def _(act):
            def decays(g, k):
                b, h0 = k // 2, HG * (k % 2)
                act.wait_ge(mb_ps.sem, mb_ps.at(g, k + 1))
                if k == 0:
                    act.wait_ge(acol_out.sem, acol_out.at(g))
                if k >= 2:
                    act.wait_ge(cmat_out.sem, cmat_out.at(g, k - 1))
                elif not g.first(1):
                    act.wait_ge(cmat_out.sem, cmat_out.at(g.back(1)))
                for i in range(HG):
                    r = b * H + h0 + i
                    ins = act.activation(decay[k % 2][:, i, :], psB[:, i * S:(i + 1) * S], ACT.Exp,
                                         bias=acol[:, r:r + 1], scale=-1.0)
                ins.then_inc(decay_out.sem, 1)

            def ab(g, step):
                p = g.off % 2
                if step == "xT":
                    act.wait_ge(xT_ps.sem, xT_ps.at(g))
                    if not g.first(1):
                        act.wait_ge(logits_ps.sem, logits_ps.at(g.back(1)))
                    act.copy(xT[:].rearrange("e b s -> e (b s)"), psA[:]).then_inc(xT_sb.sem, 1)
                elif step == "zv":
                    act.wait_ge(z_ps.sem, z_ps.at(g))
                    act.copy(zT[:].rearrange("e b s -> e (b s)"), psB[:]).then_inc(zT_sb.sem, 1)
                elif step == "logits":
                    act.wait_ge(negmax_out.sem, negmax_out.at(g))
                    if not g.first(1):
                        act.wait_ge(pT_ps.sem, pT_ps.at(g.back(1)))
                        act.wait_ge(rown_out.sem, rown_out.at(g.back(1)))
                    for b in range(G):
                        ins = act.activation(probs[:, b, :], psA[:, b * S:(b + 1) * S], ACT.Exp,
                                             bias=negmax[:, b:b + 1], scale=1.0, accum_out=rowsum[:, b:b + 1])
                    ins.then_inc(probs_out.sem, 1)
                elif step == "pT":
                    act.wait_ge(cT_ps.sem, cT_ps.at(g))
                    if not g.first(1):
                        act.wait_ge(gates_ps.sem, gates_ps.at(g.back(1)))
                        act.wait_ge(kmask_out.sem, kmask_out.at(g.back(1)))
                    act.copy(cT[:].rearrange("e b s -> e (b s)"), psC[:]).then_inc(cT_sb.sem, 1)
                    act.wait_ge(pT_ps.sem, pT_ps.at(g))
                    if not g.first(1):
                        act.wait_ge(att_ps.sem, att_ps.at(g.back(1)))
                    act.copy(probsT[:].rearrange("e b s -> e (b s)"), psB[:]).then_inc(pT_sb.sem, 1)
                elif step == "x1T":
                    act.wait_ge(x1T_ps.sem, x1T_ps.at(g))
                    if not g.first(1):
                        act.wait_ge(qk_ps.sem, qk_ps.at(g.back(1)))
                    act.copy(x1T[:].rearrange("e b s -> e (b s)"), psB[:]).then_inc(x1T_sb.sem, 1)
                elif step == "gates":
                    act.wait_ge(fneg_out.sem, fneg_out.at(g))
                    act.activation(f_exp[:], f_neg[:], ACT.Exp).then_inc(fexp_out.sem, 1)
                    act.wait_ge(fexp_out.sem, fexp_out.at(g))
                    if not g.first(1):
                        act.wait_ge(logf_out.sem, logf_out.at(g.back(1)))
                    act.activation(f_ln[:], f_exp[:], ACT.Ln, bias=1.0).then_inc(fln_out.sem, 1)
                elif step == "am":
                    act.wait_ge(am_ps.sem, am_ps.at(g))
                    if not g.first(1):
                        act.wait_ge(nrm_out.sem, nrm_out.at(g.back(1)))
                    act.activation(expm[:], psA[:, GH:2 * GH], ACT.Exp, scale=-1.0).then_inc(expm_out.sem, 1)
                elif step[0] == "half":
                    k = step[1]
                    if k < HALVES:
                        decays(g, k)
                    if k:
                        q = k - 1
                        act.wait_ge(u_ps.sem, u_ps.at(g, q + 1))
                        if q == 0 and not g.first(1):
                            act.wait_ge(hn_out.sem, hn_out.at(g.back(1)))
                        act.copy(u_sb[:, q * HG:(q + 1) * HG, :].rearrange("s h d -> s (h d)"),
                                 psA[:, 0:HG * VW]).then_inc(u_out.sem, 1)
                elif step == "x2T":
                    act.wait_ge(x2T_ps.sem, x2T_ps.at(g))
                    if not g.first(2):
                        act.wait_ge(u2_ps.sem, u2_ps.at(g.back(2)))
                    act.copy(x2hi[p][:].rearrange("e b s -> e (b s)"), psA[:]).then_inc(x2hi_out.sem, 1)
                elif step[0] == "hidden":
                    b = step[1]
                    act.wait_ge(hid_ps.sem, hid_ps.at(g, b + 1))
                    if b >= 2:
                        act.wait_ge(sc2_out.sem, sc2_out.at(g, b - 1))
                    elif not g.first(1):
                        act.wait_ge(sc2_out.sem, sc2_out.at(g.back(1)))
                    act.activation(hidsq[b % 2][:], [psB, psC][b % 2][:], ACT.Square).then_inc(hidsq_out.sem, 1)

            def c(g, step):
                p = g.off % 2
                if step[0] == "gu":
                    e, f = step[1], step[2]
                    n = e * FB + f
                    act.wait_ge(g_ps.sem, g_ps.at(g, n + 1))
                    if e:
                        act.wait_ge(silu_out.sem, silu_out.at(g, n - 1))
                    elif not g.first(1):
                        act.wait_ge(silu_out.sem, silu_out.at(g.back(1)))
                    act.activation(tanh[f][:], psG[f][:], ACT.Tanh, scale=0.5).then_inc(tanh_out.sem, 1)
                    if f in POOL_BLOCKS:
                        act.wait_ge(u2_ps.sem, u2_ps.at(g, n + 1))
                        if e:
                            act.wait_ge(hid_pool_out.sem, hid_pool_out.at(g, e))
                        elif not g.first(1):
                            act.wait_ge(hid_pool_out.sem, hid_pool_out.at(g.back(1)))
                        act.activation(up[:], psU[f][:], ACT.Copy, scale=0.5).then_inc(up_out.sem, 1)
                elif step[0] == "weights":
                    act.wait_ge(sdiff_out.sem, sdiff_out.at(g))
                    if not g.first(1):
                        act.wait_ge(wexp_out.sem, wexp_out.at(g.back(1)))
                    act.activation(sexp[:], sdiff[:], ACT.Exp).then_inc(sexp_out.sem, 1)
                elif step[0] == "finish":
                    act.wait_ge(nmr3_out.sem, nmr3_out.at(g))
                    if not g.first(1):
                        act.wait_ge(stored.sem, stored.at(g.back(1)))
                    for b in range(G):
                        ins = act.activation(y_out[:, b, :], acc[p][:, b, :], ACT.Identity,
                                             bias=nmr3[:, b:b + 1], scale=rstd3[:, b:b + 1])
                    ins.then_inc(y_ready.sem, 1)

            whole_program(act, lambda item: None, ab, c)

        @block.vector
        def _(dve):
            def prep(numbered):
                n, item = numbered
                ps = prep_bank(n)
                dve.wait_ge(prep_ps, n + 1)
                if item == "small":
                    dve.tensor_copy(qk_w[:], ps[:, 0:128])
                    dve.tensor_copy(wvT[:], ps[:, 128:256])
                    dve.tensor_copy(gate_xT[:], ps[:, 256:256 + 2 * H])
                    dve.tensor_copy(gate_t[:], ps[:, 256 + 2 * H:256 + 4 * H]).then_inc(gate_step, 1)
                    dve.wait_ge(gate_step, 1)
                    dve.tensor_tensor(gate_cT[:], ps[:, 256 + 4 * H:256 + 6 * H], gate_t[:], ALU.add)\
                        .then_inc(gate_step, 1)
                    dve.wait_ge(gate_step, 2)
                    dve.wait_ge(const_ready, 1)
                    for s, src in enumerate((gate_xT, gate_cT)):
                        for b in range(G):
                            for k in range(2):
                                ins = dve.tensor_copy(gate_p[:, s, b, k * GH + b * H:k * GH + (b + 1) * H],
                                                      src[:, k * H:(k + 1) * H])
                    ins.then_inc(prep_out, 1)
                    dve.tensor_tensor(batch_rows[:], batch_2[:, 0, :], batch_2[:, 1, :], ALU.add)
                    dve.tensor_reduce(head_rows[:], head_8[:].rearrange("r m h -> r h m"), AX_X, ALU.add)\
                        .then_inc(rows_ready, 1)
                    return
                if item[0] == "wbT":
                    dve.tensor_copy(wbT[:, 2 * item[1]:2 * item[1] + 2, :].rearrange("r e f -> r (e f)"),
                                    ps[0:R, :]).then_inc(prep_out, 1)
                    return
                if item[0] == "down":
                    dve.tensor_copy(dwT[:, 2 * item[1]:2 * item[1] + 2, :, :].rearrange("f e k h -> f (e k h)"),
                                    ps[:]).then_inc(prep_out, 1)
                    return
                if item == "wa":
                    hi, lo = (aw_hi[:], aw_lo[:])
                else:
                    pair = (gw_hi, gw_lo) if item[0] == "gw" else (uw_hi, uw_lo)
                    hi, lo = (t[:, 2 * item[1]:2 * item[1] + 2, :].rearrange("h e f -> h (e f)") for t in pair)
                dve.tensor_copy(hi, ps[:]).then_inc(prep_hi, 1)
                dve.wait_ge(prep_hi, SPLITS.index(item) + 1)
                dve.tensor_tensor(lo, ps[:], hi.bitcast(F32), ALU.subtract).then_inc(prep_out, 1)

            def layer_stats(g, src, bn, mv, bn_stage, mv_stage):
                for b in range(G):
                    ins = dve.bn_stats(bn[:, b, :], src[:, b, :])
                ins.then_inc(bn_stage.sem, 1)
                plain_wait(dve)
                dve.wait_ge(bn_stage.sem, bn_stage.at(g))
                for b in range(G):
                    ins = dve.bn_aggr(mv[:, b, :], bn[:, b, :])
                ins.then_inc(mv_stage.sem, 1)

            def token(t):
                return t.unsqueeze(2).to_broadcast([S, G, E])

            def normalize(g, dst, src, mv, rstd, rstd_stage, out_stage):
                dve.wait_ge(rstd_stage.sem, rstd_stage.at(g))
                for b in range(G):
                    ins = dve.tensor_scalar(dst[:, b, :], src[:, b, :], mv[:, b, 0:1], rstd[:, b:b + 1],
                                            ALU.subtract, ALU.mult)
                ins.then_inc(out_stage.sem, 1)

            def ab(g, step):
                p = g.off % 2
                if step == "xT":
                    dve.wait_ge(c_loaded[p].sem, c_loaded[p].at_parity(g))
                    if not g.first(1):
                        dve.wait_ge(vmean_out.sem, vmean_out.at(g.back(1)))
                    dve.tensor_reduce(vsum[:], cin[p][:].rearrange("t b (h d) -> t (b h) d", d=DH), AX_X, ALU.add)\
                        .then_inc(vsum_out.sem, 1)
                    dve.wait_ge(vsum_out.sem, vsum_out.at(g))
                    if not g.first(1):
                        dve.wait_ge(vc_out.sem, vc_out.at(g.back(1)))
                    dve.tensor_scalar(vmean[:], vsum[:], 1.0 / DH, None, ALU.mult).then_inc(vmean_out.sem, 1)
                elif step == "zv":
                    dve.wait_ge(v_ps.sem, v_ps.at(g))
                    if not g.first(1):
                        dve.wait_ge(att_ps.sem, att_ps.at(g.back(1)))
                    dve.tensor_copy(v_sb[:].rearrange("e b s -> e (b s)"), psC[:]).then_inc(v_out.sem, 1)
                elif step == "logits":
                    dve.wait_ge(logits_ps.sem, logits_ps.at(g))
                    dve.tensor_reduce(rowmax[:], psA[:].rearrange("n (b m) -> n b m", b=G), AX_X, ALU.max)\
                        .then_inc(max_out.sem, 1)
                    dve.wait_ge(max_out.sem, max_out.at(g))
                    if not g.first(1):
                        dve.wait_ge(probs_out.sem, probs_out.at(g.back(1)))
                    dve.tensor_scalar(negmax[:], rowmax[:], -1.0, None, ALU.mult).then_inc(negmax_out.sem, 1)
                elif step == "pT":
                    dve.wait_ge(probs_out.sem, probs_out.at(g))
                    dve.tensor_scalar(rowsum_n[:], rowsum[:], float(D) ** 0.5, None, ALU.mult).then_inc(rown_out.sem, 1)
                    dve.wait_ge(rown_out.sem, rown_out.at(g))
                    dve.reciprocal(rowinv[:], rowsum_n[:]).then_inc(rowinv_out.sem, 1)
                elif step == "att":
                    dve.wait_ge(rowinv_out.sem, rowinv_out.at(g))
                    dve.wait_ge(att_ps.sem, att_ps.at(g))
                    for b in range(G):
                        ins = dve.scalar_tensor_tensor(out=res1[:, b, :], in0=psA[:, b * D:(b + 1) * D],
                                                       scalar=rowinv[:, b:b + 1], in1=xin[p][:, b, :],
                                                       op0=ALU.mult, op1=ALU.add)
                    ins.then_inc(res1_out.sem, 1)
                    dve.wait_ge(res1_out.sem, res1_out.at(g))
                    if not g.first(1):
                        dve.wait_ge(var1_out.sem, var1_out.at(g.back(1)))
                    layer_stats(g, res1, bn6, mv1, bn1_out, mv1_out)
                elif step == "x1":
                    if not g.first(1):
                        dve.wait_ge(x1T_ps.sem, x1T_ps.at(g.back(1)))
                        dve.wait_ge(res2_out.sem, res2_out.at(g.back(1)))
                    normalize(g, x1, res1, mv1, rstd1, rstd1_out, x1_out)
                elif step == "gates":
                    dve.wait_ge(gates_ps.sem, gates_ps.at(g))
                    dve.tensor_scalar(f_in[:], psC[GH:2 * GH, 0:S], gbias[GH:2 * GH, 0:1], None, ALU.add)\
                        .then_inc(f_out.sem, 1)
                    dve.wait_ge(f_out.sem, f_out.at(g))
                    if not g.first(1):
                        dve.wait_ge(fexp_out.sem, fexp_out.at(g.back(1)))
                    dve.scalar_tensor_tensor(out=f_neg[:], in0=f_in[:], scalar=-1.0, in1=f_in[:], op0=ALU.mult,
                                             op1=ALU.min).then_inc(fneg_out.sem, 1)
                elif step == "scan":
                    dve.wait_ge(fln_out.sem, fln_out.at(g))
                    dve.scalar_tensor_tensor(out=logf[:], in0=f_in[:], scalar=0.0, in1=f_ln[:], op0=ALU.min,
                                             op1=ALU.subtract).then_inc(logf_out.sem, 1)
                    dve.wait_ge(logf_out.sem, logf_out.at(g))
                    dve.tensor_tensor_scan(cumf[:], ones[:], logf[:], 0.0, ALU.mult, ALU.add)\
                        .then_inc(cumf_out.sem, 1)
                    dve.wait_ge(cumf_out.sem, cumf_out.at(g))
                    if not g.first(1):
                        dve.wait_ge(am_ps.sem, am_ps.at(g.back(1)))
                    dve.scalar_tensor_tensor(out=arow[:], in0=psC[0:GH, 0:S], scalar=gbias[0:GH, 0:1], in1=cumf[:],
                                             op0=ALU.add, op1=ALU.subtract).then_inc(arow_out.sem, 1)
                    dve.wait_ge(arow_out.sem, arow_out.at(g))
                    if not g.first(1):
                        dve.wait_ge(mb_ps.sem, mb_ps.at(g.back(1)))
                    dve.tensor_tensor_scan(amax[:], arow[:], arow[:], -3.0e38, ALU.max, ALU.max)\
                        .then_inc(amax_out.sem, 1)
                    dve.wait_ge(amax_out.sem, amax_out.at(g))
                    if not g.first(1):
                        dve.wait_ge(amaxd1_out.sem, amaxd1_out.at(g.back(1)))
                    dve.tensor_copy(amax2[0:GH, :], amax[:]).then_inc(amaxhi_out.sem, 1)
                    dve.tensor_tensor(mrow[:], cumf[:], amax[:], ALU.add).then_inc(mrow_out.sem, 1)
                    dve.wait_ge(amaxhi_out.sem, amaxhi_out.at(g))
                    dve.tensor_tensor(amax2[GH:2 * GH, :], amax[:], amax2[0:GH, :].bitcast(F32), ALU.subtract)\
                        .then_inc(amax2_out.sem, 1)
                    dve.wait_ge(amax2_out.sem, amax2_out.at(g))
                    if g.first(1):
                        dve.wait_ge(rows_ready, 1)
                    spread_heads(dve, 0).then_inc(amaxd0_out.sem, 1)
                elif step == "am":
                    dve.wait_ge(am_ps.sem, am_ps.at(g))
                    dve.wait_ge(expm_out.sem, expm_out.at(g))
                    if not g.first(1):
                        dve.wait_ge(decay_out.sem, decay_out.at(g.back(1)))
                    dve.tensor_copy(acol[:], psA[:, 0:GH]).then_inc(acol_out.sem, 1)
                elif step[0] == "half":
                    k = step[1]
                    if k < HALVES:
                        dve.wait_ge(qk_ps.sem, qk_ps.at(g, k + 1))
                        dve.wait_ge(decay_out.sem, decay_out.at(g, k + 1))
                        if k >= 2:
                            dve.wait_ge(u_ps.sem, u_ps.at(g, k - 1))
                        elif not g.first(1):
                            dve.wait_ge(u_ps.sem, u_ps.at(g.back(1)))
                        dve.scalar_tensor_tensor(out=cmat[k % 2][:].rearrange("t h s -> t (h s)"), in0=psC[:],
                                                 scalar=float(DH) ** -0.5,
                                                 in1=decay[k % 2][:].rearrange("t h s -> t (h s)"),
                                                 op0=ALU.mult, op1=ALU.mult).then_inc(cmat_out.sem, 1)
                elif step[0] == "norm":
                    b = step[1]
                    heads = slice(b * H, (b + 1) * H)
                    dve.wait_ge(u_out.sem, u_out.at(g, 2 * b + 2))
                    dve.wait_ge(expm_out.sem, expm_out.at(g))
                    dve.scalar_tensor_tensor(out=sum_abs[:, heads], in0=u_sb[:, heads, 2 * DH], scalar=-1.0,
                                             in1=u_sb[:, heads, 2 * DH], op0=ALU.mult, op1=ALU.max)\
                        .then_inc(sumabs_out.sem, 1)
                    dve.tensor_tensor(usq[:], u_sb[:, heads, 0:DH], u_sb[:, heads, 0:DH], ALU.mult)\
                        .then_inc(usq_out.sem, 1)
                    dve.wait_ge(sumabs_out.sem, sumabs_out.at(g, b + 1))
                    dve.tensor_tensor(nrm[:, heads], sum_abs[:, heads], expm[:, heads], ALU.max)\
                        .then_inc(nrm_out.sem, 1)
                    dve.wait_ge(usq_out.sem, usq_out.at(g, b + 1))
                    dve.tensor_reduce(uss[:, heads], usq[:], AX_X, ALU.add).then_inc(uss_out.sem, 1)
                    dve.wait_ge(nrm_out.sem, nrm_out.at(g, b + 1))
                    dve.tensor_scalar(nrm_e[:, heads], nrm[:, heads], GATE_EPS, NORM_EPS ** 0.5, ALU.add, ALU.mult)\
                        .then_inc(nrme_out.sem, 1)
                    dve.wait_ge(nrme_out.sem, nrme_out.at(g, b + 1))
                    dve.tensor_tensor(nrm_2[:, heads], nrm_e[:, heads], nrm_e[:, heads], ALU.mult)\
                        .then_inc(nrm2_out.sem, 1)
                    dve.wait_ge(uss_out.sem, uss_out.at(g, b + 1))
                    dve.wait_ge(nrm2_out.sem, nrm2_out.at(g, b + 1))
                    if b == 0 and not g.first(1):
                        dve.wait_ge(hrstd_out.sem, hrstd_out.at(g.back(1)))
                    dve.scalar_tensor_tensor(out=hvar[:, heads], in0=uss[:, heads], scalar=1.0 / DH,
                                             in1=nrm_2[:, heads], op0=ALU.mult, op1=ALU.add)\
                        .then_inc(hvar_out.sem, 1)
                elif step[0] == "head":
                    b = step[1]
                    heads = slice(b * H, (b + 1) * H)
                    dve.wait_ge(hrstd_out.sem, hrstd_out.at(g, b + 1))
                    dve.tensor_tensor(hn[:], u_sb[:, heads, DH:2 * DH],
                                      hrstd[:, heads].unsqueeze(2).to_broadcast([S, H, DH]), ALU.mult)\
                        .then_inc(hn_out.sem, 1)
                    dve.wait_ge(hn_out.sem, hn_out.at(g, b + 1))
                    dve.tensor_tensor(res2[:, b, :], hn[:].rearrange("s h d -> s (h d)"), x1[:, b, :], ALU.add)\
                        .then_inc(res2_out.sem, 1)
                    dve.wait_ge(res2_out.sem, res2_out.at(g, b + 1))
                    dve.bn_stats(bn6b[:, b, :], res2[:, b, :]).then_inc(bn2_out.sem, 1)
                    plain_wait(dve)
                    if b == 0 and not g.first(1):
                        dve.wait_ge(var2_out.sem, var2_out.at(g.back(1)))
                    dve.wait_ge(bn2_out.sem, bn2_out.at(g, b + 1))
                    dve.bn_aggr(mv2[:, b, :], bn6b[:, b, :]).then_inc(mv2_out.sem, 1)
                elif step == "x2":
                    if not g.first(2):
                        dve.wait_ge(y_ready.sem, y_ready.at(g.back(2)))
                    normalize(g, acc[p], res2, mv2, rstd2, rstd2_out, x2_out)
                elif step == "x2T":
                    dve.wait_ge(x2hi_out.sem, x2hi_out.at(g))
                    if not g.first(2):
                        dve.wait_ge(u2_ps.sem, u2_ps.at(g.back(2)))
                    dve.tensor_tensor(x2lo[p][:].rearrange("e b s -> e (b s)"), psA[:],
                                      x2hi[p][:].rearrange("e b s -> e (b s)").bitcast(F32),
                                      ALU.subtract).then_inc(x2lo_out.sem, 1)
                elif step[0] == "hidden":
                    b = step[1]
                    dve.wait_ge(hidsq_out.sem, hidsq_out.at(g, b + 1))
                    if b == 0 and not g.first(1):
                        dve.wait_ge(score_out.sem, score_out.at(g.back(1)))
                    dve.tensor_reduce(sc2[:, b, :], hidsq[b % 2][:].rearrange("n (e r) -> n e r", r=R), AX_X, ALU.add)\
                        .then_inc(sc2_out.sem, 1)
                elif step == "choose":
                    plain_wait(dve)
                    dve.wait_ge(sc2_out.sem, sc2_out.at(g))
                    for b in range(G):
                        ins = dve.max(top8[:, b, :], sc2[:, b, :])
                    ins.then_inc(top_out.sem, 1)
                    dve.wait_ge(top_out.sem, top_out.at(g))
                    dve.tensor_tensor(equal[:], sc2[:], token(top8[:, :, 1]), ALU.is_equal).then_inc(eq_out.sem, 1)
                    dve.tensor_tensor(is1[:], top8[:, :, 0], top8[:, :, 1], ALU.is_gt).then_inc(is1_out.sem, 1)
                    dve.tensor_tensor(above[:], sc2[:], token(top8[:, :, 1]), ALU.is_gt).then_inc(above_out.sem, 1)
                    dve.wait_ge(eq_out.sem, eq_out.at(g))
                    dve.tensor_tensor_scan(rank[:].rearrange("p g e -> p (g e)"), restart[:].rearrange("p g e -> p (g e)"),
                                           equal[:].rearrange("p g e -> p (g e)"), 0.0, ALU.mult, ALU.add)\
                        .then_inc(rank_out.sem, 1)
                    dve.wait_ge(is1_out.sem, is1_out.at(g))
                    dve.tensor_scalar(lim[:], is1[:], -1.0, 2.0, ALU.mult, ALU.add).then_inc(lim_out.sem, 1)
                    dve.wait_ge(rank_out.sem, rank_out.at(g))
                    dve.wait_ge(lim_out.sem, lim_out.at(g))
                    dve.tensor_tensor(inlim[:], rank[:], token(lim[:]), ALU.is_le).then_inc(inlim_out.sem, 1)
                    dve.wait_ge(inlim_out.sem, inlim_out.at(g))
                    dve.tensor_tensor(chosen2[:], inlim[:], equal[:], ALU.mult).then_inc(ch2_out.sem, 1)
                    dve.wait_ge(ch2_out.sem, ch2_out.at(g))
                    dve.wait_ge(above_out.sem, above_out.at(g))
                    dve.tensor_tensor(chosen[:], chosen2[:], above[:], ALU.add).then_inc(sel_out.sem, 1)

            def c(g, step):
                p = g.off % 2
                if step[0] == "gu":
                    e, f = step[1], step[2]
                    n = e * FB + f
                    dve.wait_ge(tanh_out.sem, tanh_out.at(g, n + 1))
                    silu2_used = hid_pool_out if f in POOL_BLOCKS else hid_out
                    if e:
                        dve.wait_ge(silu2_used.sem, silu2_used.at(g, e))
                    elif not g.first(1):
                        dve.wait_ge(silu2_used.sem, silu2_used.at(g.back(1)))
                    dve.scalar_tensor_tensor(out=silu2[f][:], in0=tanh[f][:], scalar=1.0, in1=psG[f][:],
                                             op0=ALU.add, op1=ALU.mult).then_inc(silu_out.sem, 1)
                    if f in POOL_BLOCKS:
                        return
                    dve.wait_ge(silu_out.sem, silu_out.at(g, n + 1))
                    dve.wait_ge(u2_ps.sem, u2_ps.at(g, n + 1))
                    if e >= 2:
                        dve.wait_ge(y_ps.sem, y_ps.at(g, e - 1))
                    elif not g.first(1):
                        dve.wait_ge(y_ps.sem, y_ps.at(g.back(1)))
                    dve.scalar_tensor_tensor(out=hid[e % 2][f][:], in0=silu2[f][:], scalar=0.5, in1=psU[f][:],
                                             op0=ALU.mult, op1=ALU.mult).then_inc(hid_out.sem, 1)
                elif step[0] == "down":
                    e = step[1]
                    dve.wait_ge(y_ps.sem, y_ps.at(g, e + 1))
                    if e == 0:
                        dve.wait_ge(wtok_out.sem, wtok_out.at(g))
                        dve.wait_ge(x2_out.sem, x2_out.at(g))
                        dve.wait_ge(x2T_ps.sem, x2T_ps.at(g))
                    else:
                        dve.wait_ge(acc_out.sem, acc_out.at(g, e))
                    for b in range(G):
                        ins = dve.scalar_tensor_tensor(out=acc[p][:, b, :], in0=psY[:, b, :],
                                                       scalar=wtok[p][:, b, e:e + 1], in1=acc[p][:, b, :],
                                                       op0=ALU.mult, op1=ALU.add)
                    ins.then_inc(acc_out.sem, 1)
                elif step[0] == "weights":
                    dve.wait_ge(score_out.sem, score_out.at(g))
                    dve.tensor_reduce(smax[:], score[:], AX_X, ALU.max).then_inc(smax_out.sem, 1)
                    dve.wait_ge(smax_out.sem, smax_out.at(g))
                    if not g.first(1):
                        dve.wait_ge(sexp_out.sem, sexp_out.at(g.back(1)))
                    dve.tensor_tensor(sdiff[:], score[:], token(smax[:]), ALU.subtract).then_inc(sdiff_out.sem, 1)
                    dve.wait_ge(sel_out.sem, sel_out.at(g))
                    dve.wait_ge(sexp_out.sem, sexp_out.at(g))
                    dve.tensor_tensor(wexp[:], chosen[:], sexp[:], ALU.mult).then_inc(wexp_out.sem, 1)
                    dve.wait_ge(wexp_out.sem, wexp_out.at(g))
                    dve.tensor_reduce(wden[:], wexp[:], AX_X, ALU.add).then_inc(wden_out.sem, 1)
                    dve.wait_ge(wden_out.sem, wden_out.at(g))
                    dve.reciprocal(winv[:], wden[:]).then_inc(winv_out.sem, 1)
                    dve.wait_ge(winv_out.sem, winv_out.at(g))
                    dve.tensor_tensor(wtok[p][:], wexp[:], token(winv[:]), ALU.mult).then_inc(wtok_out.sem, 1)
                elif step[0] == "stats":
                    dve.wait_ge(acc_out.sem, acc_out.at(g))
                    if not g.first(1):
                        dve.wait_ge(var3_out.sem, var3_out.at(g.back(1)))
                    layer_stats(g, acc[p], bn6c, mv3, bn3_out, mv3_out)

            whole_program(dve, prep, ab, c)


_INS = ["x", "ctx_1024", "L0_attn_Wq", "L0_attn_Wk", "L0_attn_Wv", "L0_xattn_igate_w", "L0_xattn_igate_b",
        "L0_xattn_fgate_w", "L0_xattn_fgate_b", "L0_xattn_out_w", "L0_ffn_W_A", "L0_ffn_W_B", "L0_ffn_W_up",
        "L0_ffn_W_down"]


def kernel(**inputs):
    import numpy as np
    import concourse.bacc as bacc
    from concourse.bass_utils import run_bass_kernel_spmd

    nc = bacc.Bacc("TRN2", target_bir_lowering=False, num_devices=1)
    arrays, args = {}, []
    for name in _INS:
        a = np.ascontiguousarray(inputs[name])
        arrays[f"in_{name}"] = a
        args.append(nc.dram_tensor(f"in_{name}", a.shape, mybir.dt.from_np(a.dtype), kind="ExternalInput").ap())
    args.append(nc.dram_tensor("out_0", inputs["x"].shape, F32, kind="ExternalOutput").ap())
    decoder_kernel(nc, *args)
    r = run_bass_kernel_spmd(nc, [arrays], core_ids=[0])
    return r.results[0]["out_0"]
```

```python
from contextlib import ExitStack

import concourse.bass as bass
from concourse import mybir

ALU = mybir.AluOpType
ACT = mybir.ActivationFunctionType
F32 = mybir.dt.float32
F32R = mybir.dt.float32r
BF16 = mybir.dt.bfloat16
AX_X = mybir.AxisListType.X

NORM_EPS = 1e-5
GATE_EPS = 1e-6
MASKED = 1e30


class Stage:

    def __init__(self, sem, per):
        self.sem, self.per = sem, per

    def at(self, g, k=None):
        k = self.per if k is None else k
        return g.j * (2 * self.per) + (g.off * self.per + k)

    def at_parity(self, g):
        return g.j * self.per + (g.off // 2 + 1) * self.per


class Group:

    def __init__(self, j, off):
        self.j, self.off = j, off

    def back(self, n):
        return Group(self.j, self.off - n)

    def number(self):
        return self.j * 2 + self.off

    def first(self, n):
        return isinstance(self.j, int) and self.number() < n


def decoder_kernel(nc, x, ctx_in, wq, wk, wv, igate_w, igate_b, fgate_w, fgate_b, out_w,
                   w_a, w_b, w_up, w_down, out):
    B, S, D = x.shape
    H = igate_b.shape[0]
    DH = D // H
    E, R, _ = w_a.shape
    F = w_up.shape[1]
    FB = F // 128
    G = 4
    N = G * S
    GROUPS = B // G
    HG = 4
    HALVES = G * H // HG
    AC = E * R // 128
    VW = 2 * DH + 1
    GH = G * H
    assert S == 128 and D == 128 and GROUPS % 2 == 0 and R == 64 and FB == 2

    x_g = x.rearrange("(g b) n e -> g n b e", b=G)
    c_g = ctx_in.rearrange("(g b) n e -> g n b e", b=G)
    o_g = out.rearrange("(g b) n e -> g n b e", b=G)

    with ExitStack() as ctx:
        def sb(name, shape, dt=F32):
            return ctx.enter_context(nc.sbuf_tensor(name, shape, dt))

        def psum(name, shape, dt=F32):
            return ctx.enter_context(nc.psum_tensor(name, shape, dt))

        def sem(name):
            return ctx.enter_context(nc.semaphore(name))

        def stage(name, per=1):
            return Stage(sem(name), per)

        psG = [psum(f"psG{i}", [128, N]) for i in range(2)]
        psU = [psum(f"psU{i}", [128, N]) for i in range(2)]
        psY = psum("psY", [128, G, D])
        psA = psum("psA", [128, 512])
        psB = psum("psB", [128, 512])
        psC = psum("psC", [128, 512])

        ident = sb("ident", [128, 128])
        identb = sb("identb", [128, 128], BF16)
        future = sb("future", [128, HG, 128], BF16)
        headmask = sb("headmask", [128, H])
        restart = sb("restart", [128, G, E])
        minusone = sb("minusone", [128, G])
        epsilon = sb("epsilon", [128, G])
        minushalf = sb("minushalf", [128, GH])
        plushalf = sb("plushalf", [128, GH])
        ones = sb("ones", [GH, 128])

        y_out = sb("y_out", [S, G, D])
        wq_n, wk_n, wv_n = (y_out[:, i, :] for i in range(3))
        gate_n = sb("gate_n", [2 * H, 3 * D])
        gbias = sb("gbias", [2 * GH, 1])
        outw = sb("outw", [128, D])
        outw_s = sb("outw_s", [128, D])
        wa_r = sb("wa_r", [R, E, D])
        wa_n = sb("wa_n", [128, AC, D])
        wb_n = sb("wb_n", [128, E, FB, R])
        wup_n = sb("wup_n", [128, E, FB, D])
        wdn_n = sb("wdn_n", [D, E, FB, 128])

        qk_w = sb("qk_w", [D, D])
        wvT = sb("wvT", [D, D])
        gate_xT = sb("gate_xT", [D, 2 * H])
        gate_cT = sb("gate_cT", [D, 2 * H])
        gate_t = sb("gate_t", [D, 2 * H])
        gate_p = sb("gate_p", [D, 2, G, 2 * GH])
        wbT = sb("wbT", [R, E, F])
        gw_hi = sb("gw_hi", [D, E, F], F32R)
        gw_lo = sb("gw_lo", [D, E, F], F32R)
        uw_hi = sb("uw_hi", [D, E, F], F32R)
        uw_lo = sb("uw_lo", [D, E, F], F32R)
        aw_hi = sb("aw_hi", [D, E * R], F32R)
        aw_lo = sb("aw_lo", [D, E * R], F32R)
        dwT = sb("dwT", [128, E, FB, D])

        xin = [sb(f"xin{i}", [128, G, D]) for i in range(2)]
        cin = [sb(f"cin{i}", [128, G, D]) for i in range(2)]
        xT = sb("xT", [D, G, S])
        zT = sb("zT", [D, G, S])
        v_sb = sb("v_sb", [S, G, D])
        rowmax = sb("rowmax", [S, G])
        negmax = sb("negmax", [S, G])
        probs = sb("probs", [S, G, S])
        rowsum = sb("rowsum", [S, G])
        rowsum_n = sb("rowsum_n", [S, G])
        rowinv = sb("rowinv", [S, G])
        probsT = sb("probsT", [S, G, S])
        res1 = sb("res1", [S, G, D])
        bn6 = sb("bn6", [S, G, 6])
        mv1 = sb("mv1", [S, G, 2])
        var1 = sb("var1", [S, G])
        rstd1 = sb("rstd1", [S, G])
        x1 = sb("x1", [S, G, D])
        x1T = sb("x1T", [D, G, S])
        cT = sb("cT", [D, G, S])
        kmask = sb("kmask", [D, 2, H, S])
        vmean = sb("vmean", [S, GH])
        vsum = sb("vsum", [S, GH])
        vaug = sb("vaug", [S, GH, VW])
        f_in = sb("f_in", [GH, S])
        f_neg = sb("f_neg", [GH, S])
        f_exp = sb("f_exp", [GH, S])
        f_ln = sb("f_ln", [GH, S])
        logf = sb("logf", [GH, S])
        cumf = sb("cumf", [GH, S])
        arow_t = sb("arow_t", [3 * GH, S])
        arow = arow_t[2 * GH:3 * GH, :]
        amax = sb("amax", [GH, S])
        amax2 = sb("amax2", [2 * GH, S], F32R)
        arow2 = sb("arow2", [4 * GH, S], F32R)
        decay_w = sb("decay_w", [4 * GH, G, S], F32R)
        decay_x = sb("decay_x", [4 * GH, H, S], F32R)
        batch_rows = sb("batch_rows", [4 * GH, G])
        batch_4 = sb("batch_4", [4 * GH, 4, G])
        head_rows = sb("head_rows", [4 * GH, H])
        head_16 = sb("head_16", [4 * GH, 4 * G, H])
        mrow = sb("mrow", [GH, S])
        expm = sb("expm", [S, GH])
        decay = [sb(f"decay{i}", [S, HG, S]) for i in range(2)]
        cmat = [sb(f"cmat{i}", [S, HG, S]) for i in range(2)]
        u_sb = sb("u_sb", [S, GH, VW])
        usq = sb("usq", [S, H, DH])
        uss = sb("uss", [S, GH])
        sum_abs = sb("sum_abs", [S, GH])
        nrm = sb("nrm", [S, GH])
        expm_e = sb("expm_e", [S, GH])
        nrm_2 = sb("nrm_2", [S, GH])
        hvar = sb("hvar", [S, GH])
        hrstd = sb("hrstd", [S, GH])
        hn = sb("hn", [S, H, DH])
        res2 = sb("res2", [S, G, D])
        bn6b = sb("bn6b", [S, G, 6])
        mv2 = sb("mv2", [S, G, 2])
        var2 = sb("var2", [S, G])
        rstd2 = sb("rstd2", [S, G])

        acc = [sb(f"acc{i}", [S, G, D]) for i in range(2)]
        x2hi = [sb(f"x2hi{i}", [D, G, S], F32R) for i in range(2)]
        x2lo = [sb(f"x2lo{i}", [D, G, S], F32R) for i in range(2)]
        hidsq = [sb(f"hidsq{i}", [S, E * R]) for i in range(2)]
        sc2 = sb("sc2", [S, G, E])
        score = sb("score", [S, G, E])
        top8 = sb("top8", [S, G, 8])
        is1 = sb("is1", [S, G])
        smax = sb("smax", [S, G])
        lim = sb("lim", [S, G])
        above = sb("above", [S, G, E])
        equal = sb("equal", [S, G, E])
        rank = sb("rank", [S, G, E])
        inlim = sb("inlim", [S, G, E])
        chosen2 = sb("chosen2", [S, G, E])
        chosen = sb("chosen", [S, G, E])
        sdiff = sb("sdiff", [S, G, E])
        sexp = sb("sexp", [S, G, E])
        wexp = sb("wexp", [S, G, E])
        wden = sb("wden", [S, G])
        winv = sb("winv", [S, G])
        wtok = [sb(f"wtok{i}", [S, G, E]) for i in range(2)]
        tanh = [sb(f"tanh{i}", [128, N]) for i in range(2)]
        silu2 = [sb(f"silu2{i}", [128, N]) for i in range(2)]
        hid = [[sb(f"hid{i}{f}", [128, N]) for f in range(FB)] for i in range(2)]
        up = sb("up", [128, N])
        POOL_BLOCKS = (1,)
        bn6c = sb("bn6c", [S, G, 6])
        mv3 = sb("mv3", [S, G, 2])
        var3 = sb("var3", [S, G])
        rstd3 = sb("rstd3", [S, G])
        negmean3 = sb("negmean3", [S, G])
        nmr3 = sb("nmr3", [S, G])

        qkv_loaded = sem("qkv_loaded")
        gate_loaded = sem("gate_loaded")
        bias_loaded = sem("bias_loaded")
        outw_loaded = sem("outw_loaded")
        wb_loaded = sem("wb_loaded")
        war_loaded = sem("war_loaded")
        wup_loaded = sem("wup_loaded")
        wan_loaded = sem("wan_loaded")
        wdn_loaded = sem("wdn_loaded")
        ident_ready = sem("ident_ready")
        const_step = sem("const_step")
        const_ready = sem("const_ready")
        prep_ps = sem("prep_ps")
        prep_out = sem("prep_out")
        prep_hi = sem("prep_hi")
        qkv_out = sem("qkv_out")
        gate_step = sem("gate_step")
        rows_ready = sem("rows_ready")
        outw_ready = sem("outw_ready")

        x_loaded = [stage(f"x_loaded{i}", 16) for i in range(2)]
        c_loaded = [stage(f"c_loaded{i}", 16) for i in range(2)]
        xT_ps, xT_sb = stage("xT_ps"), stage("xT_sb")
        z_ps, zT_sb = stage("z_ps"), stage("zT_sb")
        v_ps, v_out = stage("v_ps"), stage("v_out")
        logits_ps, max_out, negmax_out = stage("logits_ps"), stage("max_out"), stage("negmax_out")
        probs_out, rown_out, rowinv_out = stage("probs_out"), stage("rown_out"), stage("rowinv_out")
        pT_ps, pT_sb = stage("pT_ps"), stage("pT_sb")
        cT_ps, cT_sb = stage("cT_ps"), stage("cT_sb")
        kmask_out = stage("kmask_out", G)
        vsum_out, vmean_out, vc_out, vaug_out = stage("vsum_out"), stage("vmean_out"), stage("vc_out"), stage("vaug_out")
        att_ps, res1_out, bn1_out, mv1_out = stage("att_ps"), stage("res1_out"), stage("bn1_out"), stage("mv1_out")
        var1_out, rstd1_out, x1_out = stage("var1_out"), stage("rstd1_out"), stage("x1_out")
        x1T_ps, x1T_sb = stage("x1T_ps"), stage("x1T_sb")
        gates_ps = stage("gates_ps")
        f_out, fneg_out, fexp_out, fln_out = stage("f_out"), stage("fneg_out"), stage("fexp_out"), stage("fln_out")
        logf_out, cumf_out, arow_out = stage("logf_out"), stage("cumf_out"), stage("arow_out")
        maxrows0_out, maxrows1_out, arows_out = stage("maxrows0_out"), stage("maxrows1_out"), stage("arows_out")
        arowhi_out, arow2_out = stage("arowhi_out"), stage("arow2_out")
        amaxhi_out, amax2_out = stage("amaxhi_out"), stage("amax2_out")
        amax_out, mrow_out = stage("amax_out"), stage("mrow_out")
        am_ps, expm_out, expm_e_out = stage("am_ps"), stage("expm_out"), stage("expm_e_out")
        mb_ps, qk_ps = stage("mb_ps", HALVES), stage("qk_ps", HALVES)
        decay_out, cmat_out = stage("decay_out", HALVES), stage("cmat_out", HALVES)
        u_ps, u_out = stage("u_ps", HALVES), stage("u_out", HALVES)
        usq_out, uss_out = stage("usq_out", G), stage("uss_out", G)
        sumabs_out = stage("sumabs_out", G)
        nrm_out, nrm2_out = stage("nrm_out", G), stage("nrm2_out", G)
        hvar_out, hrstd_out, hn_out = stage("hvar_out", G), stage("hrstd_out", G), stage("hn_out", G)
        res2_out, bn2_out, mv2_out = stage("res2_out", G), stage("bn2_out", G), stage("mv2_out", G)
        var2_out, rstd2_out, x2_out = stage("var2_out"), stage("rstd2_out"), stage("x2_out")
        x2T_ps, x2hi_out, x2lo_out = stage("x2T_ps"), stage("x2hi_out"), stage("x2lo_out")
        hid_ps, hidsq_out = stage("hid_ps", G), stage("hidsq_out", G)
        sc2_out, score_out = stage("sc2_out", G), stage("score_out", G)
        top_out, is1_out, lim_out = stage("top_out"), stage("is1_out"), stage("lim_out")
        above_out, smax_out, nmr3_out = stage("above_out"), stage("smax_out"), stage("nmr3_out")
        negmean3_out = stage("negmean3_out")
        up_out = stage("up_out", E)
        hid_pool_out = stage("hid_pool_out", E)
        eq_out, rank_out, inlim_out = stage("eq_out"), stage("rank_out"), stage("inlim_out")
        ch2_out, sel_out, sdiff_out = stage("ch2_out"), stage("sel_out"), stage("sdiff_out")
        sexp_out, wexp_out, wden_out = stage("sexp_out"), stage("wexp_out"), stage("wden_out")
        winv_out, wtok_out = stage("winv_out"), stage("wtok_out")
        g_ps, u2_ps = stage("g_ps", E * FB), stage("u2_ps", E * FB)
        tanh_out, silu_out, hid_out = stage("tanh_out", E * FB), stage("silu_out", E * FB), stage("hid_out", E)
        y_ps, acc_out = stage("y_ps", E), stage("acc_out", E)
        bn3_out, mv3_out, var3_out = stage("bn3_out"), stage("mv3_out"), stage("var3_out")
        rstd3_out, y_ready = stage("rstd3_out"), stage("y_ready")
        stored = stage("stored", 16)

        UP_BANKS = B_BANKS = E * FB // 4
        GW_BANKS = E // 2
        NAMES = ["small"] + [("wbT", i) for i in range(B_BANKS)] + [("gw", i) for i in range(GW_BANKS)]
        NAMES += [("up", i) for i in range(UP_BANKS)] + ["wa"] + [("down", i) for i in range(UP_BANKS)]
        PREP = list(enumerate(NAMES))
        SPLITS = [i for i in NAMES if i == "wa" or i[0] in ("gw", "up")]
        prep_banks = [psG[0], psG[1], psU[0], psU[1]]

        def down_bank(e):
            return psG[1][:].rearrange("s (b d) -> s b d", b=G) if e == E - 1 else psY[:]

        def prep_bank(n):
            return prep_banks[n % 4]

        def parts(item):
            if item == "wa":
                return aw_hi[:], aw_lo[:]
            pair = (gw_hi, gw_lo) if item[0] == "gw" else (uw_hi, uw_lo)
            return [t[:, 2 * item[1]:2 * item[1] + 2, :].rearrange("h e f -> h (e f)") for t in pair]

        def expert_steps():
            for e in range(E):
                for f in range(FB):
                    yield "g", e, f
                    yield "u", e, f
                yield ("down", e - 1) if e else ("weights",)
            yield "down", E - 1
            yield "stats",

        CHAIN = [1, 2, 4, 2, 4, 4, 1, 1, 4, 0]
        HALF = [1, 0, 0, 0, 0, 0, 0, 1, 0]
        TAIL = [3, 2, 3, 1]
        HIDDEN = [0, 1, 1, 0]
        SCORE = [2, 0, 1, 0]
        LAST = 1
        FINISH = "pT"
        PREP_BEHIND = [1, 3, 0, 1, 2, 2, 2, 0, 2, 0, 0, 0, 0, 0, 0, 0, 0, 0, 0, 0, 0, 0, 0, 0, 0, 2, 2, 0, 1,
                       0, 0, 0, 0, 0, 0, 0, 0, 0]
        AB = list(zip(("xT", "zv", "logits", "pT", "att", "x1", "x1T", "gates", "scan", "am"), CHAIN))
        for k in range(HALVES + 1):
            AB += [(("half", k), HALF[k])]
            if k and k % 2 == 0:
                AB += [(("norm", k // 2 - 1), 0 if k < HALVES else TAIL[0])]
            if k >= 3 and k % 2 == 1:
                AB += [(("head", k // 2 - 1), 0)]
        AB += [(("head", G - 1), TAIL[1]), ("x2", TAIL[2]), ("x2T", TAIL[3])]
        AB += [(("hidden", b), HIDDEN[b]) for b in range(G)]
        AB += [(("score", b), SCORE[b]) for b in range(G)]
        AB += [("choose", LAST)]

        def both_stages():
            experts = list(expert_steps())

            def take(n):
                while experts and (n > 0 or experts[0][0] == "weights"):
                    n -= experts[0][0] in ("g", "u", "down")
                    yield "C", experts.pop(0)
            for step, n in AB:
                yield "AB", step
                if step == FINISH:
                    yield "C", ("finish",)
                yield from take(n)
            while experts:
                yield "C", experts.pop(0)

        ACT_LATER = {'logits': 1, 'zv': 1}
        DVE_LATER = {'logits': -1, ('half', 0): -1, 'xT': 1}
        POOL_LATER = {('half', 7): 1}

        def shifted(steps, later):
            steps = list(steps)
            for step, n in later.items():
                i, way = steps.index(("AB", step)), 1 if n > 0 else -1
                for _ in range(abs(n)):
                    if 0 <= i + way < len(steps) and steps[i + way][0] == "C":
                        steps[i], steps[i + way] = steps[i + way], steps[i]
                        i += way
            return steps

        def whole_program(eng, prep, ab, c, later):
            def both(g):
                for part, step in shifted(both_stages(), later):
                    if part == "AB":
                        ab(Group(g.j, g.off + 1), step)
                    elif step[0] != "finish":
                        c(g, step)
                    elif not g.first(1):
                        c(g.back(1), step)
            todo = list(PREP)
            for n, (step, _) in enumerate(AB):
                ab(Group(0, 0), step)
                for item in todo[:PREP_BEHIND[n]]:
                    prep(item)
                del todo[:PREP_BEHIND[n]]
            assert not todo
            both(Group(0, 0))
            with eng.Fori(0, (GROUPS - 2) // 2) as j:
                both(Group(j, 1))
                both(Group(j, 2))
            for step in expert_steps():
                c(Group(0, GROUPS - 1), step)
                if step[0] == "weights":
                    c(Group(0, GROUPS - 2), ("finish",))
            c(Group(0, GROUPS - 1), ("finish",))

        def plain_wait(eng):
            eng.wait_ge(const_ready, 1)

        def spread_heads(eng, half):
            heads = slice(half * HG, (half + 1) * HG)
            return eng.tensor_tensor(decay_x[0:2 * GH, heads, :],
                                     amax2[:].bitcast(F32).unsqueeze(1).to_broadcast([2 * GH, HG, S]),
                                     head_rows[0:2 * GH, heads].unsqueeze(2).to_broadcast([2 * GH, HG, S]), ALU.mult)

        block = ctx.enter_context(nc.Block())

        @block.sync
        def _(sp):
            def load(g):
                p = g.off % 2
                if not g.first(2):
                    sp.wait_ge(res1_out.sem, res1_out.at(g.back(2)))
                    sp.wait_ge(cT_ps.sem, cT_ps.at(g.back(2)))
                    sp.wait_ge(vc_out.sem, vc_out.at(g.back(2)))
                i = g.number()
                src_x = x_g[i] if isinstance(i, int) else x_g[bass.ds(i, 1)].rearrange("g n b e -> (g n) b e")
                src_c = c_g[i] if isinstance(i, int) else c_g[bass.ds(i, 1)].rearrange("g n b e -> (g n) b e")
                sp.dma_start(xin[p][:], src_x).then_inc(x_loaded[p].sem, 16)
                sp.dma_start(cin[p][:], src_c).then_inc(c_loaded[p].sem, 16)

            def store(g):
                p = g.off % 2
                i = g.number()
                dst = o_g[i] if isinstance(i, int) else o_g[bass.ds(i, 1)].rearrange("g n b e -> (g n) b e")
                sp.wait_ge(y_ready.sem, y_ready.at(g))
                sp.dma_start(dst, y_out[:]).then_inc(stored.sem, 16)

            sp.dma_start(xin[0][:], x_g[0]).then_inc(x_loaded[0].sem, 16)
            for t, src in ((wq_n, wq), (wk_n, wk), (wv_n, wv)):
                sp.dma_start(t, src).then_inc(qkv_loaded, 16)
            sp.dma_start(gate_n[0:H, :], igate_w).then_inc(gate_loaded, 16)
            sp.dma_start(gate_n[H:2 * H, :], fgate_w).then_inc(gate_loaded, 16)
            sp.dma_start(cin[0][:], c_g[0]).then_inc(c_loaded[0].sem, 16)
            sp.dma_start(wb_n[:], w_b.rearrange("e (k f) r -> f e k r", f=128)).then_inc(wb_loaded, 16)
            sp.dma_start(wa_r[:], w_a.rearrange("e r h -> r e h")).then_inc(war_loaded, 16)
            sp.dma_start(outw[:], out_w.rearrange("(a d) -> a d", a=1).to_broadcast([128, D])).then_inc(outw_loaded, 16)
            sp.dma_start(wup_n[:], w_up.rearrange("e (k f) h -> f e k h", f=128)).then_inc(wup_loaded, 16)
            for b in range(G):
                sp.dma_start(gbias[b * H:(b + 1) * H, :],
                             igate_b.rearrange("(h a) -> h a", a=1)).then_inc(bias_loaded, 16)
                sp.dma_start(gbias[GH + b * H:GH + (b + 1) * H, :],
                             fgate_b.rearrange("(h a) -> h a", a=1)).then_inc(bias_loaded, 16)
            sp.dma_start(wa_n[:], w_a.rearrange("(c a) r h -> (a r) c h", a=2)).then_inc(wan_loaded, 16)
            sp.dma_start(wdn_n[:], w_down.rearrange("e h (k f) -> h e k f", f=128)).then_inc(wdn_loaded, 16)
            load(Group(0, 1))
            load(Group(0, 2))
            store(Group(0, 0))
            with sp.Fori(0, (GROUPS - 4) // 2) as j:
                load(Group(j, 3))
                store(Group(j, 1))
                load(Group(j, 4))
                store(Group(j, 2))
            load(Group(0, GROUPS - 1))
            for i in range(GROUPS - 3, GROUPS):
                store(Group(0, i))
            sp.wait_ge(stored.sem, stored.at(Group(0, GROUPS - 1)))

        @block.gpsimd
        def _(pool):
            steps = [0]

            def done(ins):
                steps[0] += 1
                ins.then_inc(const_step, 1)
                pool.wait_ge(const_step, steps[0])

            done(pool.memset(ident[:], 0.0))
            done(pool.affine_select(out=ident[:], in_=ident[:], pattern=[[-1, 128]], base=0,
                                    channel_multiplier=1, compare_op=ALU.not_equal, fill=1.0))
            pool.tensor_copy(identb[:], ident[:]).then_inc(ident_ready, 1)
            pool.wait_ge(ident_ready, 1)
            done(pool.memset(ones[:], 1.0))
            done(pool.memset(minusone[:], -1.0))
            done(pool.memset(epsilon[:], NORM_EPS))
            done(pool.memset(minushalf[:], -0.5))
            done(pool.memset(plushalf[:], 0.5))
            done(pool.memset(future[:], 0.0))
            done(pool.affine_select(out=future[:], in_=future[:], pattern=[[0, HG], [1, 128]], base=0,
                                    channel_multiplier=-1, compare_op=ALU.is_ge, fill=MASKED))
            done(pool.memset(headmask[:], 1.0))
            done(pool.affine_select(out=headmask[:], in_=headmask[:], pattern=[[-DH, H]], base=0,
                                    channel_multiplier=1, compare_op=ALU.is_ge, fill=0.0))
            done(pool.affine_select(out=headmask[:], in_=headmask[:], pattern=[[DH, H]], base=DH - 1,
                                    channel_multiplier=-1, compare_op=ALU.is_ge, fill=0.0))
            done(pool.memset(batch_4[:], 1.0))
            done(pool.affine_select(out=batch_4[:], in_=batch_4[:], pattern=[[-GH, 4], [-H, G]], base=0,
                                    channel_multiplier=1, compare_op=ALU.is_ge, fill=0.0))
            done(pool.affine_select(out=batch_4[:], in_=batch_4[:], pattern=[[GH, 4], [H, G]], base=H - 1,
                                    channel_multiplier=-1, compare_op=ALU.is_ge, fill=0.0))
            done(pool.memset(head_16[:], 0.0))
            done(pool.affine_select(out=head_16[:], in_=head_16[:], pattern=[[-H, 4 * G], [-1, H]], base=0,
                                    channel_multiplier=1, compare_op=ALU.not_equal, fill=1.0))
            done(pool.memset(restart[:], 1.0))
            done(pool.affine_select(out=restart[:], in_=restart[:], pattern=[[0, G], [1, E]], base=0,
                                    channel_multiplier=0, compare_op=ALU.not_equal, fill=0.0))
            done(pool.memset(gate_p[:], 0.0))
            pool.memset(vaug[:], 1.0).then_inc(const_ready, 1)
            pool.wait_ge(const_ready, 1)

            def rstd(g, mv, var, out_, mv_stage, var_stage, out_stage, readers):
                pool.wait_ge(mv_stage.sem, mv_stage.at(g))
                if not g.first(1):
                    pool.wait_ge(readers.sem, readers.at(g.back(1)))
                pool.tensor_tensor(var[:], mv[:, :, 1], epsilon[:, 0:G], ALU.add).then_inc(var_stage.sem, 1)
                pool.wait_ge(var_stage.sem, var_stage.at(g))
                pool.tensor_tensor(out_[:], var[:], minushalf[:, 0:G], ALU.pow).then_inc(out_stage.sem, 1)

            def mask_heads(b):
                pool.tensor_tensor(kmask[:, b % 2, :, :], cT[:, b, :].unsqueeze(1).to_broadcast([D, H, S]),
                                   headmask[:].unsqueeze(2).to_broadcast([D, H, S]),
                                   ALU.mult).then_inc(kmask_out.sem, 1)

            def ab(g, step):
                p = g.off % 2
                if step == "pT":
                    pool.wait_ge(vmean_out.sem, vmean_out.at(g))
                    if not g.first(1):
                        pool.wait_ge(u_ps.sem, u_ps.at(g.back(1)))
                    pool.tensor_tensor(vaug[:, :, 0:DH], cin[p][:].rearrange("t b (h d) -> t (b h) d", d=DH),
                                       vmean[:].unsqueeze(2).to_broadcast([S, GH, DH]),
                                       ALU.subtract).then_inc(vc_out.sem, 1)
                    pool.wait_ge(vc_out.sem, vc_out.at(g))
                    if g.first(1):
                        pool.wait_ge(outw_ready, 1)
                    for b in range(G):
                        ins = pool.tensor_tensor(vaug[:, b * H:(b + 1) * H, DH:2 * DH], vaug[:, b * H:(b + 1) * H, 0:DH],
                                                 outw_s[:].rearrange("p (h d) -> p h d", d=DH), ALU.mult)
                    ins.then_inc(vaug_out.sem, 1)
                elif step == "x1T":
                    pool.wait_ge(cT_sb.sem, cT_sb.at(g))
                    if not g.first(1):
                        pool.wait_ge(qk_ps.sem, qk_ps.at(g.back(1)))
                    mask_heads(0)
                    mask_heads(1)
                elif step[0] == "half" and step[1] in (2, 4):
                    pool.wait_ge(qk_ps.sem, qk_ps.at(g, step[1]))
                    mask_heads(step[1] // 2 + 1)
                elif step == "scan":
                    pool.wait_ge(arow2_out.sem, arow2_out.at(g))
                    if g.first(1):
                        pool.wait_ge(rows_ready, 1)
                    else:
                        pool.wait_ge(mb_ps.sem, mb_ps.at(g.back(1)))
                    pool.tensor_tensor(decay_w[:], arow2[:].bitcast(F32).unsqueeze(1).to_broadcast([4 * GH, G, S]),
                                       batch_rows[:].unsqueeze(2).to_broadcast([4 * GH, G, S]),
                                       ALU.mult).then_inc(arows_out.sem, 1)
                    pool.wait_ge(amax2_out.sem, amax2_out.at(g))
                    spread_heads(pool, 1).then_inc(maxrows1_out.sem, 1)
                elif step == "att":
                    rstd(g, mv1, var1, rstd1, mv1_out, var1_out, rstd1_out, x1_out)
                elif step[0] == "norm":
                    b = step[1]
                    heads = slice(b * H, (b + 1) * H)
                    pool.wait_ge(hvar_out.sem, hvar_out.at(g, b + 1))
                    if b == 0 and not g.first(1):
                        pool.wait_ge(hn_out.sem, hn_out.at(g.back(1)))
                    pool.tensor_tensor(hrstd[:, heads], hvar[:, heads], minushalf[:, 0:H], ALU.pow)\
                        .then_inc(hrstd_out.sem, 1)
                elif step == ("head", G - 1):
                    rstd(g, mv2, var2, rstd2, mv2_out, var2_out, rstd2_out, x2_out)
                elif step[0] == "score":
                    b = step[1]
                    pool.wait_ge(sc2_out.sem, sc2_out.at(g, b + 1))
                    if b == 0 and not g.first(1):
                        pool.wait_ge(sdiff_out.sem, sdiff_out.at(g.back(1)))
                    pool.tensor_tensor(score[:, b, :], sc2[:, b, :], plushalf[:, 0:E], ALU.pow)\
                        .then_inc(score_out.sem, 1)

            def c(g, step):
                if step[0] == "stats":
                    pool.wait_ge(mv3_out.sem, mv3_out.at(g))
                    pool.tensor_tensor(negmean3[:], mv3[:, :, 0], minusone[:, 0:G], ALU.mult).then_inc(negmean3_out.sem, 1)
                    rstd(g, mv3, var3, rstd3, mv3_out, var3_out, rstd3_out, y_ready)
                    pool.wait_ge(rstd3_out.sem, rstd3_out.at(g))
                    pool.wait_ge(negmean3_out.sem, negmean3_out.at(g))
                    pool.tensor_tensor(nmr3[:], negmean3[:], rstd3[:], ALU.mult).then_inc(nmr3_out.sem, 1)
                elif step[0] == "u" and step[2] in POOL_BLOCKS:
                    e, f = step[1], step[2]
                    n = e * FB + f
                    pool.wait_ge(silu_out.sem, silu_out.at(g, n + 1))
                    pool.wait_ge(up_out.sem, up_out.at(g, e + 1))
                    if e >= 2:
                        pool.wait_ge(y_ps.sem, y_ps.at(g, e - 1))
                    elif not g.first(1):
                        pool.wait_ge(y_ps.sem, y_ps.at(g.back(1)))
                    pool.tensor_tensor(hid[e % 2][f][:], silu2[f][:], up[:], ALU.mult).then_inc(hid_pool_out.sem, 1)

            whole_program(pool, lambda item: None, ab, c, POOL_LATER)

        @block.tensor
        def _(pe):
            pe.wait_ge(ident_ready, 1)

            def prep(numbered):
                n, item = numbered
                ps = prep_bank(n)
                if n >= 4:
                    pe.wait_ge(prep_out, n - 3)
                if item == "small":
                    pe.wait_ge(qkv_loaded, 16 * 3)
                    pe.wait_ge(gate_loaded, 16 * 2)
                    pe.matmul(ps[:, 0:128], wq_n, wk_n, start=True, stop=True)
                    pe.transpose(ps[:, 128:256], wv_n, ident[:])
                    for k in range(3):
                        ins = pe.transpose(ps[:, 256 + 2 * H * k:256 + 2 * H * (k + 1)],
                                           gate_n[:, k * D:(k + 1) * D], ident[0:2 * H, 0:2 * H])
                elif item == "wa":
                    pe.wait_ge(wan_loaded, 16)
                    for k in range(AC):
                        ins = pe.transpose(ps[:, k * 128:(k + 1) * 128], wa_n[:, k, :], ident[:])
                elif item[0] == "wbT":
                    if item[1] == 0:
                        pe.wait_ge(wb_loaded, 16)
                    for k in range(4):
                        q = item[1] * 4 + k
                        ins = pe.transpose(ps[0:R, k * 128:(k + 1) * 128], wb_n[:, q // FB, q % FB, :], ident[:])
                elif item[0] == "gw":
                    if item[1] == 0:
                        pe.wait_ge(war_loaded, 16)
                        pe.wait_ge(prep_out, 1 + B_BANKS)
                    for k in range(2):
                        e = item[1] * 2 + k
                        ins = pe.matmul(ps[:, k * F:(k + 1) * F], wa_r[:, e, :], wbT[:, e, :], start=True, stop=True)
                else:
                    src, loaded = (wup_n, wup_loaded) if item[0] == "up" else (wdn_n, wdn_loaded)
                    if item[1] == 0:
                        pe.wait_ge(loaded, 16)
                    for k in range(4):
                        q = item[1] * 4 + k
                        ins = pe.transpose(ps[:, k * 128:(k + 1) * 128], src[:, q // FB, q % FB, :], ident[:])
                ins.then_inc(prep_ps, 1)

            def split_product(out_, w_hi, w_lo, x_hi, x_lo):
                pe.matmul(out_, w_lo, x_hi, start=True, stop=False)
                pe.matmul(out_, w_hi, x_lo, start=False, stop=False)
                return pe.matmul(out_, w_hi, x_hi, start=False, stop=True)

            def ab(g, step):
                p = g.off % 2
                if step == "xT":
                    pe.wait_ge(x_loaded[p].sem, x_loaded[p].at_parity(g))
                    if not g.first(1):
                        pe.wait_ge(x2lo_out.sem, x2lo_out.at(g.back(1)))
                    for b in range(G):
                        ins = pe.transpose(psA[:, b * S:(b + 1) * S], xin[p][:, b, :], ident[:])
                    ins.then_inc(xT_ps.sem, 1)
                elif step == "zv":
                    pe.wait_ge(xT_sb.sem, xT_sb.at(g))
                    if g.first(1):
                        pe.wait_ge(qkv_out, 1)
                    if not g.first(1):
                        pe.wait_ge(hidsq_out.sem, hidsq_out.at(g.back(1)))
                    pe.matmul(psB[:], qk_w[:], xT[:].rearrange("e b s -> e (b s)"), start=True, stop=True)\
                        .then_inc(z_ps.sem, 1)
                    for b in range(G):
                        ins = pe.matmul(psC[:, b * D:(b + 1) * D], xT[:, b, :], wvT[:], start=True, stop=True)
                    ins.then_inc(v_ps.sem, 1)
                elif step == "logits":
                    pe.wait_ge(zT_sb.sem, zT_sb.at(g))
                    for b in range(G):
                        ins = pe.matmul(psA[:, b * S:(b + 1) * S], zT[:, b, :], xT[:, b, :], start=True, stop=True)
                    ins.then_inc(logits_ps.sem, 1)
                elif step == "pT":
                    pe.wait_ge(c_loaded[p].sem, c_loaded[p].at_parity(g))
                    pe.wait_ge(v_out.sem, v_out.at(g))
                    for b in range(G):
                        ins = pe.transpose(psC[:, b * S:(b + 1) * S], cin[p][:, b, :], ident[:])
                    ins.then_inc(cT_ps.sem, 1)
                    pe.wait_ge(probs_out.sem, probs_out.at(g))
                    for b in range(G):
                        ins = pe.transpose(psB[:, b * S:(b + 1) * S], probs[:, b, :], ident[:])
                    ins.then_inc(pT_ps.sem, 1)
                elif step == "att":
                    pe.wait_ge(pT_sb.sem, pT_sb.at(g))
                    for b in range(G):
                        ins = pe.matmul(psA[:, b * D:(b + 1) * D], probsT[:, b, :], v_sb[:, b, :], start=True, stop=True)
                    ins.then_inc(att_ps.sem, 1)
                elif step == "x1T":
                    pe.wait_ge(x1_out.sem, x1_out.at(g))
                    for b in range(G):
                        ins = pe.transpose(psB[:, b * S:(b + 1) * S], x1[:, b, :], ident[:])
                    ins.then_inc(x1T_ps.sem, 1)
                elif step == "gates":
                    pe.wait_ge(x1T_sb.sem, x1T_sb.at(g))
                    pe.wait_ge(cT_sb.sem, cT_sb.at(g))
                    if g.first(1):
                        pe.wait_ge(prep_out, 1)
                    for b in range(G):
                        pe.matmul(psC[0:2 * GH, 0:S], gate_p[:, 0, b, :], x1T[:, b, :], start=(b == 0), stop=False)
                        ins = pe.matmul(psC[0:2 * GH, 0:S], gate_p[:, 1, b, :], cT[:, b, :], start=False,
                                        stop=(b == G - 1))
                    ins.then_inc(gates_ps.sem, 1)
                elif step == "am":
                    pe.wait_ge(mrow_out.sem, mrow_out.at(g))
                    pe.wait_ge(res1_out.sem, res1_out.at(g))
                    pe.matmul(psA[:, 0:GH], mrow[:], ident[0:GH, 0:GH], start=True, stop=True)\
                        .then_inc(am_ps.sem, 1)
                elif step[0] == "half":
                    k = step[1]
                    if k < HALVES:
                        b, h0 = k // 2, HG * (k % 2)
                        if k == 0:
                            if g.first(1):
                                pe.wait_ge(rows_ready, 1)
                            pe.wait_ge(maxrows0_out.sem, maxrows0_out.at(g))
                            pe.wait_ge(arows_out.sem, arows_out.at(g))
                            pe.wait_ge(x1T_sb.sem, x1T_sb.at(g))
                            pe.wait_ge(arow_out.sem, arow_out.at(g))
                        else:
                            pe.wait_ge(decay_out.sem, decay_out.at(g, k))
                        if k == 1:
                            pe.wait_ge(maxrows1_out.sem, maxrows1_out.at(g))
                        pe.matmul(psB[:], identb[:], future[:].rearrange("t h s -> t (h s)"), start=True, stop=False)
                        pe.matmul(psB[:], decay_w[:, b, :], decay_x[:, h0:h0 + HG, :].rearrange("r h s -> r (h s)"),
                                  start=False, stop=True)\
                            .then_inc(mb_ps.sem, 1)
                        if k % 2 == 0:
                            pe.wait_ge(kmask_out.sem, kmask_out.at(g, b + 1))
                        if k:
                            pe.wait_ge(cmat_out.sem, cmat_out.at(g, k))
                        for i in range(HG):
                            ins = pe.matmul(psC[:, i * S:(i + 1) * S], kmask[:, b % 2, h0 + i, :], x1T[:, b, :],
                                            start=True, stop=True)
                        ins.then_inc(qk_ps.sem, 1)
                    if k:
                        q = k - 1
                        b, h0 = q // 2, HG * (q % 2)
                        pe.wait_ge(cmat_out.sem, cmat_out.at(g, q + 1))
                        if q == 0:
                            pe.wait_ge(expm_out.sem, expm_out.at(g))
                            pe.wait_ge(vaug_out.sem, vaug_out.at(g))
                        else:
                            pe.wait_ge(u_out.sem, u_out.at(g, q))
                        for i in range(HG):
                            ins = pe.matmul(psA[:, i * VW:(i + 1) * VW], cmat[q % 2][:, i, :], vaug[:, b * H + h0 + i, :],
                                            start=True, stop=True)
                        ins.then_inc(u_ps.sem, 1)
                elif step == "x2T":
                    pe.wait_ge(x2_out.sem, x2_out.at(g))
                    pe.wait_ge(u_out.sem, u_out.at(g))
                    for b in range(G):
                        ins = pe.transpose(psA[:, b * S:(b + 1) * S], acc[p][:, b, :], ident[:])
                    ins.then_inc(x2T_ps.sem, 1)
                elif step[0] == "hidden":
                    b = step[1]
                    if b == 0:
                        if g.first(1):
                            pe.wait_ge(prep_out, len(PREP))
                        pe.wait_ge(x2lo_out.sem, x2lo_out.at(g))
                        pe.wait_ge(decay_out.sem, decay_out.at(g))
                        pe.wait_ge(cmat_out.sem, cmat_out.at(g))
                    if b >= 2:
                        pe.wait_ge(hidsq_out.sem, hidsq_out.at(g, b - 1))
                    split_product([psB, psC][b % 2][:], x2hi[p][:, b, :], x2lo[p][:, b, :], aw_hi[:], aw_lo[:])\
                        .then_inc(hid_ps.sem, 1)

            def c(g, step):
                p = g.off % 2
                xh, xl = (t[p][:].rearrange("e b s -> e (b s)") for t in (x2hi, x2lo))
                if step[0] == "g":
                    e, f = step[1], step[2]
                    n = e * FB + f
                    if n == 0:
                        pe.wait_ge(x2lo_out.sem, x2lo_out.at(g))
                        pe.wait_ge(x2hi_out.sem, x2hi_out.at(g))
                    cols = slice(f * 128, (f + 1) * 128)
                    if e:
                        pe.wait_ge(silu_out.sem, silu_out.at(g, n - 1))
                    elif f and not g.first(1):
                        pe.wait_ge(acc_out.sem, acc_out.at(g.back(1)))
                    elif not g.first(1):
                        pe.wait_ge(silu_out.sem, silu_out.at(g.back(1)))
                    split_product(psG[f][:], gw_hi[:, e, cols], gw_lo[:, e, cols], xh, xl).then_inc(g_ps.sem, 1)
                elif step[0] == "u":
                    e, f = step[1], step[2]
                    cols = slice(f * 128, (f + 1) * 128)
                    psU_out = up_out if f in POOL_BLOCKS else hid_out
                    if e:
                        pe.wait_ge(psU_out.sem, psU_out.at(g, e))
                    elif not g.first(1):
                        pe.wait_ge(psU_out.sem, psU_out.at(g.back(1)))
                    split_product(psU[f][:], uw_hi[:, e, cols], uw_lo[:, e, cols], xh, xl).then_inc(u2_ps.sem, 1)
                elif step[0] == "down":
                    e = step[1]
                    pe.wait_ge(hid_out.sem, hid_out.at(g, e + 1))
                    pe.wait_ge(hid_pool_out.sem, hid_pool_out.at(g, e + 1))
                    if e == E - 1:
                        pe.wait_ge(silu_out.sem, silu_out.at(g))
                    elif e:
                        pe.wait_ge(acc_out.sem, acc_out.at(g, e))
                    elif not g.first(1):
                        pe.wait_ge(acc_out.sem, acc_out.at(g.back(1)))
                    for b in range(G):
                        for f in range(FB):
                            ins = pe.matmul(down_bank(e)[:, b, :], hid[e % 2][f][:, b * S:(b + 1) * S], dwT[:, e, f, :],
                                            start=(f == 0), stop=(f == FB - 1))
                    ins.then_inc(y_ps.sem, 1)

            whole_program(pe, prep, ab, c, {})

        @block.scalar
        def _(act):
            def prep(numbered):
                n, item = numbered
                ps = prep_bank(n)
                if item in SPLITS:
                    act.wait_ge(prep_ps, n + 1)
                    act.copy(parts(item)[0], ps[:]).then_inc(prep_hi, 1)
                elif item[0] == "down":
                    act.wait_ge(prep_ps, n + 1)
                    act.wait_ge(prep_out, n)
                    act.copy(dwT[:, 2 * item[1]:2 * item[1] + 2, :, :].rearrange("f e k h -> f (e k h)"),
                             ps[:]).then_inc(prep_out, 1)

            def decays(g, k):
                act.wait_ge(mb_ps.sem, mb_ps.at(g, k + 1))
                if k >= 2:
                    act.wait_ge(cmat_out.sem, cmat_out.at(g, k - 1))
                elif not g.first(1):
                    act.wait_ge(cmat_out.sem, cmat_out.at(g.back(1)))
                act.activation(decay[k % 2][:].rearrange("t h s -> t (h s)"), psB[:], ACT.Exp, scale=-1.0)\
                    .then_inc(decay_out.sem, 1)

            def ab(g, step):
                p = g.off % 2
                if step == "xT":
                    act.wait_ge(xT_ps.sem, xT_ps.at(g))
                    if not g.first(1):
                        act.wait_ge(logits_ps.sem, logits_ps.at(g.back(1)))
                    act.copy(xT[:].rearrange("e b s -> e (b s)"), psA[:]).then_inc(xT_sb.sem, 1)
                elif step == "zv":
                    act.wait_ge(z_ps.sem, z_ps.at(g))
                    act.copy(zT[:].rearrange("e b s -> e (b s)"), psB[:]).then_inc(zT_sb.sem, 1)
                elif step == "logits":
                    act.wait_ge(negmax_out.sem, negmax_out.at(g))
                    if not g.first(1):
                        act.wait_ge(pT_ps.sem, pT_ps.at(g.back(1)))
                        act.wait_ge(rown_out.sem, rown_out.at(g.back(1)))
                    for b in range(G):
                        ins = act.activation(probs[:, b, :], psA[:, b * S:(b + 1) * S], ACT.Exp,
                                             bias=negmax[:, b:b + 1], scale=1.0, accum_out=rowsum[:, b:b + 1])
                    ins.then_inc(probs_out.sem, 1)
                elif step == "pT":
                    act.wait_ge(cT_ps.sem, cT_ps.at(g))
                    if not g.first(1):
                        act.wait_ge(gates_ps.sem, gates_ps.at(g.back(1)))
                        act.wait_ge(kmask_out.sem, kmask_out.at(g.back(1)))
                    act.copy(cT[:].rearrange("e b s -> e (b s)"), psC[:]).then_inc(cT_sb.sem, 1)
                    act.wait_ge(pT_ps.sem, pT_ps.at(g))
                    if not g.first(1):
                        act.wait_ge(att_ps.sem, att_ps.at(g.back(1)))
                    act.copy(probsT[:].rearrange("e b s -> e (b s)"), psB[:]).then_inc(pT_sb.sem, 1)
                elif step == "x1T":
                    act.wait_ge(x1T_ps.sem, x1T_ps.at(g))
                    if not g.first(1):
                        act.wait_ge(qk_ps.sem, qk_ps.at(g.back(1)))
                    act.copy(x1T[:].rearrange("e b s -> e (b s)"), psB[:]).then_inc(x1T_sb.sem, 1)
                elif step == "gates":
                    act.wait_ge(fneg_out.sem, fneg_out.at(g))
                    act.activation(f_exp[:], f_neg[:], ACT.Exp).then_inc(fexp_out.sem, 1)
                    act.wait_ge(fexp_out.sem, fexp_out.at(g))
                    if not g.first(1):
                        act.wait_ge(logf_out.sem, logf_out.at(g.back(1)))
                    act.activation(f_ln[:], f_exp[:], ACT.Ln, bias=1.0).then_inc(fln_out.sem, 1)
                elif step == "am":
                    act.wait_ge(am_ps.sem, am_ps.at(g))
                    if not g.first(1):
                        act.wait_ge(expm_e_out.sem, expm_e_out.at(g.back(1)))
                    act.activation(expm[:], psA[:, 0:GH], ACT.Exp, scale=-1.0).then_inc(expm_out.sem, 1)
                elif step[0] == "half":
                    k = step[1]
                    if k < HALVES:
                        decays(g, k)
                    if k:
                        q = k - 1
                        act.wait_ge(u_ps.sem, u_ps.at(g, q + 1))
                        if q == 0 and not g.first(1):
                            act.wait_ge(hn_out.sem, hn_out.at(g.back(1)))
                        act.copy(u_sb[:, q * HG:(q + 1) * HG, :].rearrange("s h d -> s (h d)"),
                                 psA[:, 0:HG * VW]).then_inc(u_out.sem, 1)
                elif step[0] == "norm":
                    b = step[1]
                    heads = slice(b * H, (b + 1) * H)
                    act.wait_ge(u_out.sem, u_out.at(g, 2 * b + 2))
                    if b == 0 and not g.first(1):
                        act.wait_ge(nrm_out.sem, nrm_out.at(g.back(1)))
                        act.wait_ge(uss_out.sem, uss_out.at(g.back(1)))
                    act.activation(sum_abs[:, heads], u_sb[:, heads, 2 * DH], ACT.Abs).then_inc(sumabs_out.sem, 1)
                    if b:
                        act.wait_ge(uss_out.sem, uss_out.at(g, b))
                    act.activation(usq[:], u_sb[:, heads, 0:DH], ACT.Square).then_inc(usq_out.sem, 1)
                elif step == "x2T":
                    act.wait_ge(x2T_ps.sem, x2T_ps.at(g))
                    if not g.first(2):
                        act.wait_ge(u2_ps.sem, u2_ps.at(g.back(2)))
                    act.copy(x2hi[p][:].rearrange("e b s -> e (b s)"), psA[:]).then_inc(x2hi_out.sem, 1)
                elif step[0] == "hidden":
                    b = step[1]
                    act.wait_ge(hid_ps.sem, hid_ps.at(g, b + 1))
                    if b >= 2:
                        act.wait_ge(sc2_out.sem, sc2_out.at(g, b - 1))
                    elif not g.first(1):
                        act.wait_ge(sc2_out.sem, sc2_out.at(g.back(1)))
                    act.activation(hidsq[b % 2][:], [psB, psC][b % 2][:], ACT.Square).then_inc(hidsq_out.sem, 1)

            def c(g, step):
                p = g.off % 2
                if step[0] == "g":
                    e, f = step[1], step[2]
                    n = e * FB + f
                    act.wait_ge(g_ps.sem, g_ps.at(g, n + 1))
                    if e:
                        act.wait_ge(silu_out.sem, silu_out.at(g, n - 1))
                    elif not g.first(1):
                        act.wait_ge(silu_out.sem, silu_out.at(g.back(1)))
                    act.activation(tanh[f][:], psG[f][:], ACT.Tanh, scale=0.5).then_inc(tanh_out.sem, 1)
                elif step[0] == "u" and step[2] in POOL_BLOCKS:
                    e, f = step[1], step[2]
                    act.wait_ge(u2_ps.sem, u2_ps.at(g, e * FB + f + 1))
                    if e:
                        act.wait_ge(hid_pool_out.sem, hid_pool_out.at(g, e))
                    elif not g.first(1):
                        act.wait_ge(hid_pool_out.sem, hid_pool_out.at(g.back(1)))
                    act.activation(up[:], psU[f][:], ACT.Copy, scale=0.5).then_inc(up_out.sem, 1)
                elif step[0] == "weights":
                    act.wait_ge(sdiff_out.sem, sdiff_out.at(g))
                    if not g.first(1):
                        act.wait_ge(wexp_out.sem, wexp_out.at(g.back(1)))
                    act.activation(sexp[:], sdiff[:], ACT.Exp).then_inc(sexp_out.sem, 1)
                elif step[0] == "finish":
                    act.wait_ge(nmr3_out.sem, nmr3_out.at(g))
                    if not g.first(1):
                        act.wait_ge(stored.sem, stored.at(g.back(1)))
                    for b in range(G):
                        ins = act.activation(y_out[:, b, :], acc[p][:, b, :], ACT.Identity,
                                             bias=nmr3[:, b:b + 1], scale=rstd3[:, b:b + 1])
                    ins.then_inc(y_ready.sem, 1)

            whole_program(act, prep, ab, c, ACT_LATER)

        @block.vector
        def _(dve):
            def prep(numbered):
                n, item = numbered
                ps = prep_bank(n)
                dve.wait_ge(prep_ps, n + 1)
                if item == "small":
                    dve.tensor_copy(qk_w[:], ps[:, 0:128])
                    dve.tensor_copy(wvT[:], ps[:, 128:256]).then_inc(qkv_out, 1)
                    dve.tensor_copy(gate_xT[:], ps[:, 256:256 + 2 * H])
                    dve.tensor_copy(gate_t[:], ps[:, 256 + 2 * H:256 + 4 * H]).then_inc(gate_step, 1)
                    dve.wait_ge(gate_step, 1)
                    dve.tensor_tensor(gate_cT[:], ps[:, 256 + 4 * H:256 + 6 * H], gate_t[:], ALU.add)\
                        .then_inc(gate_step, 1)
                    dve.wait_ge(gate_step, 2)
                    dve.wait_ge(outw_loaded, 16)
                    dve.tensor_scalar(outw_s[:], outw[:], NORM_EPS ** -0.5, None, ALU.mult).then_inc(outw_ready, 1)
                    dve.wait_ge(const_ready, 1)
                    for s, src in enumerate((gate_xT, gate_cT)):
                        for b in range(G):
                            for k in range(2):
                                ins = dve.tensor_copy(gate_p[:, s, b, k * GH + b * H:k * GH + (b + 1) * H],
                                                      src[:, k * H:(k + 1) * H])
                    ins.then_inc(prep_out, 1)
                    dve.tensor_reduce(batch_rows[:], batch_4[:].rearrange("r m b -> r b m"), AX_X, ALU.add)
                    dve.tensor_reduce(head_rows[:], head_16[:].rearrange("r m h -> r h m"), AX_X, ALU.add)\
                        .then_inc(gate_step, 1)
                    dve.wait_ge(gate_step, 3)
                    for part in range(2):
                        dve.tensor_copy(arow2[part * GH:(part + 1) * GH, :], ones[:])
                    dve.tensor_scalar(decay_x[2 * GH:4 * GH, :, :],
                                      head_rows[2 * GH:4 * GH, :].unsqueeze(2).to_broadcast([2 * GH, H, S]),
                                      -1.0, None, ALU.mult).then_inc(rows_ready, 1)
                    return
                if item[0] == "wbT":
                    dve.tensor_copy(wbT[:, 2 * item[1]:2 * item[1] + 2, :].rearrange("r e f -> r (e f)"),
                                    ps[0:R, :]).then_inc(prep_out, 1)
                    return
                if item[0] == "down":
                    return
                hi, lo = parts(item)
                dve.wait_ge(prep_hi, SPLITS.index(item) + 1)
                dve.tensor_tensor(lo, ps[:], hi.bitcast(F32), ALU.subtract).then_inc(prep_out, 1)

            def layer_stats(g, src, bn, mv, bn_stage, mv_stage):
                for b in range(G):
                    ins = dve.bn_stats(bn[:, b, :], src[:, b, :])
                ins.then_inc(bn_stage.sem, 1)
                plain_wait(dve)
                dve.wait_ge(bn_stage.sem, bn_stage.at(g))
                for b in range(G):
                    ins = dve.bn_aggr(mv[:, b, :], bn[:, b, :])
                ins.then_inc(mv_stage.sem, 1)

            def add_residual(g, b):
                dve.wait_ge(hn_out.sem, hn_out.at(g, b + 1))
                dve.tensor_tensor(res2[:, b, :], hn[:].rearrange("s h d -> s (h d)"), x1[:, b, :], ALU.add)\
                    .then_inc(res2_out.sem, 1)

            def batch_stats(g, b):
                dve.wait_ge(res2_out.sem, res2_out.at(g, b + 1))
                dve.bn_stats(bn6b[:, b, :], res2[:, b, :]).then_inc(bn2_out.sem, 1)

            def batch_moments(g, b):
                plain_wait(dve)
                if b == 0 and not g.first(1):
                    dve.wait_ge(var2_out.sem, var2_out.at(g.back(1)))
                dve.wait_ge(bn2_out.sem, bn2_out.at(g, b + 1))
                dve.bn_aggr(mv2[:, b, :], bn6b[:, b, :]).then_inc(mv2_out.sem, 1)

            def token(t):
                return t.unsqueeze(2).to_broadcast([S, G, E])

            def normalize(g, dst, src, mv, rstd, rstd_stage, out_stage):
                dve.wait_ge(rstd_stage.sem, rstd_stage.at(g))
                for b in range(G):
                    ins = dve.tensor_scalar(dst[:, b, :], src[:, b, :], mv[:, b, 0:1], rstd[:, b:b + 1],
                                            ALU.subtract, ALU.mult)
                ins.then_inc(out_stage.sem, 1)

            def ab(g, step):
                p = g.off % 2
                if step == "xT":
                    dve.wait_ge(c_loaded[p].sem, c_loaded[p].at_parity(g))
                    if not g.first(1):
                        dve.wait_ge(vmean_out.sem, vmean_out.at(g.back(1)))
                    dve.tensor_reduce(vsum[:], cin[p][:].rearrange("t b (h d) -> t (b h) d", d=DH), AX_X, ALU.add)\
                        .then_inc(vsum_out.sem, 1)
                    dve.wait_ge(vsum_out.sem, vsum_out.at(g))
                    if not g.first(1):
                        dve.wait_ge(vc_out.sem, vc_out.at(g.back(1)))
                    dve.tensor_scalar(vmean[:], vsum[:], 1.0 / DH, None, ALU.mult).then_inc(vmean_out.sem, 1)
                elif step == "zv":
                    dve.wait_ge(v_ps.sem, v_ps.at(g))
                    if not g.first(1):
                        dve.wait_ge(att_ps.sem, att_ps.at(g.back(1)))
                    dve.tensor_copy(v_sb[:].rearrange("e b s -> e (b s)"), psC[:]).then_inc(v_out.sem, 1)
                elif step == "logits":
                    dve.wait_ge(logits_ps.sem, logits_ps.at(g))
                    dve.tensor_reduce(rowmax[:], psA[:].rearrange("n (b m) -> n b m", b=G), AX_X, ALU.max)\
                        .then_inc(max_out.sem, 1)
                    dve.wait_ge(max_out.sem, max_out.at(g))
                    if not g.first(1):
                        dve.wait_ge(probs_out.sem, probs_out.at(g.back(1)))
                    dve.tensor_scalar(negmax[:], rowmax[:], -1.0, None, ALU.mult).then_inc(negmax_out.sem, 1)
                elif step == "pT":
                    dve.wait_ge(probs_out.sem, probs_out.at(g))
                    dve.tensor_scalar(rowsum_n[:], rowsum[:], float(D) ** 0.5, None, ALU.mult).then_inc(rown_out.sem, 1)
                    dve.wait_ge(rown_out.sem, rown_out.at(g))
                    dve.reciprocal(rowinv[:], rowsum_n[:]).then_inc(rowinv_out.sem, 1)
                elif step == "att":
                    dve.wait_ge(rowinv_out.sem, rowinv_out.at(g))
                    dve.wait_ge(att_ps.sem, att_ps.at(g))
                    for b in range(G):
                        ins = dve.scalar_tensor_tensor(out=res1[:, b, :], in0=psA[:, b * D:(b + 1) * D],
                                                       scalar=rowinv[:, b:b + 1], in1=xin[p][:, b, :],
                                                       op0=ALU.mult, op1=ALU.add)
                    ins.then_inc(res1_out.sem, 1)
                    dve.wait_ge(res1_out.sem, res1_out.at(g))
                    if not g.first(1):
                        dve.wait_ge(var1_out.sem, var1_out.at(g.back(1)))
                    layer_stats(g, res1, bn6, mv1, bn1_out, mv1_out)
                elif step == "x1":
                    if not g.first(1):
                        dve.wait_ge(x1T_ps.sem, x1T_ps.at(g.back(1)))
                        dve.wait_ge(res2_out.sem, res2_out.at(g.back(1)))
                    normalize(g, x1, res1, mv1, rstd1, rstd1_out, x1_out)
                elif step == "gates":
                    dve.wait_ge(gates_ps.sem, gates_ps.at(g))
                    if g.first(1):
                        dve.wait_ge(bias_loaded, 16 * 2 * G)
                    dve.tensor_scalar(f_in[:], psC[GH:2 * GH, 0:S], gbias[GH:2 * GH, 0:1], None, ALU.add)\
                        .then_inc(f_out.sem, 1)
                    dve.wait_ge(f_out.sem, f_out.at(g))
                    if not g.first(1):
                        dve.wait_ge(fexp_out.sem, fexp_out.at(g.back(1)))
                    dve.scalar_tensor_tensor(out=f_neg[:], in0=f_in[:], scalar=-1.0, in1=f_in[:], op0=ALU.mult,
                                             op1=ALU.min).then_inc(fneg_out.sem, 1)
                elif step == "scan":
                    dve.wait_ge(fln_out.sem, fln_out.at(g))
                    dve.scalar_tensor_tensor(out=logf[:], in0=f_in[:], scalar=0.0, in1=f_ln[:], op0=ALU.min,
                                             op1=ALU.subtract).then_inc(logf_out.sem, 1)
                    dve.wait_ge(logf_out.sem, logf_out.at(g))
                    dve.tensor_tensor_scan(cumf[:], ones[:], logf[:], 0.0, ALU.mult, ALU.add)\
                        .then_inc(cumf_out.sem, 1)
                    dve.wait_ge(cumf_out.sem, cumf_out.at(g))
                    if not g.first(1):
                        dve.wait_ge(amax_out.sem, amax_out.at(g.back(1)))
                    dve.scalar_tensor_tensor(out=arow, in0=psC[0:GH, 0:S], scalar=gbias[0:GH, 0:1], in1=cumf[:],
                                             op0=ALU.add, op1=ALU.subtract).then_inc(arow_out.sem, 1)
                    dve.wait_ge(arow_out.sem, arow_out.at(g))
                    if not g.first(1):
                        dve.wait_ge(mb_ps.sem, mb_ps.at(g.back(1)))
                        dve.wait_ge(arows_out.sem, arows_out.at(g.back(1)))
                    dve.tensor_copy(arow2[2 * GH:3 * GH, :], arow).then_inc(arowhi_out.sem, 1)
                    dve.tensor_tensor_scan(amax[:], arow, arow, -3.0e38, ALU.max, ALU.max)\
                        .then_inc(amax_out.sem, 1)
                    dve.wait_ge(arowhi_out.sem, arowhi_out.at(g))
                    dve.tensor_tensor(arow2[3 * GH:4 * GH, :], arow, arow2[2 * GH:3 * GH, :].bitcast(F32), ALU.subtract)\
                        .then_inc(arow2_out.sem, 1)
                    dve.wait_ge(amax_out.sem, amax_out.at(g))
                    if not g.first(1):
                        dve.wait_ge(maxrows1_out.sem, maxrows1_out.at(g.back(1)))
                    dve.tensor_copy(amax2[0:GH, :], amax[:]).then_inc(amaxhi_out.sem, 1)
                    if not g.first(1):
                        dve.wait_ge(am_ps.sem, am_ps.at(g.back(1)))
                    dve.tensor_tensor(mrow[:], cumf[:], amax[:], ALU.add).then_inc(mrow_out.sem, 1)
                    dve.wait_ge(amaxhi_out.sem, amaxhi_out.at(g))
                    dve.tensor_tensor(amax2[GH:2 * GH, :], amax[:], amax2[0:GH, :].bitcast(F32), ALU.subtract)\
                        .then_inc(amax2_out.sem, 1)
                    dve.wait_ge(amax2_out.sem, amax2_out.at(g))
                    if g.first(1):
                        dve.wait_ge(rows_ready, 1)
                    spread_heads(dve, 0).then_inc(maxrows0_out.sem, 1)
                elif step == "am":
                    dve.wait_ge(expm_out.sem, expm_out.at(g))
                    if not g.first(1):
                        dve.wait_ge(nrm_out.sem, nrm_out.at(g.back(1)))
                    dve.tensor_scalar(expm_e[:], expm[:], GATE_EPS, None, ALU.add).then_inc(expm_e_out.sem, 1)
                elif step[0] == "half":
                    k = step[1]
                    if k < HALVES:
                        dve.wait_ge(qk_ps.sem, qk_ps.at(g, k + 1))
                        dve.wait_ge(decay_out.sem, decay_out.at(g, k + 1))
                        if k >= 2:
                            dve.wait_ge(u_ps.sem, u_ps.at(g, k - 1))
                        elif not g.first(1):
                            dve.wait_ge(u_ps.sem, u_ps.at(g.back(1)))
                        dve.scalar_tensor_tensor(out=cmat[k % 2][:].rearrange("t h s -> t (h s)"), in0=psC[:],
                                                 scalar=float(DH) ** -0.5,
                                                 in1=decay[k % 2][:].rearrange("t h s -> t (h s)"),
                                                 op0=ALU.mult, op1=ALU.mult).then_inc(cmat_out.sem, 1)
                elif step[0] == "norm":
                    b = step[1]
                    heads = slice(b * H, (b + 1) * H)
                    dve.wait_ge(sumabs_out.sem, sumabs_out.at(g, b + 1))
                    if b == 0:
                        dve.wait_ge(expm_e_out.sem, expm_e_out.at(g))
                    dve.scalar_tensor_tensor(out=nrm[:, heads], in0=sum_abs[:, heads], scalar=GATE_EPS,
                                             in1=expm_e[:, heads], op0=ALU.add, op1=ALU.max).then_inc(nrm_out.sem, 1)
                    dve.wait_ge(usq_out.sem, usq_out.at(g, b + 1))
                    dve.tensor_reduce(uss[:, heads], usq[:], AX_X, ALU.add).then_inc(uss_out.sem, 1)
                    dve.wait_ge(nrm_out.sem, nrm_out.at(g, b + 1))
                    dve.tensor_tensor(nrm_2[:, heads], nrm[:, heads], nrm[:, heads], ALU.mult)\
                        .then_inc(nrm2_out.sem, 1)
                    if b:
                        add_residual(g, b - 1)
                    dve.wait_ge(uss_out.sem, uss_out.at(g, b + 1))
                    dve.wait_ge(nrm2_out.sem, nrm2_out.at(g, b + 1))
                    if b == 0 and not g.first(1):
                        dve.wait_ge(hrstd_out.sem, hrstd_out.at(g.back(1)))
                    dve.scalar_tensor_tensor(out=hvar[:, heads], in0=uss[:, heads], scalar=1.0 / (DH * NORM_EPS),
                                             in1=nrm_2[:, heads], op0=ALU.mult, op1=ALU.add)\
                        .then_inc(hvar_out.sem, 1)
                    if b:
                        batch_stats(g, b - 1)
                elif step[0] == "head":
                    b = step[1]
                    heads = slice(b * H, (b + 1) * H)
                    if b:
                        batch_moments(g, b - 1)
                    dve.wait_ge(hrstd_out.sem, hrstd_out.at(g, b + 1))
                    if b:
                        dve.wait_ge(res2_out.sem, res2_out.at(g, b))
                    dve.tensor_tensor(hn[:], u_sb[:, heads, DH:2 * DH],
                                      hrstd[:, heads].unsqueeze(2).to_broadcast([S, H, DH]), ALU.mult)\
                        .then_inc(hn_out.sem, 1)
                    if b == G - 1:
                        add_residual(g, b)
                        batch_stats(g, b)
                        batch_moments(g, b)
                elif step == "x2":
                    if not g.first(2):
                        dve.wait_ge(y_ready.sem, y_ready.at(g.back(2)))
                    normalize(g, acc[p], res2, mv2, rstd2, rstd2_out, x2_out)
                elif step == "x2T":
                    dve.wait_ge(x2hi_out.sem, x2hi_out.at(g))
                    if not g.first(2):
                        dve.wait_ge(u2_ps.sem, u2_ps.at(g.back(2)))
                    dve.tensor_tensor(x2lo[p][:].rearrange("e b s -> e (b s)"), psA[:],
                                      x2hi[p][:].rearrange("e b s -> e (b s)").bitcast(F32),
                                      ALU.subtract).then_inc(x2lo_out.sem, 1)
                elif step[0] == "hidden":
                    b = step[1]
                    dve.wait_ge(hidsq_out.sem, hidsq_out.at(g, b + 1))
                    if b == 0 and not g.first(1):
                        dve.wait_ge(score_out.sem, score_out.at(g.back(1)))
                    dve.tensor_reduce(sc2[:, b, :], hidsq[b % 2][:].rearrange("n (e r) -> n e r", r=R), AX_X, ALU.add)\
                        .then_inc(sc2_out.sem, 1)
                elif step == "choose":
                    plain_wait(dve)
                    dve.wait_ge(sc2_out.sem, sc2_out.at(g))
                    for b in range(G):
                        ins = dve.max(top8[:, b, :], sc2[:, b, :])
                    ins.then_inc(top_out.sem, 1)
                    dve.wait_ge(top_out.sem, top_out.at(g))
                    dve.tensor_tensor(equal[:], sc2[:], token(top8[:, :, 1]), ALU.is_equal).then_inc(eq_out.sem, 1)
                    dve.tensor_tensor(is1[:], top8[:, :, 0], top8[:, :, 1], ALU.is_gt).then_inc(is1_out.sem, 1)
                    dve.tensor_tensor(above[:], sc2[:], token(top8[:, :, 1]), ALU.is_gt).then_inc(above_out.sem, 1)
                    dve.wait_ge(eq_out.sem, eq_out.at(g))
                    dve.tensor_tensor_scan(rank[:].rearrange("p g e -> p (g e)"), restart[:].rearrange("p g e -> p (g e)"),
                                           equal[:].rearrange("p g e -> p (g e)"), 0.0, ALU.mult, ALU.add)\
                        .then_inc(rank_out.sem, 1)
                    dve.wait_ge(is1_out.sem, is1_out.at(g))
                    dve.tensor_scalar(lim[:], is1[:], -1.0, 2.0, ALU.mult, ALU.add).then_inc(lim_out.sem, 1)
                    dve.wait_ge(rank_out.sem, rank_out.at(g))
                    dve.wait_ge(lim_out.sem, lim_out.at(g))
                    dve.tensor_tensor(inlim[:], rank[:], token(lim[:]), ALU.is_le).then_inc(inlim_out.sem, 1)
                    dve.wait_ge(inlim_out.sem, inlim_out.at(g))
                    dve.tensor_tensor(chosen2[:], inlim[:], equal[:], ALU.mult).then_inc(ch2_out.sem, 1)
                    dve.wait_ge(ch2_out.sem, ch2_out.at(g))
                    dve.wait_ge(above_out.sem, above_out.at(g))
                    dve.tensor_tensor(chosen[:], chosen2[:], above[:], ALU.add).then_inc(sel_out.sem, 1)

            def c(g, step):
                p = g.off % 2
                if step[0] == "g":
                    e, f = step[1], step[2]
                    n = e * FB + f
                    dve.wait_ge(tanh_out.sem, tanh_out.at(g, n + 1))
                    silu2_used = hid_pool_out if f in POOL_BLOCKS else hid_out
                    if e:
                        dve.wait_ge(silu2_used.sem, silu2_used.at(g, e))
                    elif not g.first(1):
                        dve.wait_ge(silu2_used.sem, silu2_used.at(g.back(1)))
                    dve.scalar_tensor_tensor(out=silu2[f][:], in0=tanh[f][:], scalar=1.0, in1=psG[f][:],
                                             op0=ALU.add, op1=ALU.mult).then_inc(silu_out.sem, 1)
                elif step[0] == "u" and step[2] not in POOL_BLOCKS:
                    e, f = step[1], step[2]
                    n = e * FB + f
                    dve.wait_ge(silu_out.sem, silu_out.at(g, n + 1))
                    dve.wait_ge(u2_ps.sem, u2_ps.at(g, n + 1))
                    if e >= 2:
                        dve.wait_ge(y_ps.sem, y_ps.at(g, e - 1))
                    elif not g.first(1):
                        dve.wait_ge(y_ps.sem, y_ps.at(g.back(1)))
                    dve.scalar_tensor_tensor(out=hid[e % 2][f][:], in0=silu2[f][:], scalar=0.5, in1=psU[f][:],
                                             op0=ALU.mult, op1=ALU.mult).then_inc(hid_out.sem, 1)
                elif step[0] == "down":
                    e = step[1]
                    dve.wait_ge(y_ps.sem, y_ps.at(g, e + 1))
                    if e == 0:
                        dve.wait_ge(wtok_out.sem, wtok_out.at(g))
                        dve.wait_ge(x2_out.sem, x2_out.at(g))
                        dve.wait_ge(x2T_ps.sem, x2T_ps.at(g))
                    else:
                        dve.wait_ge(acc_out.sem, acc_out.at(g, e))
                    for b in range(G):
                        ins = dve.scalar_tensor_tensor(out=acc[p][:, b, :], in0=down_bank(e)[:, b, :],
                                                       scalar=wtok[p][:, b, e:e + 1], in1=acc[p][:, b, :],
                                                       op0=ALU.mult, op1=ALU.add)
                    ins.then_inc(acc_out.sem, 1)
                elif step[0] == "weights":
                    dve.wait_ge(score_out.sem, score_out.at(g))
                    dve.tensor_reduce(smax[:], score[:], AX_X, ALU.max).then_inc(smax_out.sem, 1)
                    dve.wait_ge(smax_out.sem, smax_out.at(g))
                    if not g.first(1):
                        dve.wait_ge(sexp_out.sem, sexp_out.at(g.back(1)))
                    dve.tensor_tensor(sdiff[:], score[:], token(smax[:]), ALU.subtract).then_inc(sdiff_out.sem, 1)
                    dve.wait_ge(sel_out.sem, sel_out.at(g))
                    dve.wait_ge(sexp_out.sem, sexp_out.at(g))
                    dve.tensor_tensor(wexp[:], chosen[:], sexp[:], ALU.mult).then_inc(wexp_out.sem, 1)
                    dve.wait_ge(wexp_out.sem, wexp_out.at(g))
                    dve.tensor_reduce(wden[:], wexp[:], AX_X, ALU.add).then_inc(wden_out.sem, 1)
                    dve.wait_ge(wden_out.sem, wden_out.at(g))
                    dve.reciprocal(winv[:], wden[:]).then_inc(winv_out.sem, 1)
                    dve.wait_ge(winv_out.sem, winv_out.at(g))
                    dve.tensor_tensor(wtok[p][:], wexp[:], token(winv[:]), ALU.mult).then_inc(wtok_out.sem, 1)
                elif step[0] == "stats":
                    dve.wait_ge(acc_out.sem, acc_out.at(g))
                    if not g.first(1):
                        dve.wait_ge(var3_out.sem, var3_out.at(g.back(1)))
                    layer_stats(g, acc[p], bn6c, mv3, bn3_out, mv3_out)

            whole_program(dve, prep, ab, c, DVE_LATER)


_INS = ["x", "ctx_1024", "L0_attn_Wq", "L0_attn_Wk", "L0_attn_Wv", "L0_xattn_igate_w", "L0_xattn_igate_b",
        "L0_xattn_fgate_w", "L0_xattn_fgate_b", "L0_xattn_out_w", "L0_ffn_W_A", "L0_ffn_W_B", "L0_ffn_W_up",
        "L0_ffn_W_down"]


def kernel(**inputs):
    import numpy as np
    import concourse.bacc as bacc
    from concourse.bass_utils import run_bass_kernel_spmd

    nc = bacc.Bacc("TRN2", target_bir_lowering=False, num_devices=1)
    arrays, args = {}, []
    for name in _INS:
        a = np.ascontiguousarray(inputs[name])
        arrays[f"in_{name}"] = a
        args.append(nc.dram_tensor(f"in_{name}", a.shape, mybir.dt.from_np(a.dtype), kind="ExternalInput").ap())
    args.append(nc.dram_tensor("out_0", inputs["x"].shape, F32, kind="ExternalOutput").ap())
    decoder_kernel(nc, *args)
    r = run_bass_kernel_spmd(nc, [arrays], core_ids=[0])
    return r.results[0]["out_0"]
```
